# Optimizing a Trainium2 kernel written in Bass

```python
import numpy as np
import jax
import jax.numpy as jnp

def _softmax(x, axis=-1):
    return jax.nn.softmax(x, axis=axis)

def _gelu(x):
    return jax.nn.gelu(x, approximate=True)

def _silu(x):
    return jax.nn.silu(x)

def _sigmoid(x):
    return jax.nn.sigmoid(x)

def _layernorm(x, axis=-1, eps=1e-05):
    m = jnp.mean(x, axis=axis, keepdims=True)
    v = jnp.var(x, axis=axis, keepdims=True)
    return (x - m) / jnp.sqrt(v + eps)

def _scatter_add(tgt, idx, src, axis=0):
    return tgt.at[idx].add(src)

def _segment_sum(src, seg, n):
    return jax.ops.segment_sum(src, seg, n)
kernel_name = 'mk_vit_tower_cls_d2_tok_img1024_r4_6027a5'

def setup_inputs(seed: int=0):
    np.random.seed(seed)
    _w = jnp.asarray

    def _rec_inputs():
        import jax
        import jax.numpy as jnp
        _rk = jax.random.key(seed)
        x = 7.22013e-05 + 1.00017 * jax.random.normal(jax.random.fold_in(_rk, 1), (16, 64, 256, 4), jnp.float32)
        cls_tok = 0.02 * jax.random.normal(jax.random.fold_in(_rk, 5), (1, 1, 256), jnp.float32)
        return (x, cls_tok)
    x, cls_tok = _rec_inputs()

    def _L0_tok_setup():
        import jax, jax.numpy as jnp
        import numpy as np
        B, F, L, H, D = (8, 64, 256, 4, 64)
        MODEL = H * F
        WIN = 128

        def _local_mask():
            m = np.ones((L, L), dtype=bool)
            m = np.tril(m, WIN - 1)
            m = np.triu(m, -(WIN - 1))
            return jnp.asarray(m)

        def _flatten(y):
            n = y.shape[0]
            return y.transpose(0, 2, 3, 1).reshape(n, L, -1)
        key = jax.random.key(seed)
        ks = jax.random.split(key, 12)
        s = lambda n: 1.0 / np.sqrt(n)
        xav = np.sqrt(6.0 / (L + L))
        return {'x': jax.random.normal(ks[0], (B, F, L, H), jnp.float32), 'Wq_w': jax.random.normal(ks[1], (D, F), jnp.float32) * s(F), 'Wq_b': jnp.zeros((D,), jnp.float32), 'Wk_w': jax.random.normal(ks[2], (D, F), jnp.float32) * s(F), 'Wk_b': jnp.zeros((D,), jnp.float32), 'Wv_w': jax.random.normal(ks[3], (D, F), jnp.float32) * s(F), 'Wv_b': jnp.zeros((D,), jnp.float32), 'w_bias': jax.random.uniform(ks[4], (L, L), jnp.float32, -xav, xav), 'out_w': jax.random.normal(ks[5], (H * D, MODEL), jnp.float32) * s(H * D), 'out_b': jnp.zeros((MODEL,), jnp.float32), 'ln_g': jnp.ones((MODEL,), jnp.float32), 'ln_b': jnp.zeros((MODEL,), jnp.float32), 'local_mask': _local_mask()}
    _L0_tok_all = _L0_tok_setup()
    _L0_tok_in = {k: v for k, v in _L0_tok_all.items() if k in ('Wq_w', 'Wq_b', 'Wk_w', 'Wk_b', 'Wv_w', 'Wv_b', 'w_bias', 'out_w', 'out_b', 'ln_g', 'ln_b', 'local_mask')}
    del _L0_tok_all

    def _L0_attn_setup():
        import jax, jax.numpy as jnp
        import numpy as np
        T, B, D = (256, 32, 256)
        N_STATE, BLOCK = (256, 8)
        NB = N_STATE // BLOCK

        def _xavier(key, shape):
            fan_out, fan_in = shape
            a = (6.0 / (fan_in + fan_out)) ** 0.5
            return jax.random.uniform(key, shape, jnp.float32, -a, a)
        key = jax.random.key(seed)
        kx, kk, kv, kq = jax.random.split(key, 4)
        return {'x': jax.random.normal(kx, (T, B, D), jnp.float32), 'W_k': _xavier(kk, (N_STATE, D)), 'W_v': _xavier(kv, (N_STATE, D)), 'W_q': _xavier(kq, (N_STATE, D))}
    _L0_attn_all = _L0_attn_setup()
    _L0_attn_in = {k: v for k, v in _L0_attn_all.items() if k in ('W_k', 'W_v', 'W_q')}
    del _L0_attn_all

    def _L0_ffn_setup():
        import jax, jax.numpy as jnp
        import numpy as np
        ALPHA = 1.702
        LIMIT = 7.0
        TOPK = 2
        D, I, E = (256, 512, 8)
        B, S = (2, 512)

        def swiglu(x):
            g = x[..., ::2]
            l = x[..., 1::2]
            g = jnp.minimum(g, LIMIT)
            l = jnp.clip(l, -LIMIT, LIMIT)
            return g * jax.nn.sigmoid(ALPHA * g) * (l + 1.0)
        key = jax.random.key(seed)
        ks = jax.random.split(key, 16)
        sc = 0.02
        n = lambda k, shape, s=sc: jax.random.normal(k, shape, dtype=jnp.float32) * s
        return {'x': jax.random.normal(ks[0], (B, S, D), dtype=jnp.float32), 'gate_w': n(ks[1], (E, D)), 'gate_b': n(ks[2], (E,)), 'w1': n(ks[3], (E, D, 2 * I)), 'b1': n(ks[4], (E, 2 * I)), 'w3': n(ks[5], (E, D, 2 * I)), 'b3': n(ks[6], (E, 2 * I)), 'w2': n(ks[7], (E, I, D)), 'b2': n(ks[8], (E, D)), 'sw1': n(ks[9], (D, 2 * I)), 'sb1': n(ks[10], (2 * I,)), 'sw3': n(ks[11], (D, 2 * I)), 'sb3': n(ks[12], (2 * I,)), 'sw2': n(ks[13], (I, D)), 'sb2': n(ks[14], (D,))}
    _L0_ffn_all = _L0_ffn_setup()
    _L0_ffn_in = {k: v for k, v in _L0_ffn_all.items() if k in ('gate_w', 'gate_b', 'w1', 'b1', 'w3', 'b3', 'w2', 'b2', 'sw1', 'sb1', 'sw3', 'sb3', 'sw2', 'sb2')}
    del _L0_ffn_all

    def _L1_attn_setup():
        import jax, jax.numpy as jnp
        import numpy as np
        NUM_HEADS = 16
        D_MODEL = 256
        D_K = D_MODEL // NUM_HEADS
        MAX_SEQ_LEN = 1024
        ROPE_BASE = 10000.0
        BATCH = 2
        SEQ_LEN = 512

        def _rope_tables(seq_len, d_k, base=ROPE_BASE):
            theta = 1.0 / base ** (jnp.arange(0, d_k, 2, dtype=jnp.float32) / d_k)
            m = jnp.arange(seq_len, dtype=jnp.float32)
            m_theta = jnp.outer(m, theta)
            ang = jnp.concatenate([m_theta, m_theta], axis=-1)
            return (jnp.cos(ang), jnp.sin(ang))

        def _apply_rope(x, cos, sin):
            d2 = x.shape[-1] // 2
            x1, x2 = (x[..., :d2], x[..., d2:])
            x_flip = jnp.concatenate([-x2, x1], axis=-1)
            return x * cos + x_flip * sin
        key = jax.random.key(seed)
        kx, kq, kk, kv, ko = jax.random.split(key, 5)
        s = 1.0 / np.sqrt(D_MODEL)
        x = jax.random.normal(kx, (BATCH, SEQ_LEN, D_MODEL), dtype=jnp.float32)
        W_Q = jax.random.uniform(kq, (D_MODEL, D_MODEL), jnp.float32, -s, s)
        W_K = jax.random.uniform(kk, (D_MODEL, D_MODEL), jnp.float32, -s, s)
        W_V = jax.random.uniform(kv, (D_MODEL, D_MODEL), jnp.float32, -s, s)
        W_O = jax.random.uniform(ko, (D_MODEL, D_MODEL), jnp.float32, -s, s)
        return {'x': x, 'W_Q': W_Q, 'W_K': W_K, 'W_V': W_V, 'W_O': W_O}
    _L1_attn_all = _L1_attn_setup()
    _L1_attn_in = {k: v for k, v in _L1_attn_all.items() if k in ('W_Q', 'W_K', 'W_V', 'W_O')}
    del _L1_attn_all

    def _L1_ffn_setup():
        import jax, jax.numpy as jnp
        import numpy as np
        HIDDEN = 256
        INNER = 1024

        def _weight_quant(w):
            scale = 1.0 / jnp.clip(jnp.mean(jnp.abs(w)), 1e-05)
            wq = jnp.clip(jnp.round(w * scale), -1.0, 1.0) / scale
            return w + jax.lax.stop_gradient(wq - w)

        def _act_quant(x):
            scale = 127.0 / jnp.clip(jnp.max(jnp.abs(x), axis=-1, keepdims=True), 1e-05)
            xq = jnp.clip(jnp.round(x * scale), -128.0, 127.0) / scale
            return x + jax.lax.stop_gradient(xq - x)

        def _bitlinear(x, w):
            return jnp.einsum('bsi,oi->bso', _act_quant(x), _weight_quant(w))
        key = jax.random.key(seed)
        k0, k1, k2, k3 = jax.random.split(key, 4)
        x = jax.random.normal(k0, (4, 512, HIDDEN), dtype=jnp.float32)
        w_gate = jax.random.normal(k1, (INNER, HIDDEN), dtype=jnp.float32) / np.sqrt(HIDDEN)
        w_up = jax.random.normal(k2, (INNER, HIDDEN), dtype=jnp.float32) / np.sqrt(HIDDEN)
        w_down = jax.random.normal(k3, (HIDDEN, INNER), dtype=jnp.float32) / np.sqrt(INNER)
        return {'x': x, 'w_gate': w_gate, 'w_up': w_up, 'w_down': w_down}
    _L1_ffn_all = _L1_ffn_setup()
    _L1_ffn_in = {k: v for k, v in _L1_ffn_all.items() if k in ('w_gate', 'w_up', 'w_down')}
    del _L1_ffn_all
    return {'x': x, 'cls_tok': cls_tok, 'L0_tok_Wq_w': _L0_tok_in['Wq_w'], 'L0_tok_Wq_b': _L0_tok_in['Wq_b'], 'L0_tok_Wk_w': _L0_tok_in['Wk_w'], 'L0_tok_Wk_b': _L0_tok_in['Wk_b'], 'L0_tok_Wv_w': _L0_tok_in['Wv_w'], 'L0_tok_Wv_b': _L0_tok_in['Wv_b'], 'L0_tok_w_bias': _L0_tok_in['w_bias'], 'L0_tok_out_w': _L0_tok_in['out_w'], 'L0_tok_out_b': _L0_tok_in['out_b'], 'L0_tok_ln_g': _L0_tok_in['ln_g'], 'L0_tok_ln_b': _L0_tok_in['ln_b'], 'L0_tok_local_mask': _L0_tok_in['local_mask'], 'L0_attn_W_k': _L0_attn_in['W_k'], 'L0_attn_W_v': _L0_attn_in['W_v'], 'L0_attn_W_q': _L0_attn_in['W_q'], 'L0_ffn_gate_w': _L0_ffn_in['gate_w'], 'L0_ffn_gate_b': _L0_ffn_in['gate_b'], 'L0_ffn_w1': _L0_ffn_in['w1'], 'L0_ffn_b1': _L0_ffn_in['b1'], 'L0_ffn_w3': _L0_ffn_in['w3'], 'L0_ffn_b3': _L0_ffn_in['b3'], 'L0_ffn_w2': _L0_ffn_in['w2'], 'L0_ffn_b2': _L0_ffn_in['b2'], 'L0_ffn_sw1': _L0_ffn_in['sw1'], 'L0_ffn_sb1': _L0_ffn_in['sb1'], 'L0_ffn_sw3': _L0_ffn_in['sw3'], 'L0_ffn_sb3': _L0_ffn_in['sb3'], 'L0_ffn_sw2': _L0_ffn_in['sw2'], 'L0_ffn_sb2': _L0_ffn_in['sb2'], 'L1_attn_W_Q': _L1_attn_in['W_Q'], 'L1_attn_W_K': _L1_attn_in['W_K'], 'L1_attn_W_V': _L1_attn_in['W_V'], 'L1_attn_W_O': _L1_attn_in['W_O'], 'L1_ffn_w_gate': _L1_ffn_in['w_gate'], 'L1_ffn_w_up': _L1_ffn_in['w_up'], 'L1_ffn_w_down': _L1_ffn_in['w_down']}

def reference(x, cls_tok, L0_tok_Wq_w, L0_tok_Wq_b, L0_tok_Wk_w, L0_tok_Wk_b, L0_tok_Wv_w, L0_tok_Wv_b, L0_tok_w_bias, L0_tok_out_w, L0_tok_out_b, L0_tok_ln_g, L0_tok_ln_b, L0_tok_local_mask, L0_attn_W_k, L0_attn_W_v, L0_attn_W_q, L0_ffn_gate_w, L0_ffn_gate_b, L0_ffn_w1, L0_ffn_b1, L0_ffn_w3, L0_ffn_b3, L0_ffn_w2, L0_ffn_b2, L0_ffn_sw1, L0_ffn_sb1, L0_ffn_sw3, L0_ffn_sb3, L0_ffn_sw2, L0_ffn_sb2, L1_attn_W_Q, L1_attn_W_K, L1_attn_W_V, L1_attn_W_O, L1_ffn_w_gate, L1_ffn_w_up, L1_ffn_w_down):
    import jax
    import jax.numpy as jnp

    def _L0_tok_ref(x, Wq_w, Wq_b, Wk_w, Wk_b, Wv_w, Wv_b, w_bias, out_w, out_b, ln_g, ln_b, local_mask):
        import jax, jax.numpy as jnp
        import numpy as np
        B, F, L, H, D = (8, 64, 256, 4, 64)
        MODEL = H * F
        WIN = 128

        def _local_mask():
            m = np.ones((L, L), dtype=bool)
            m = np.tril(m, WIN - 1)
            m = np.triu(m, -(WIN - 1))
            return jnp.asarray(m)

        def _flatten(y):
            n = y.shape[0]
            return y.transpose(0, 2, 3, 1).reshape(n, L, -1)

        def proj(w, b):
            y = jnp.einsum('nclh,dc->ndlh', x, w) + b[None, :, None, None]
            return _flatten(y)
        q = proj(Wq_w, Wq_b)
        k = proj(Wk_w, Wk_b)
        v = proj(Wv_w, Wv_b)
        wb = w_bias * local_mask.astype(w_bias.dtype)
        ew = jnp.exp(wb)
        ek = jnp.exp(k)
        num = jnp.einsum('ts,nsd->ntd', ew, ek * v)
        den = jnp.einsum('ts,nsd->ntd', ew, ek)
        y = jax.nn.sigmoid(q) * num / den
        h = y @ out_w + out_b + _flatten(x)
        mu = jnp.mean(h, axis=-1, keepdims=True)
        var = jnp.mean(jnp.square(h - mu), axis=-1, keepdims=True)
        return (h - mu) * jax.lax.rsqrt(var + 1e-05) * ln_g + ln_b

    def _L0_attn_ref(x, W_k, W_v, W_q):
        import jax, jax.numpy as jnp
        import numpy as np
        T, B, D = (256, 32, 256)
        N_STATE, BLOCK = (256, 8)
        NB = N_STATE // BLOCK

        def _xavier(key, shape):
            fan_out, fan_in = shape
            a = (6.0 / (fan_in + fan_out)) ** 0.5
            return jax.random.uniform(key, shape, jnp.float32, -a, a)
        T_, B_, D_ = x.shape
        n = W_k.shape[0]
        b = BLOCK
        nb = n // b
        k = jnp.einsum('tbd,nd->tbn', x, W_k).reshape(T_, B_, nb, b)
        v = jnp.einsum('tbd,nd->tbn', x, W_v).reshape(T_, B_, nb, b)
        q = jnp.einsum('tbd,nd->tbn', x, W_q).reshape(T_, B_, nb, b)

        def step(S, kvq):
            k_t, v_t, q_t = kvq
            k_norm = k_t / (jnp.linalg.norm(k_t, axis=-1, keepdims=True) + 1e-06)
            retrieved = jnp.einsum('bnij,bnj->bni', S, k_norm)
            delta = v_t - retrieved
            S_new = jnp.tanh(S + jnp.einsum('bni,bnj->bnij', delta, k_norm))
            Sq = jnp.einsum('bnij,bnj->bni', S_new, q_t).reshape(B_, n)
            out = Sq * jax.nn.silu(Sq)
            return (S_new, out)
        S0 = jnp.zeros((B_, nb, b, b), x.dtype)
        _, outputs = jax.lax.scan(step, S0, (k, v, q))
        return outputs

    def _L0_ffn_ref(x, gate_w, gate_b, w1, b1, w3, b3, w2, b2, sw1, sb1, sw3, sb3, sw2, sb2):
        import jax, jax.numpy as jnp
        import numpy as np
        ALPHA = 1.702
        LIMIT = 7.0
        TOPK = 2
        D, I, E = (256, 512, 8)
        B, S = (2, 512)

        def swiglu(x):
            g = x[..., ::2]
            l = x[..., 1::2]
            g = jnp.minimum(g, LIMIT)
            l = jnp.clip(l, -LIMIT, LIMIT)
            return g * jax.nn.sigmoid(ALPHA * g) * (l + 1.0)
        b, s, d = x.shape
        xt = x.reshape(-1, d)
        scores = jax.nn.softmax(xt @ gate_w.T, axis=-1)
        biased = scores + gate_b
        _, idx = jax.lax.top_k(biased, TOPK)
        weights = jnp.take_along_axis(scores, idx, axis=-1)
        comb = (weights[..., None] * jax.nn.one_hot(idx, E, dtype=xt.dtype)).sum(1)

        def body(acc, p):
            ew1, eb1, ew3, eb3, ew2, eb2, ce = p
            h = swiglu((xt @ ew1 + eb1) * (xt @ ew3 + eb3))
            return (acc + ce[:, None] * (h @ ew2 + eb2), None)
        routed, _ = jax.lax.scan(body, jnp.zeros_like(xt), (w1, b1, w3, b3, w2, b2, comb.T))
        shared = swiglu((xt @ sw1 + sb1) * (xt @ sw3 + sb3)) @ sw2 + sb2
        return (routed + shared).reshape(b, s, d)

    def _L1_attn_ref(x, W_Q, W_K, W_V, W_O):
        import jax, jax.numpy as jnp
        import numpy as np
        NUM_HEADS = 16
        D_MODEL = 256
        D_K = D_MODEL // NUM_HEADS
        MAX_SEQ_LEN = 1024
        ROPE_BASE = 10000.0
        BATCH = 2
        SEQ_LEN = 512

        def _rope_tables(seq_len, d_k, base=ROPE_BASE):
            theta = 1.0 / base ** (jnp.arange(0, d_k, 2, dtype=jnp.float32) / d_k)
            m = jnp.arange(seq_len, dtype=jnp.float32)
            m_theta = jnp.outer(m, theta)
            ang = jnp.concatenate([m_theta, m_theta], axis=-1)
            return (jnp.cos(ang), jnp.sin(ang))

        def _apply_rope(x, cos, sin):
            d2 = x.shape[-1] // 2
            x1, x2 = (x[..., :d2], x[..., d2:])
            x_flip = jnp.concatenate([-x2, x1], axis=-1)
            return x * cos + x_flip * sin
        B, S, _ = x.shape

        def proj(W):
            y = jnp.einsum('bsd,ed->bse', x, W)
            return y.reshape(B, S, NUM_HEADS, D_K).transpose(0, 2, 1, 3)
        Q, K, V = (proj(W_Q), proj(W_K), proj(W_V))
        cos, sin = _rope_tables(S, D_K)
        Q = _apply_rope(Q, cos, sin)
        K = _apply_rope(K, cos, sin)
        scores = jnp.einsum('bhsd,bhtd->bhst', Q, K) / jnp.sqrt(jnp.float32(D_K))
        causal = jnp.tril(jnp.ones((S, S), dtype=bool))
        scores = jnp.where(causal[None, None], scores, -jnp.inf)
        attn = jax.nn.softmax(scores, axis=-1)
        out = jnp.einsum('bhst,bhtd->bhsd', attn, V)
        out = out.transpose(0, 2, 1, 3).reshape(B, S, D_MODEL)
        return jnp.einsum('bsd,ed->bse', out, W_O)

    def _L1_ffn_ref(x, w_gate, w_up, w_down):
        import jax, jax.numpy as jnp
        import numpy as np
        HIDDEN = 256
        INNER = 1024

        def _weight_quant(w):
            scale = 1.0 / jnp.clip(jnp.mean(jnp.abs(w)), 1e-05)
            wq = jnp.clip(jnp.round(w * scale), -1.0, 1.0) / scale
            return w + jax.lax.stop_gradient(wq - w)

        def _act_quant(x):
            scale = 127.0 / jnp.clip(jnp.max(jnp.abs(x), axis=-1, keepdims=True), 1e-05)
            xq = jnp.clip(jnp.round(x * scale), -128.0, 127.0) / scale
            return x + jax.lax.stop_gradient(xq - x)

        def _bitlinear(x, w):
            return jnp.einsum('bsi,oi->bso', _act_quant(x), _weight_quant(w))
        gate = jax.nn.silu(_bitlinear(x, w_gate))
        up = _bitlinear(x, w_up)
        return _bitlinear(gate * up, w_down)
    h = _L0_tok_ref(x, L0_tok_Wq_w, L0_tok_Wq_b, L0_tok_Wk_w, L0_tok_Wk_b, L0_tok_Wv_w, L0_tok_Wv_b, L0_tok_w_bias, L0_tok_out_w, L0_tok_out_b, L0_tok_ln_g, L0_tok_ln_b, L0_tok_local_mask)
    h = jnp.concatenate([jnp.broadcast_to(cls_tok, (h.shape[0], 1, h.shape[2])), h], axis=1)
    h = h + _L0_attn_ref(_layernorm(h, axis=-1), L0_attn_W_k, L0_attn_W_v, L0_attn_W_q)
    h = h + _L0_ffn_ref(_layernorm(h, axis=-1), L0_ffn_gate_w, L0_ffn_gate_b, L0_ffn_w1, L0_ffn_b1, L0_ffn_w3, L0_ffn_b3, L0_ffn_w2, L0_ffn_b2, L0_ffn_sw1, L0_ffn_sb1, L0_ffn_sw3, L0_ffn_sb3, L0_ffn_sw2, L0_ffn_sb2)
    h = h + _L1_attn_ref(_layernorm(h, axis=-1), L1_attn_W_Q, L1_attn_W_K, L1_attn_W_V, L1_attn_W_O)
    h = h + _L1_ffn_ref(_layernorm(h, axis=-1), L1_ffn_w_gate, L1_ffn_w_up, L1_ffn_w_down)
    return h

_drawn_inputs = setup_inputs


def setup_inputs(seed=0):
    import zlib

    import numpy as np

    out = dict(_drawn_inputs(seed))
    spreads = {'L0_tok_Wq_b': (0.0, 0.8),
     'L0_tok_Wk_b': (0.0, 2.0),
     'L0_tok_Wv_b': (0.0, 0.1),
     'L0_tok_out_b': (0.0, 0.1),
     'L0_tok_ln_g': (1.0, 0.2),
     'L0_tok_ln_b': (0.0, 0.1)}
    factors = {'L0_tok_w_bias': 8.0,
     'L0_ffn_gate_w': 8.0,
     'L0_ffn_gate_b': 8.0,
     'L0_ffn_w1': 8.0,
     'L0_ffn_b1': 8.0,
     'L0_ffn_w3': 8.0,
     'L0_ffn_b3': 8.0,
     'L0_ffn_w2': 8.0,
     'L0_ffn_b2': 64.0,
     'L0_ffn_sw1': 4.982,
     'L0_ffn_sb1': 8.0,
     'L0_ffn_sw3': 4.966,
     'L0_ffn_sb3': 8.0,
     'L0_ffn_sw2': 4.9,
     'L0_ffn_sb2': 47.28,
     'L1_attn_W_Q': 44.196,
     'L1_attn_W_K': 44.32,
     'L1_attn_W_V': 5.747,
     'L1_attn_W_O': 5.742,
     'L1_ffn_w_gate': 8.0,
     'L1_ffn_w_up': 8.0,
     'L1_ffn_w_down': 8.0}
    for name, (base, spread) in spreads.items():
        noise = np.random.default_rng([zlib.crc32(name.encode()), seed]).standard_normal(out[name].shape)
        drawn = base * np.exp(spread * noise) if base else spread * noise
        out[name] = jnp.asarray(drawn.astype(out[name].dtype))
    for name, factor in factors.items():
        out[name] = (out[name] * factor).astype(out[name].dtype)
    return out
```

```python
from contextlib import ExitStack

import concourse.bass as bass
from concourse import mybir

P = 128
D = 256
NB = 16
L = 256
C = 64
HT = 4
NT = 2 * NB + 2
CLS = 2 * NB
EPS = 1e-5
E = 8
I = 512
MT = 256
ROUTED = 2 * NB * (L + 1) // MT + E
SHARED = NT * P // MT
MTILES = ROUTED + SHARED
AH = 16
DH = D // AH
MAGIC = 1.5 * 2 ** 23

F32 = mybir.dt.float32
BF16 = mybir.dt.bfloat16
I32 = mybir.dt.int32
U8 = mybir.dt.uint8
U32 = mybir.dt.uint32
ALU = mybir.AluOpType
ACT = mybir.ActivationFunctionType
AX = mybir.AxisListType


class Steps:

    def __init__(self, engine, sem, per):
        self.engine, self.sem, self.per, self.base, self.k = engine, sem, per, 0, 0

    def round(self, n):
        assert self.k in (0, self.per), (self.k, self.per)
        self.base, self.k = n * self.per, 0

    def then_wait(self, instruction, passed=None):
        instruction.then_inc(self.sem, 1)
        self.k += 1
        value = self.base + self.k
        if passed:
            if not isinstance(value, int):
                value = self.engine.to_reg(value)
            self.engine.wait_ge(*passed)
        self.engine.wait_ge(self.sem, value)


class Memory:

    def __init__(self, nc, stack, prefix):
        self.nc, self.stack, self.prefix = nc, stack, prefix

    def sb(self, name, shape, dt=F32):
        return self.stack.enter_context(self.nc.sbuf_tensor(self.prefix + name, shape, dt))

    def ps(self, name, shape, dt=F32):
        return self.stack.enter_context(self.nc.psum_tensor(self.prefix + name, shape, dt))

    def sem(self, name):
        return self.nc.alloc_semaphore(self.prefix + name)


def over(ap, axis, count):
    a = ap.unsqueeze(axis)
    shape = list(a.shape)
    shape[axis] = count
    return a.broadcast_to(shape)


def tokenizer(nc, H, args):
    with ExitStack() as stack:
        m = Memory(nc, stack, "tok_")
        wqkv = m.sb("wqkv", [C + 1, 3 * C])
        ew = m.sb("ew", [P, 2, L])
        mask8 = m.sb("mask8", [P, 2, L], U8)
        maskf = m.sb("maskf", [P, 2, L])
        outw = m.sb("outw", [P, 2, D])
        outb = m.sb("outb", [P, D])
        gain = m.sb("gain", [P, D])
        shift = m.sb("shift", [P, D])
        ident = m.sb("ident", [P, P])
        xa = [m.sb(f"xa{b}", [C + 1, HT, L]) for b in range(2)]
        xr = [m.sb(f"xr{b}", [P, 2, D]) for b in range(2)]
        mix = m.sb("mix", [P, 2, 2, D])
        eq = [m.sb(f"eq{b}", [P, 2, D]) for b in range(2)]
        den = m.sb("den", [P, 2, D])
        rec = m.sb("rec", [P, 2, D])
        y = m.sb("y", [P, 2, D])
        yT = m.sb("yT", [P, 2, L])
        hres = m.sb("hres", [P, 2, D])
        stats = m.sb("stats", [P, 2, 6])
        mv = m.sb("mv", [P, 2, 2])
        rstd = m.sb("rstd", [P, 2])
        mhalf = m.sb("mhalf", [P, 2])
        eps = m.sb("eps", [P, 2])
        hn = [m.sb(f"hn{b}", [P, 2, D]) for b in range(2)]

        ps_qkv = m.ps("ps_qkv", [P, 2, HT, 256])
        ps_nd = m.ps("ps_nd", [P, 2, 2, D])
        ps_yT = m.ps("ps_yT", [P, 2, L])
        ps_h = m.ps("ps_h", [P, 2, D])

        weights_in = m.sem("weights_in")
        class_in = m.sem("class_in")
        zeroed = m.sem("zeroed")
        ident_done = m.sem("ident_done")
        mask_steps = m.sem("mask_steps")
        ew_ready = m.sem("ew_ready")
        xa_in = [m.sem(f"xa_in{b}") for b in range(2)]
        xr_in = [m.sem(f"xr_in{b}") for b in range(2)]
        qkv_done = m.sem("qkv_done")
        exps_done = m.sem("exps_done")
        mix_done = m.sem("mix_done")
        nd_done = m.sem("nd_done")
        y_done = m.sem("y_done")
        yT_done = m.sem("yT_done")
        yT_copied = m.sem("yT_copied")
        hproj_done = m.sem("hproj_done")
        residual_ready = m.sem("residual_ready")
        var_done = m.sem("var_done")
        rstd_done = m.sem("rstd_done")
        normed = m.sem("normed")
        h_written = m.sem("h_written")
        y_steps = m.sem("y_steps")
        norm_steps = m.sem("norm_steps")
        pool_steps = m.sem("pool_steps")

        block = stack.enter_context(nc.Block())

        @block.sync
        def _(sp):
            sp.dma_start(wqkv[:, :], args["tok_wqkv"]).then_inc(weights_in, 16)
            sp.dma_start(ew[:, :, :], args["tok_wbT"].rearrange("(s p) t -> p s t", p=P)).then_inc(weights_in, 16)
            sp.dma_start(mask8[:, :, :], args["tok_maskT"].rearrange("(s p) t -> p s t", p=P)).then_inc(weights_in, 16)
            sp.dma_start(outw[:, :, :], args["L0_tok_out_w"].rearrange("(c p) n -> p c n", p=P)).then_inc(weights_in, 16)
            sp.dma_start(outb[:, :], args["L0_tok_out_b"].partition_broadcast(P)).then_inc(weights_in, 16)
            sp.dma_start(gain[:, :], args["L0_tok_ln_g"].partition_broadcast(P)).then_inc(weights_in, 16)
            sp.dma_start(shift[:, :], args["L0_tok_ln_b"].partition_broadcast(P)).then_inc(weights_in, 16)
            sp.wait_ge(zeroed, 1)
            sp.dma_start(H[0:NB, CLS, :], args["cls_row"].partition_broadcast(NB)).then_inc(class_in, 16)

            def load(i, b, first):
                n = 2 * i + b
                if not first:
                    sp.wait_ge(qkv_done, n - 1)
                    sp.wait_ge(normed, n - 1)
                sp.dma_start(xa[b][:, :, :], args["tok_x"][bass.ds(n, 1)].rearrange(
                    "o c (h l) -> (o c) h l", h=HT)).then_inc(xa_in[b], 16)
                sp.dma_start(xr[b][:, :, :], args["tok_xr"][bass.ds(n, 1)].rearrange(
                    "o (s p) d -> (o p) s d", p=P)).then_inc(xr_in[b], 16)

            load(0, 0, True)
            load(0, 1, True)
            with sp.Fori(1, NB // 2) as i:
                load(i, 0, False)
                load(i, 1, False)
            sp.wait_ge(class_in, 16)

        @block.gpsimd
        def _(pool):
            nc.gpsimd.memset(H[:, CLS:NT, :], 0.0).then_inc(zeroed, 1)
            nc.gpsimd.memset(mhalf[:, :], -0.5).then_inc(pool_steps, 1)
            nc.gpsimd.memset(eps[:, :], EPS).then_inc(pool_steps, 1)
            nc.gpsimd.memset(ident[:, :], 0.0).then_inc(pool_steps, 1)
            pool.wait_ge(pool_steps, 3)
            nc.gpsimd.affine_select(out=ident[:, :], in_=ident[:, :], compare_op=ALU.not_equal, fill=1.0,
                                    base=0, pattern=[[-1, P]], channel_multiplier=1).then_inc(ident_done, 1)
            pool.wait_ge(weights_in, 7 * 16)
            steps = Steps(pool, m.sem("pool_ln"), 2)
            with pool.Fori(0, NB // 2) as i:
                for b in range(2):
                    n = 2 * i + b
                    pool.wait_ge(xr_in[b], 16 * i + 16)
                    nc.gpsimd.tensor_tensor(xr[b][:, :, :], xr[b][:, :, :], over(outb[:, :], 1, 2), ALU.add)\
                        .then_inc(residual_ready, 1)
                    steps.round(n)
                    pool.wait_ge(var_done, n + 1)
                    steps.then_wait(nc.gpsimd.tensor_tensor(rstd[:, :], mv[:, :, 1], eps[:, :], ALU.add))
                    nc.gpsimd.tensor_tensor(rstd[:, :], rstd[:, :], mhalf[:, :], ALU.pow).then_inc(rstd_done, 1)
                    pool.wait_ge(normed, n + 1)
                    steps.then_wait(nc.gpsimd.tensor_tensor(
                        hn[b][:, :, :], hn[b][:, :, :], over(gain[:, :], 1, 2), ALU.mult))
                    nc.gpsimd.tensor_tensor(H[:, bass.ds(2 * n, 2), :], hn[b][:, :, :],
                                            over(shift[:, :], 1, 2), ALU.add).then_inc(h_written, 1)

        @block.tensor
        def _(pe):
            pe.wait_ge(weights_in, 7 * 16)

            def project(i, b, first):
                n = 2 * i + b
                pe.wait_ge(xa_in[b], 16 * i + 16)
                if not first:
                    pe.wait_ge(exps_done, n)
                    pe.wait_ge(mix_done, n)
                for s in range(2):
                    for h in range(HT):
                        last = nc.tensor.matmul(ps_qkv[:, s, h, 0:3 * C], xa[b][:, h, s * P:(s + 1) * P],
                                                wqkv[:, :], start=True, stop=True)
                last.then_inc(qkv_done, 1)

            def mixed(i, b):
                n = 2 * i + b
                pe.wait_ge(mix_done, n + 1)
                pe.wait_ge(exps_done, n + 1)
                for t in range(2):
                    for s in range(2):
                        last = nc.tensor.matmul(ps_nd[:, t, :, :], ew[:, s, t * P:(t + 1) * P],
                                                mix[:, s, :, :], start=s == 0, stop=s == 1)
                last.then_inc(nd_done, 1)

            def out(i, b):
                n = 2 * i + b
                pe.wait_ge(y_done, n + 1)
                for c in range(2):
                    for s in range(2):
                        last = nc.tensor.transpose(ps_yT[:, c, s * P:(s + 1) * P],
                                                   y[:, s, c * P:(c + 1) * P], ident[:, :])
                last.then_inc(yT_done, 1)
                pe.wait_ge(yT_copied, n + 1)
                for s in range(2):
                    for c in range(2):
                        last = nc.tensor.matmul(ps_h[:, s, :], yT[:, c, s * P:(s + 1) * P], outw[:, c, :],
                                                start=c == 0, stop=c == 1)
                last.then_inc(hproj_done, 1)

            project(0, 0, True)
            pe.wait_ge(ew_ready, 1)
            pe.wait_ge(ident_done, 1)
            with pe.Fori(0, NB // 2 - 1) as i:
                for b in range(2):
                    mixed(i, b)
                    project(i + b, 1 - b, False)
                    out(i, b)
            last_i = NB // 2 - 1
            mixed(last_i, 0)
            project(last_i, 1, False)
            out(last_i, 0)
            mixed(last_i, 1)
            out(last_i, 1)

        @block.scalar
        def _(act):
            act.wait_ge(mask_steps, 2)
            nc.scalar.activation(ew[:, :, :], ew[:, :, :], ACT.Exp).then_inc(ew_ready, 1)

            def exps(i, b, first):
                n = 2 * i + b
                act.wait_ge(qkv_done, n + 1)
                if not first:
                    act.wait_ge(nd_done, n)
                for s in range(2):
                    nc.scalar.activation(mix[:, s, 1, :].rearrange("p (h c) -> p h c", h=HT),
                                         ps_qkv[:, s, :, C:2 * C], ACT.Exp)
                    last = nc.scalar.activation(eq[b][:, s, :].rearrange("p (h c) -> p h c", h=HT),
                                                ps_qkv[:, s, :, 0:C], ACT.Exp, scale=-1.0)
                last.then_inc(exps_done, 1)

            def copy(i, b):
                n = 2 * i + b
                act.wait_ge(yT_done, n + 1)
                nc.scalar.activation(yT[:, :, :], ps_yT[:, :, :], ACT.Copy).then_inc(yT_copied, 1)

            exps(0, 0, True)
            with act.Fori(0, NB // 2 - 1) as i:
                for b in range(2):
                    exps(i + b, 1 - b, False)
                    copy(i, b)
            last_i = NB // 2 - 1
            exps(last_i, 1, False)
            copy(last_i, 0)
            copy(last_i, 1)

        @block.vector
        def _(dve):
            dve.wait_ge(weights_in, 7 * 16)
            nc.vector.tensor_copy(maskf[:, :, :], mask8[:, :, :]).then_inc(mask_steps, 1)
            dve.wait_ge(mask_steps, 1)
            nc.vector.tensor_tensor(ew[:, :, :], ew[:, :, :], maskf[:, :, :], ALU.mult).then_inc(mask_steps, 1)
            y_chain = Steps(dve, y_steps, 2)
            norm_chain = Steps(dve, norm_steps, 2)

            def weigh(i, b):
                n = 2 * i + b
                dve.wait_ge(exps_done, n + 1)
                for s in range(2):
                    last = nc.vector.tensor_tensor(
                        mix[:, s, 0, :].rearrange("p (h c) -> p h c", h=HT), ps_qkv[:, s, :, 2 * C:3 * C],
                        mix[:, s, 1, :].rearrange("p (h c) -> p h c", h=HT), ALU.mult)
                last.then_inc(mix_done, 1)

            def gate(i, b):
                n = 2 * i + b
                y_chain.round(n)
                dve.wait_ge(nd_done, n + 1)
                y_chain.then_wait(nc.vector.scalar_tensor_tensor(
                    den[:, :, :], eq[b][:, :, :], 1.0, ps_nd[:, :, 1, :], ALU.add, ALU.mult))
                y_chain.then_wait(nc.vector.reciprocal(rec[:, :, :], den[:, :, :]))
                nc.vector.tensor_tensor(y[:, :, :], ps_nd[:, :, 0, :], rec[:, :, :], ALU.mult).then_inc(y_done, 1)

            def norm(i, b):
                n = 2 * i + b
                norm_chain.round(n)
                dve.wait_ge(hproj_done, n + 1)
                dve.wait_ge(residual_ready, n + 1)
                norm_chain.then_wait(nc.vector.tensor_tensor(hres[:, :, :], ps_h[:, :, :], xr[b][:, :, :], ALU.add))
                for s in range(2):
                    last = nc.vector.bn_stats(stats[:, s, :], hres[:, s, :])
                norm_chain.then_wait(last, (weights_in, 7 * 16))
                for s in range(2):
                    last = nc.vector.bn_aggr(mv[:, s, :], stats[:, s, :])
                last.then_inc(var_done, 1)
                dve.wait_ge(rstd_done, n + 1)
                for s in range(2):
                    last = nc.vector.tensor_scalar(hn[b][:, s, :], hres[:, s, :], mv[:, s, 0:1], rstd[:, s:s + 1],
                                                   ALU.subtract, ALU.mult)
                last.then_inc(normed, 1)

            weigh(0, 0)
            with dve.Fori(0, NB // 2 - 1) as i:
                for b in range(2):
                    gate(i, b)
                    weigh(i + b, 1 - b)
                    norm(i, b)
            last_i = NB // 2 - 1
            gate(last_i, 0)
            weigh(last_i, 1)
            norm(last_i, 0)
            gate(last_i, 1)
            norm(last_i, 1)


def recurrence(nc, H, xs, args):
    NBLK, BW = 32, 8
    U = 2 * NBLK + 1
    GROUPS = [(0, 33), (33, U)]
    with ExitStack() as stack:
        m = Memory(nc, stack, "rec_")
        w = m.sb("w", [P, 2, 3 * D])
        ident = m.sb("ident", [P, P])
        mhalf = m.sb("mhalf", [P, 2])
        eps = m.sb("eps", [P, 2])
        half = m.sb("half", [P, U])
        stats = m.sb("stats", [P, 2, 6])
        mv = m.sb("mv", [P, 2, 2])
        rstd = m.sb("rstd", [P, 2])
        xn = m.sb("xn", [P, 2, D])
        xT = m.sb("xT", [P, 2, 2 * P])
        kvq = [m.sb(f"kvq{b}", [P, 3, U, BW]) for b in range(2)]
        kn = [m.sb(f"kn{b}", [P, U, BW]) for b in range(2)]
        ksq = m.sb("ksq", [P, U, BW])
        ss = m.sb("ss", [P, U])
        nrm = m.sb("nrm", [P, U])
        rn = m.sb("rn", [P, U])
        row = m.sb("row", [1, 3 * D])
        S = m.sb("S", [P, U, BW, BW])
        T = m.sb("T", [P, U, BW, BW])
        got = m.sb("got", [P, U, BW])
        delta = m.sb("delta", [P, U, BW])
        sq = [m.sb(f"sq{b}", [P, U, BW]) for b in range(2)]
        th = [m.sb(f"th{b}", [P, U, BW]) for b in range(2)]
        sqh = [m.sb(f"sqh{b}", [P, U, BW]) for b in range(2)]
        o = m.sb("o", [P, U, BW])
        ocls = m.sb("ocls", [NBLK, NB, BW])
        ocls_rows = m.sb("ocls_rows", [NB, D])
        zero_rows = m.sb("zero_rows", [P, 8 * D])
        row_dram = nc.dram_tensor("rec_row_dram", (3 * D,), F32).ap()
        ocls_dram = nc.dram_tensor("rec_ocls_dram", (NB, D), F32).ap()

        ps_xT = m.ps("ps_xT", [P, 2, 2 * P])
        ps_kvq = m.ps("ps_kvq", [P, 2, 4, D])

        weights_in = m.sem("weights_in")
        zero_ready = m.sem("zero_ready")
        xs_zeroed = m.sem("xs_zeroed")
        consts = m.sem("consts")
        ident_done = m.sem("ident_done")
        row_copied = m.sem("row_copied")
        row_out = m.sem("row_out")
        row_in = m.sem("row_in")
        state_zero = m.sem("state_zero")
        var_done = m.sem("var_done")
        rstd_done = m.sem("rstd_done")
        xn_done = m.sem("xn_done")
        xT_done = m.sem("xT_done")
        xT_copied = m.sem("xT_copied")
        kvq_done = m.sem("kvq_done")
        kvq_copied = m.sem("kvq_copied")
        ss_done = m.sem("ss_done")
        nrm_done = m.sem("nrm_done")
        pre_done = [m.sem(f"pre_done{g}") for g in range(2)]
        tanh_done = [m.sem(f"tanh_done{g}") for g in range(2)]
        sq_done = m.sem("sq_done")
        gate_done = m.sem("gate_done")
        out_done = [m.sem(f"out_done{b}") for b in range(2)]
        ocls_out = m.sem("ocls_out")
        ocls_in = m.sem("ocls_in")

        block = stack.enter_context(nc.Block())

        @block.sync
        def _(sp):
            sp.dma_start(w[:, :, :], args["rec_w"].rearrange("(c p) n -> p c n", p=P)).then_inc(weights_in, 16)
            sp.wait_ge(row_copied, 1)
            sp.dma_start(row_dram.unsqueeze(0), row[:, :]).then_inc(row_out, 16)
            sp.wait_ge(row_out, 16)
            sp.wait_ge(consts, 6)
            for b in range(2):
                sp.dma_start(kvq[b][0:NBLK, :, U - 1, :],
                             row_dram.rearrange("(c b j) -> b c j", c=3, j=BW)).then_inc(row_in, 16)
            sp.wait_ge(zero_ready, 1)
            xs_v = xs[0:ROUTED * MT, :].rearrange("(p g r) d -> g p (r d)", p=P, r=8)
            chunks = ROUTED * MT // P // 8
            with sp.Fori(0, chunks) as g:
                sp.dma_start(xs_v[bass.ds(g, 1)].rearrange("o p d -> (o p) d"), zero_rows[:, :])\
                    .then_inc(xs_zeroed, 16)
            sp.wait_ge(out_done[0], NB // 2 + 1)
            sp.wait_ge(out_done[1], NB // 2 + 1)
            sp.dma_start(ocls_dram.rearrange("n (b j) -> b n j", j=BW), ocls[:, :, :]).then_inc(ocls_out, 16)
            sp.wait_ge(ocls_out, 16)
            sp.dma_start(ocls_rows[:, :], ocls_dram).then_inc(ocls_in, 16)
            sp.wait_ge(ocls_in, 16)
            sp.wait_ge(xs_zeroed, 16 * chunks)

        @block.gpsimd
        def _(pool):
            for b in range(2):
                pool.sem_inc(out_done[b], 1)
            nc.gpsimd.memset(mhalf[:, :], -0.5).then_inc(consts, 1)
            nc.gpsimd.memset(eps[:, :], EPS).then_inc(consts, 1)
            nc.gpsimd.memset(half[:, :], 0.5).then_inc(consts, 1)
            nc.gpsimd.memset(ident[:, :], 0.0).then_inc(consts, 1)
            for b in range(2):
                nc.gpsimd.memset(kvq[b][:, :, U - 1, :], 0.0).then_inc(consts, 1)
            pool.wait_ge(consts, 6)
            nc.gpsimd.affine_select(out=ident[:, :], in_=ident[:, :], compare_op=ALU.not_equal, fill=1.0,
                                    base=0, pattern=[[-1, P]], channel_multiplier=1).then_inc(ident_done, 1)
            nc.gpsimd.memset(zero_rows[:, :], 0.0).then_inc(zero_ready, 1)
            rstd_steps = Steps(pool, m.sem("pool_rstd"), 1)
            out_steps = Steps(pool, m.sem("pool_out"), 4)

            def root(k):
                rstd_steps.round(k)
                pool.wait_ge(var_done, k + 1)
                rstd_steps.then_wait(nc.gpsimd.tensor_tensor(rstd[:, :], mv[:, :, 1], eps[:, :], ALU.add))
                nc.gpsimd.tensor_tensor(rstd[:, :], rstd[:, :], mhalf[:, :], ALU.pow).then_inc(rstd_done, 1)

            def norm(n):
                pool.wait_ge(ss_done, n + 1)
                nc.gpsimd.tensor_tensor(nrm[:, :], ss[:, :], half[:, :], ALU.pow).then_inc(nrm_done, 1)

            def gate(i, b):
                n = 2 * i + b
                out_steps.round(n)
                pool.wait_ge(gate_done, n + 1)
                out_steps.then_wait(nc.gpsimd.tensor_tensor(o[:, :, :], th[b][:, :, :], sqh[b][:, :, :], ALU.mult))
                out_steps.then_wait(nc.gpsimd.tensor_tensor(o[:, :, :], o[:, :, :], sqh[b][:, :, :], ALU.add))
                out_steps.then_wait(nc.gpsimd.tensor_tensor(o[:, :, :], o[:, :, :], sq[b][:, :, :], ALU.mult))
                tiles = H[:, bass.ds(2 * n, 2), :]
                out_steps.then_wait(nc.gpsimd.tensor_tensor(
                    tiles, tiles, o[:, 0:U - 1, :].rearrange("p (s u) j -> p s (u j)", s=2), ALU.add))
                nc.gpsimd.tensor_copy(ocls[:, bass.ds(n, 1), :], o[0:NBLK, U - 1:U, :]).then_inc(out_done[b], 1)
                pool.wait_ge(out_done[b], i + 2)

            root(0)
            root(1)
            norm(0)
            with pool.Fori(0, NB // 2 - 1) as i:
                for b in range(2):
                    root(2 * i + b + 2)
                    norm(2 * i + b + 1)
                    gate(i, b)
            root(NB)
            norm(NB - 1)
            gate(NB // 2 - 1, 0)
            gate(NB // 2 - 1, 1)
            pool.wait_ge(ocls_in, 16)
            nc.gpsimd.tensor_tensor(H[0:NB, CLS, :], H[0:NB, CLS, :], ocls_rows[:, :], ALU.add)

        @block.tensor
        def _(pe):
            pe.wait_ge(ident_done, 1)
            pe.wait_ge(weights_in, 16)

            def project(k):
                pe.wait_ge(xn_done, k + 1)
                for c in range(2):
                    for s in range(2):
                        last = nc.tensor.transpose(ps_xT[:, c, s * P:(s + 1) * P],
                                                   xn[:, s, c * P:(c + 1) * P], ident[:, :])
                last.then_inc(xT_done, 1)
                pe.wait_ge(xT_copied, k + 1)
                pe.wait_ge(kvq_copied, k)
                for s in range(2):
                    for j in range(3):
                        for c in range(2):
                            last = nc.tensor.matmul(ps_kvq[:, s, j, :], xT[:, c, s * P:(s + 1) * P],
                                                    w[:, c, j * D:(j + 1) * D], start=c == 0, stop=c == 1)
                last.then_inc(kvq_done, 1)

            project(0)
            project(1)
            with pe.Fori(2, NB + 1) as k:
                project(k)

        @block.scalar
        def _(act):
            def copy_xT(k):
                act.wait_ge(xT_done, k + 1)
                nc.scalar.activation(xT[:, :, :], ps_xT[:, :, :], ACT.Copy).then_inc(xT_copied, 1)

            def copy_kvq(k, b):
                act.wait_ge(kvq_done, k + 1)
                for s in range(2):
                    last = nc.scalar.activation(
                        kvq[b][:, :, s * NBLK:(s + 1) * NBLK, :].rearrange("p c u j -> p c (u j)"),
                        ps_kvq[:, s, 0:3, :], ACT.Copy)
                last.then_inc(kvq_copied, 1)

            def squash(n, g):
                lo, hi = GROUPS[g]
                act.wait_ge(pre_done[g], n + 1)
                nc.scalar.activation(S[:, lo:hi], S[:, lo:hi], ACT.Tanh).then_inc(tanh_done[g], 1)

            def gate(i, b):
                n = 2 * i + b
                act.wait_ge(sq_done, n + 1)
                act.wait_ge(out_done[b], i + 1)
                nc.scalar.activation(th[b][:, :, :], sq[b][:, :, :], ACT.Tanh, scale=0.5)
                nc.scalar.activation(sqh[b][:, :, :], sq[b][:, :, :], ACT.Copy, scale=0.5).then_inc(gate_done, 1)

            copy_xT(0)
            act.wait_ge(kvq_done, 1)
            nc.scalar.activation(row[:, :].rearrange("p (c d) -> p c d", c=3), ps_kvq[0:1, 0, 0:3, :],
                                 ACT.Copy).then_inc(row_copied, 1)
            act.wait_ge(row_copied, 1)
            act.sem_inc(kvq_copied, 1)
            copy_xT(1)
            copy_kvq(1, 0)
            with act.Fori(0, NB // 2 - 1) as i:
                for b in range(2):
                    n = 2 * i + b
                    squash(n, 0)
                    copy_xT(n + 2)
                    copy_kvq(n + 2, 1 - b)
                    squash(n, 1)
                    gate(i, b)
            squash(NB - 2, 0)
            copy_xT(NB)
            copy_kvq(NB, 1)
            squash(NB - 2, 1)
            gate(NB // 2 - 1, 0)
            squash(NB - 1, 0)
            squash(NB - 1, 1)
            gate(NB // 2 - 1, 1)

        @block.vector
        def _(dve):
            stat_steps = Steps(dve, m.sem("dve_stat"), 1)
            ksq_steps = Steps(dve, m.sem("dve_ksq"), 1)
            kn_steps = Steps(dve, m.sem("dve_kn"), 3)
            pre_steps = [Steps(dve, m.sem(f"dve_pre{g}"), 4) for g in range(2)]
            post_steps = [Steps(dve, m.sem(f"dve_post{g}"), 1) for g in range(2)]

            def normalise(k, tiles):
                stat_steps.round(k)
                for s in range(2):
                    last = nc.vector.bn_stats(stats[:, s, :], tiles(s))
                stat_steps.then_wait(last, (state_zero, 1))
                for s in range(2):
                    last = nc.vector.bn_aggr(mv[:, s, :], stats[:, s, :])
                last.then_inc(var_done, 1)
                dve.wait_ge(xT_done, k)
                dve.wait_ge(rstd_done, k + 1)
                for s in range(2):
                    last = nc.vector.tensor_scalar(xn[:, s, :], tiles(s), mv[:, s, 0:1], rstd[:, s:s + 1],
                                                   ALU.subtract, ALU.mult)
                last.then_inc(xn_done, 1)

            def sums(n, b):
                ksq_steps.round(n)
                dve.wait_ge(kvq_copied, n + 2)
                k = kvq[b][:, 0]
                ksq_steps.then_wait(nc.vector.tensor_tensor(ksq[:, :, :], k, k, ALU.mult))
                nc.vector.tensor_reduce(ss[:, :], ksq[:, :, :], axis=AX.X, op=ALU.add).then_inc(ss_done, 1)

            def unit(n, b):
                kn_steps.round(n)
                dve.wait_ge(nrm_done, n + 1)
                kn_steps.then_wait(nc.vector.tensor_scalar(nrm[:, :], nrm[:, :], 1e-6, None, ALU.add))
                kn_steps.then_wait(nc.vector.reciprocal(rn[:, :], nrm[:, :]))
                kn_steps.then_wait(nc.vector.tensor_tensor(kn[b][:, :, :], kvq[b][:, 0], over(rn[:, :], 2, BW),
                                                           ALU.mult))

            def pre(n, b, g):
                lo, hi = GROUPS[g]
                steps = pre_steps[g]
                steps.round(n)
                k = kn[b][:, lo:hi]
                s, t = S[:, lo:hi], T[:, lo:hi]
                steps.then_wait(nc.vector.tensor_tensor(t, s, over(k, 2, BW), ALU.mult))
                steps.then_wait(nc.vector.tensor_reduce(got[:, lo:hi], t, axis=AX.X, op=ALU.add))
                steps.then_wait(nc.vector.tensor_tensor(delta[:, lo:hi], kvq[b][:, 1, lo:hi], got[:, lo:hi],
                                                        ALU.subtract))
                steps.then_wait(nc.vector.tensor_tensor(t, over(delta[:, lo:hi], 3, BW), over(k, 2, BW), ALU.mult))
                nc.vector.tensor_tensor(s, s, t, ALU.add).then_inc(pre_done[g], 1)

            def post(i, b, g):
                n = 2 * i + b
                lo, hi = GROUPS[g]
                post_steps[g].round(n)
                t = T[:, lo:hi]
                dve.wait_ge(tanh_done[g], n + 1)
                post_steps[g].then_wait(nc.vector.tensor_tensor(t, S[:, lo:hi], over(kvq[b][:, 2, lo:hi], 2, BW),
                                                                ALU.mult))
                if g == 0:
                    dve.wait_ge(out_done[b], i + 1)
                r = nc.vector.tensor_reduce(sq[b][:, lo:hi], t, axis=AX.X, op=ALU.add)
                if g == 1:
                    r.then_inc(sq_done, 1)

            nc.vector.memset(S[:, :, :, :], 0.0).then_inc(state_zero, 1)
            dve.wait_ge(consts, 3)
            normalise(0, lambda s: H[:, CLS + s, :])
            normalise(1, lambda s: H[:, s, :])
            dve.wait_ge(row_in, 32)
            sums(0, 0)
            unit(0, 0)
            with dve.Fori(0, NB // 2 - 1) as i:
                for b in range(2):
                    n = 2 * i + b
                    pre(n, b, 0)
                    normalise(n + 2, lambda s: H[:, bass.ds(2 * n + 2 + s, 1), :])
                    pre(n, b, 1)
                    post(i, b, 0)
                    sums(n + 1, 1 - b)
                    post(i, b, 1)
                    unit(n + 1, 1 - b)
            n = NB - 2
            pre(n, 0, 0)
            normalise(NB, lambda s: H[:, 2 * n + 2 + s, :])
            pre(n, 0, 1)
            post(NB // 2 - 1, 0, 0)
            sums(n + 1, 1)
            post(NB // 2 - 1, 0, 1)
            unit(n + 1, 1)
            n = NB - 1
            pre(n, 1, 0)
            pre(n, 1, 1)
            post(NB // 2 - 1, 1, 0)
            post(NB // 2 - 1, 1, 1)


def route(nc, H, xs, place, share, whose, args):
    with ExitStack() as stack:
        m = Memory(nc, stack, "rt_")
        ident = m.sb("ident", [P, P])
        mhalf = m.sb("mhalf", [P, 2])
        eps = m.sb("eps", [P, 2])
        ones = m.sb("ones", [P, P])
        earlier = m.sb("earlier", [P, P])
        gw = m.sb("gw", [P, 2, E])
        gb = m.sb("gb", [P, E])
        first_wins = m.sb("first_wins", [P, E])
        is_token = m.sb("is_token", [P, NT])
        tile_no = m.sb("tile_no", [P, ROUTED])
        xn = m.sb("xn", [P, NT, D])
        xp = m.sb("xp", [P, 2, D])
        xT = m.sb("xT", [P, 2, 2 * P])
        stats = m.sb("stats", [P, 2, 6])
        mv = m.sb("mv", [P, 2, 2])
        rstd = m.sb("rstd", [P, 2])
        logits = m.sb("logits", [P, NT, E])
        top = m.sb("top", [P, NT])
        scores = m.sb("scores", [P, NT, E])
        biased = m.sb("biased", [P, NT, E])
        tied = m.sb("tied", [P, NT, E])
        chosen = [m.sb(f"chosen{k}", [P, NT, E]) for k in range(2)]
        taken = m.sb("taken", [P, NT, E])
        upto = m.sb("upto", [P, E, NT])
        one_row = m.sb("one_row", [P, NT])
        tiles_of = m.sb("tiles_of", [P, E])
        ends = m.sb("ends", [P, E])
        start = m.sb("start", [P, E])
        row = m.sb("row", [P, NT, E])
        tmp = m.sb("tmp", [P, NT, E])
        ended = m.sb("ended", [P, ROUTED, E])
        owner = m.sb("owner", [P, ROUTED])
        placef = m.sb("placef", [P, NT])

        ps_xT = m.ps("ps_xT", [P, 2, 2 * P])
        ps_lg = m.ps("ps_lg", [P, 2, E])
        ps_rank = m.ps("ps_rank", [P, NT, E])
        ps_total = m.ps("ps_total", [P, NT, E])

        consts_in = m.sem("consts_in")
        consts = m.sem("consts")
        ident_done = m.sem("ident_done")
        var_done = m.sem("var_done")
        rstd_done = m.sem("rstd_done")
        xn_done = m.sem("xn_done")
        xT_done = m.sem("xT_done")
        xT_copied = m.sem("xT_copied")
        lg_done = m.sem("lg_done")
        lg_copied = m.sem("lg_copied")
        less_max = m.sem("less_max")
        exp_done = m.sem("exp_done")
        taken_done = m.sem("taken_done")
        ranks_done = m.sem("ranks_done")
        placed = m.sem("placed")
        shared_out = m.sem("shared_out")
        rows_out = m.sem("rows_out")
        PAIRS = NT // 2

        block = stack.enter_context(nc.Block())

        @block.sync
        def _(sp):
            sp.dma_start(gw[:, :, :], args["gate_wT"].rearrange("(c p) e -> p c e", p=P)).then_inc(consts_in, 16)
            sp.dma_start(gb[:, :], args["gate_b"].partition_broadcast(P)).then_inc(consts_in, 16)
            sp.dma_start(earlier[:, :], args["earlier"]).then_inc(consts_in, 16)
            sp.dma_start(first_wins[:, :], args["first_wins"].partition_broadcast(P)).then_inc(consts_in, 16)
            sp.dma_start(is_token[:, :], args["is_token"]).then_inc(consts_in, 16)
            sp.dma_start(tile_no[:, :], args["tile_no"].partition_broadcast(P)).then_inc(consts_in, 16)
            sp.wait_ge(xT_copied, PAIRS)
            sp.dma_start(xs[ROUTED * MT:MTILES * MT, :].rearrange("(t p) d -> p t d", p=P), xn[:, :, :])\
                .then_inc(shared_out, 16)
            sp.wait_ge(shared_out, 16)

        @block.gpsimd
        def _(pool):
            nc.gpsimd.memset(mhalf[:, :], -0.5).then_inc(consts, 1)
            nc.gpsimd.memset(eps[:, :], EPS).then_inc(consts, 1)
            nc.gpsimd.memset(ones[:, :], 1.0).then_inc(consts, 1)
            nc.gpsimd.memset(one_row[:, :], 1.0).then_inc(consts, 1)
            nc.gpsimd.memset(ident[:, :], 0.0).then_inc(consts, 1)
            pool.wait_ge(consts, 5)
            nc.gpsimd.affine_select(out=ident[:, :], in_=ident[:, :], compare_op=ALU.not_equal, fill=1.0,
                                    base=0, pattern=[[-1, P]], channel_multiplier=1).then_inc(ident_done, 1)
            steps = Steps(pool, m.sem("pool_rstd"), 1)
            with pool.Fori(0, PAIRS) as k:
                steps.round(k)
                pool.wait_ge(var_done, k + 1)
                steps.then_wait(nc.gpsimd.tensor_tensor(rstd[:, :], mv[:, :, 1], eps[:, :], ALU.add))
                nc.gpsimd.tensor_tensor(rstd[:, :], rstd[:, :], mhalf[:, :], ALU.pow).then_inc(rstd_done, 1)
            pool.wait_ge(placed, 1)
            pool.wait_ge(xT_copied, PAIRS)
            for t in range(CLS + 1):
                n = P if t < CLS else NB
                for k in range(2):
                    pool.indirect_dma_start(
                        out=xs, out_offset=bass.IndirectOffsetOnAxis(ap=place[k][0:n, t, :], axis=0),
                        in_=xn[0:n, t, :], in_offset=None).then_inc(rows_out, 16)
            pool.wait_ge(rows_out, 16 * 2 * (CLS + 1))

        @block.tensor
        def _(pe):
            pe.wait_ge(ident_done, 1)
            pe.wait_ge(consts_in, 6 * 16)
            with pe.Fori(0, PAIRS) as k:
                pe.wait_ge(xn_done, k + 1)
                for c in range(2):
                    for s in range(2):
                        last = nc.tensor.transpose(ps_xT[:, c, s * P:(s + 1) * P],
                                                   xp[:, s, c * P:(c + 1) * P], ident[:, :])
                last.then_inc(xT_done, 1)
                pe.wait_ge(xT_copied, k + 1)
                pe.wait_ge(lg_copied, k + 1)
                for s in range(2):
                    for c in range(2):
                        last = nc.tensor.matmul(ps_lg[:, s, :], xT[:, c, s * P:(s + 1) * P], gw[:, c, :],
                                                start=c == 0, stop=c == 1)
                last.then_inc(lg_done, 1)
            pe.wait_ge(taken_done, 1)
            nc.tensor.matmul(ps_rank[:, :, :], earlier[:, :], taken[:, :, :], start=True, stop=True)
            nc.tensor.matmul(ps_total[:, :, :], ones[:, :], taken[:, :, :], start=True, stop=True)\
                .then_inc(ranks_done, 1)

        @block.scalar
        def _(act):
            with act.Fori(0, PAIRS) as k:
                act.wait_ge(xn_done, k + 1)
                nc.scalar.activation(xn[:, bass.ds(2 * k, 2), :], xp[:, :, :], ACT.Copy)
                act.wait_ge(xT_done, k + 1)
                nc.scalar.activation(xT[:, :, :], ps_xT[:, :, :], ACT.Copy).then_inc(xT_copied, 1)
            act.wait_ge(less_max, 1)
            nc.scalar.activation(scores[:, :, :], scores[:, :, :], ACT.Exp).then_inc(exp_done, 1)

        @block.vector
        def _(dve):
            stat_steps = Steps(dve, m.sem("dve_stat"), 1)
            dve.sem_inc(lg_copied, 1)
            dve.wait_ge(consts_in, 6 * 16)
            with dve.Fori(0, PAIRS) as k:
                stat_steps.round(k)
                for s in range(2):
                    last = nc.vector.bn_stats(stats[:, s, :], H[:, bass.ds(2 * k + s, 1), :])
                stat_steps.then_wait(last, (consts_in, 6 * 16))
                for s in range(2):
                    last = nc.vector.bn_aggr(mv[:, s, :], stats[:, s, :])
                last.then_inc(var_done, 1)
                dve.wait_ge(rstd_done, k + 1)
                for s in range(2):
                    last = nc.vector.tensor_scalar(xp[:, s, :], H[:, bass.ds(2 * k + s, 1), :],
                                                   mv[:, s, 0:1], rstd[:, s:s + 1], ALU.subtract, ALU.mult)
                last.then_inc(xn_done, 1)
                dve.wait_ge(lg_done, k + 1)
                nc.vector.tensor_copy(logits[:, bass.ds(2 * k, 2), :], ps_lg[:, :, :]).then_inc(lg_copied, 1)

            one = Steps(dve, m.sem("dve_route"), 100)
            dve.wait_ge(lg_copied, PAIRS + 1)
            go = one.then_wait
            v = nc.vector
            go(v.tensor_reduce(top[:, :], logits[:, :, :], axis=AX.X, op=ALU.max))
            v.tensor_tensor(scores[:, :, :], logits[:, :, :], over(top[:, :], 2, E), ALU.subtract)\
                .then_inc(less_max, 1)
            dve.wait_ge(exp_done, 1)
            go(v.tensor_reduce(top[:, :], scores[:, :, :], axis=AX.X, op=ALU.add))
            go(v.reciprocal(top[:, :], top[:, :]))
            go(v.tensor_tensor(scores[:, :, :], scores[:, :, :], over(top[:, :], 2, E), ALU.mult))
            go(v.tensor_tensor(biased[:, :, :], scores[:, :, :], over(gb[:, :], 1, NT), ALU.add))
            for k in range(2):
                go(v.tensor_reduce(top[:, :], biased[:, :, :], axis=AX.X, op=ALU.max))
                go(v.tensor_tensor(tied[:, :, :], biased[:, :, :], over(top[:, :], 2, E), ALU.is_equal))
                go(v.tensor_tensor(tied[:, :, :], tied[:, :, :], over(first_wins[:, :], 1, NT), ALU.mult))
                go(v.tensor_reduce(top[:, :], tied[:, :, :], axis=AX.X, op=ALU.max))
                go(v.tensor_tensor(chosen[k][:, :, :], tied[:, :, :], over(top[:, :], 2, E), ALU.is_equal))
                go(v.tensor_tensor(tmp[:, :, :], chosen[k][:, :, :], scores[:, :, :], ALU.mult))
                go(v.tensor_reduce(share[k][:, :], tmp[:, :, :], axis=AX.X, op=ALU.add))
                if k == 0:
                    go(v.tensor_scalar(tmp[:, :, :], chosen[k][:, :, :], -1e30, None, ALU.mult))
                    go(v.tensor_tensor(biased[:, :, :], biased[:, :, :], tmp[:, :, :], ALU.add))
            go(v.tensor_tensor(taken[:, :, :], chosen[0][:, :, :], chosen[1][:, :, :], ALU.add))
            v.tensor_tensor(taken[:, :, :], taken[:, :, :], over(is_token[:, :], 2, E), ALU.mult)\
                .then_inc(taken_done, 1)
            dve.wait_ge(ranks_done, 1)
            for e in range(E):
                last = v.tensor_tensor_scan(upto[:, e, :], one_row[:, :], ps_total[:, :, e], 0.0, ALU.mult, ALU.add)
            go(last)
            go(v.tensor_scalar(tiles_of[:, :], upto[:, :, NT - 1], 1.0 / MT, (MT - 1) / MT - 0.5 + 0.25 / MT,
                               ALU.mult, ALU.add))
            go(v.tensor_scalar(tiles_of[:, :], tiles_of[:, :], MAGIC, None, ALU.add))
            go(v.tensor_scalar(tiles_of[:, :], tiles_of[:, :], MAGIC, None, ALU.subtract))
            go(v.tensor_tensor_scan(ends[:, :], one_row[:, 0:E], tiles_of[:, :], 0.0, ALU.mult, ALU.add))
            go(v.tensor_tensor(start[:, :], ends[:, :], tiles_of[:, :], ALU.subtract))
            go(v.tensor_scalar(start[:, :], start[:, :], float(MT), None, ALU.mult))
            go(v.tensor_tensor(row[:, :, :], upto[:, :, :].rearrange("p e t -> p t e"), ps_total[:, :, :],
                               ALU.subtract))
            go(v.tensor_tensor(row[:, :, :], row[:, :, :], ps_rank[:, :, :], ALU.add))
            go(v.tensor_tensor(row[:, :, :], row[:, :, :], over(start[:, :], 1, NT), ALU.add))
            for k in range(2):
                go(v.tensor_tensor(tmp[:, :, :], row[:, :, :], chosen[k][:, :, :], ALU.mult))
                go(v.tensor_reduce(placef[:, :], tmp[:, :, :], axis=AX.X, op=ALU.add))
                go(v.tensor_copy(place[k][:, :, 0], placef[:, :]))
            go(v.tensor_tensor(ended[:, :, :], over(tile_no[:, :], 2, E), over(ends[:, :], 1, ROUTED), ALU.is_ge))
            go(v.tensor_reduce(owner[:, :], ended[:, :, :], axis=AX.X, op=ALU.add))
            go(v.tensor_scalar(owner[:, :], owner[:, :], float(E - 1), None, ALU.min))
            go(v.tensor_copy(whose[:, 0:ROUTED], owner[0:1, :]))
            v.memset(whose[:, ROUTED:MTILES], E).then_inc(placed, 1)


def experts(nc, xs, ys, whose, args):
    CH = I // P
    W13 = 2 * 2 * 2 * I
    COLS = W13 + CH * D + CH * 4
    with ExitStack() as stack:
        m = Memory(nc, stack, "ex_")
        ident = m.sb("ident", [P, P])
        wt = [m.sb(f"wt{b}", [P, COLS]) for b in range(2)]
        w13 = [w[:, 0:W13].rearrange("p (c w g i) -> p c w g i", c=2, w=2, g=2) for w in wt]
        w2 = [w[:, W13:W13 + CH * D].rearrange("p (h d) -> p h d", h=CH) for w in wt]
        b13 = [w[:, W13 + CH * D:COLS].rearrange("p (h w g) -> p h w g", h=CH, w=2) for w in wt]
        b2 = [m.sb(f"b2{b}", [P, D]) for b in range(2)]
        xrow = [m.sb(f"xrow{b}", [P, 2, D]) for b in range(2)]
        xT = [m.sb(f"xT{b}", [P, 2, MT]) for b in range(2)]
        x3 = m.sb("x3", [P, 2, MT])
        gl = m.sb("gl", [P, 2, MT])
        glc = m.sb("glc", [P, 2, MT])
        th = m.sb("th", [P, MT])
        gate = m.sb("gate", [P, MT])
        hT = [m.sb(f"hT{b}", [P, CH, MT]) for b in range(2)]
        yrow = [m.sb(f"yrow{b}", [P, 2, D]) for b in range(2)]

        ps_xT = m.ps("ps_xT", [P, 2, MT])
        ps_up = [m.ps(f"ps_up{b}", [P, 2, 2, MT]) for b in range(2)]
        ps_y = m.ps("ps_y", [P, 2, D])

        ident_done = m.sem("ident_done")
        w_in = [m.sem(f"w_in{b}") for b in range(2)]
        x_in = [m.sem(f"x_in{b}") for b in range(2)]
        xT_done = m.sem("xT_done")
        xT_copied = m.sem("xT_copied")
        up_done = m.sem("up_done")
        x3_done = m.sem("x3_done")
        half_gate = m.sem("half_gate")
        th_done = m.sem("th_done")
        h_done = m.sem("h_done")
        down_done = m.sem("down_done")
        y_copied = m.sem("y_copied")
        y_out = [m.sem(f"y_out{b}") for b in range(2)]

        xs_v = xs.rearrange("(j s p) d -> j p s d", s=2, p=P)
        ys_v = ys.rearrange("(j s p) d -> j p s d", s=2, p=P)
        J = MTILES
        assert J % 2 == 1

        block = stack.enter_context(nc.Block())

        @block.sync
        def _(sp):
            def load(i, b, first):
                j = 2 * i + b
                e = sp.value_load(whose[0:1, bass.ds(j, 1)], min_val=0, max_val=E)
                if not first:
                    sp.wait_ge(down_done, j - 1)
                    sp.wait_ge(y_copied, j)
                sp.dma_start(xrow[b][:, :, :], xs_v[bass.ds(j, 1)].rearrange("o p s d -> (o p) s d"))\
                    .then_inc(x_in[b], 16)
                sp.dma_start(wt[b][:, :], args["experts"][bass.ds(e, 1)].rearrange("o p n -> (o p) n"))\
                    .then_inc(w_in[b], 16)
                sp.dma_start(b2[b][:, :], args["experts_b2"][bass.ds(e, 1), :].broadcast_to([P, D]))\
                    .then_inc(w_in[b], 16)

            load(0, 0, True)
            load(0, 1, True)
            with sp.Fori(1, J // 2) as i:
                load(i, 0, False)
                load(i, 1, False)
            load(J // 2, 0, False)

        @block.gpsimd
        def _(pool):
            zeroed = m.sem("zeroed")
            nc.gpsimd.memset(ident[:, :], 0.0).then_inc(zeroed, 1)
            pool.wait_ge(zeroed, 1)
            nc.gpsimd.affine_select(out=ident[:, :], in_=ident[:, :], compare_op=ALU.not_equal, fill=1.0,
                                    base=0, pattern=[[-1, P]], channel_multiplier=1).then_inc(ident_done, 1)

        @block.tensor
        def _(pe):
            def turn(i, b):
                j = 2 * i + b
                pe.wait_ge(x_in[b], 16 * i + 16)
                for c in range(2):
                    for s in range(2):
                        last = nc.tensor.transpose(ps_xT[:, c, s * P:(s + 1) * P],
                                                   xrow[b][:, s, c * P:(c + 1) * P], ident[:, :])
                last.then_inc(xT_done, 1)

            def up(i, b, h, first):
                j = 2 * i + b
                if h == 0:
                    pe.wait_ge(w_in[b], 32 * i + 32)
                    pe.wait_ge(xT_copied, j + 1)
                if not first:
                    pe.wait_ge(half_gate, 4 * j + h - 1)
                for w in range(2):
                    for g in range(2):
                        for c in range(2):
                            last = nc.tensor.matmul(ps_up[h % 2][:, w, g, :],
                                                    w13[b][:, c, w, g, h * P:(h + 1) * P], xT[b][:, c, :],
                                                    start=c == 0, stop=c == 1)
                last.then_inc(up_done, 1)

            def down(i, b):
                j = 2 * i + b
                pe.wait_ge(h_done, 4 * j + 4)
                pe.wait_ge(y_copied, j + 1)
                for s in range(2):
                    for h in range(CH):
                        last = nc.tensor.matmul(ps_y[:, s, :], hT[b][:, h, s * P:(s + 1) * P], w2[b][:, h, :],
                                                start=h == 0, stop=h == CH - 1)
                last.then_inc(down_done, 1)

            def tile(i, b, first=False, last=False):
                up(i, b, 0, first)
                if not first:
                    down(i - 1 + b, 1 - b)
                up(i, b, 1, first)
                up(i, b, 2, False)
                up(i, b, 3, False)
                if not last:
                    turn(i + b, 1 - b)

            pe.wait_ge(ident_done, 1)
            turn(0, 0)
            tile(0, 0, first=True)
            with pe.Fori(0, J // 2 - 1) as i:
                tile(i, 1)
                tile(i + 1, 0)
            tile(J // 2 - 1, 1)
            tile(J // 2, 0, last=True)
            down(J // 2, 0)

        @block.scalar
        def _(act):
            def copy(i, b):
                j = 2 * i + b
                act.wait_ge(xT_done, j + 1)
                nc.scalar.activation(xT[b][:, :, :], ps_xT[:, :, :], ACT.Copy).then_inc(xT_copied, 1)

            def chunk(i, b, h, first):
                q = 4 * (2 * i + b) + h
                act.wait_ge(up_done, q + 1)
                if not first:
                    act.wait_ge(half_gate, q)
                for g in range(2):
                    last = nc.scalar.activation(x3[:, g, :], ps_up[h % 2][:, 1, g, :], ACT.Identity,
                                                bias=b13[b][:, h, 1, g:g + 1])
                last.then_inc(x3_done, 1)
                act.wait_ge(half_gate, q + 1)
                nc.scalar.activation(th[:, :], glc[:, 0, :], ACT.Tanh, scale=1.702).then_inc(th_done, 1)

            def store(i, b):
                j = 2 * i + b
                act.wait_ge(y_copied, j + 2)
                act.dma_start(ys_v[bass.ds(j, 1)].rearrange("o p s d -> (o p) s d"), yrow[b][:, :, :])\
                    .then_inc(y_out[b], 16)

            def tile(i, b, first=False, last=False):
                for h in range(CH):
                    chunk(i, b, h, first and h == 0)
                    if h == 2 and not first:
                        store(i - 1 + b, 1 - b)
                if not last:
                    copy(i + b, 1 - b)

            for b in range(2):
                act.sem_inc(y_out[b], 16)
            copy(0, 0)
            tile(0, 0, first=True)
            with act.Fori(0, J // 2 - 1) as i:
                tile(i, 1)
                tile(i + 1, 0)
            tile(J // 2 - 1, 1)
            tile(J // 2, 0, last=True)
            store(J // 2, 0)
            act.wait_ge(y_out[0], 16 * (J // 2 + 2))
            act.wait_ge(y_out[1], 16 * (J // 2 + 1))

        @block.vector
        def _(dve):
            head_steps = Steps(dve, m.sem("dve_head"), 1)
            tail_steps = Steps(dve, m.sem("dve_tail"), 1)
            dve.sem_inc(y_copied, 1)

            def chunk(i, b, h):
                q = 4 * (2 * i + b) + h
                head_steps.round(q)
                tail_steps.round(q)
                dve.wait_ge(x3_done, q + 1)
                for g in range(2):
                    last = nc.vector.scalar_tensor_tensor(gl[:, g, :], ps_up[h % 2][:, 0, g, :],
                                                          b13[b][:, h, 0, g:g + 1], x3[:, g, :], ALU.add, ALU.mult)
                head_steps.then_wait(last)
                nc.vector.tensor_scalar(glc[:, 0, :], gl[:, 0, :], 7.0, 0.5, ALU.min, ALU.mult)
                nc.vector.tensor_scalar(glc[:, 1, :], gl[:, 1, :], -7.0, 7.0, ALU.max, ALU.min)\
                    .then_inc(half_gate, 1)
                dve.wait_ge(th_done, q + 1)
                tail_steps.then_wait(nc.vector.scalar_tensor_tensor(gate[:, :], th[:, :], 1.0, glc[:, 0, :],
                                                                    ALU.add, ALU.mult))
                nc.vector.scalar_tensor_tensor(hT[b][:, h, :], glc[:, 1, :], 1.0, gate[:, :],
                                               ALU.add, ALU.mult).then_inc(h_done, 1)

            def copy_y(i, b):
                j = 2 * i + b
                dve.wait_ge(down_done, j + 1)
                dve.wait_ge(y_out[b], 16 * i + 16)
                nc.vector.tensor_tensor(yrow[b][:, :, :], ps_y[:, :, :], over(b2[b][:, :], 1, 2), ALU.add)\
                    .then_inc(y_copied, 1)

            def tile(i, b, first=False):
                for h in range(CH):
                    chunk(i, b, h)
                    if h == 1 and not first:
                        copy_y(i - 1 + b, 1 - b)

            tile(0, 0, first=True)
            with dve.Fori(0, J // 2 - 1) as i:
                tile(i, 1)
                tile(i + 1, 0)
            tile(J // 2 - 1, 1)
            tile(J // 2, 0)
            copy_y(J // 2, 0)


def combine(nc, H, ys, place, share):
    with ExitStack() as stack:
        m = Memory(nc, stack, "cb_")
        N = CLS + 1
        routed = [m.sb(f"routed{k}", [P, N, D]) for k in range(2)]
        shared = m.sb("shared", [P, N, D])
        zeroed = m.sem("zeroed")
        gathered = m.sem("gathered")
        shared_in = m.sem("shared_in")
        added = m.sem("added")
        block = stack.enter_context(nc.Block())

        @block.sync
        def _(sp):
            sp.dma_start(shared[:, :, :], ys[ROUTED * MT:ROUTED * MT + N * P, :].rearrange("(t p) d -> p t d", p=P))\
                .then_inc(shared_in, 16)

        @block.gpsimd
        def _(pool):
            for t in range(N):
                n = P if t < CLS else NB
                for k in range(2):
                    pool.indirect_dma_start(
                        out=routed[k][0:n, t, :], out_offset=None, in_=ys,
                        in_offset=bass.IndirectOffsetOnAxis(ap=place[k][0:n, t, :], axis=0)).then_inc(gathered, 16)

        @block.vector
        def _(dve):
            steps = Steps(dve, added, 3)
            dve.wait_ge(shared_in, 16)
            dve.wait_ge(gathered, 16 * 2 * N)

            def add(t, n):
                at = bass.ds(t, 1)
                h = H[0:n, at, :]
                steps.then_wait(nc.vector.tensor_tensor(h, h, shared[0:n, at, :], ALU.add))
                for k in range(2):
                    steps.then_wait(nc.vector.scalar_tensor_tensor(h, routed[k][0:n, at, :], share[k][0:n, at], h,
                                                                   ALU.mult, ALU.add))

            with dve.Fori(0, CLS) as t:
                steps.round(t)
                add(t, P)
            steps.round(CLS)
            add(CLS, NB)


def queries_keys_values(nc, H, qkv, class_keys, vcls, args):
    G = AH // 4
    with ExitStack() as stack:
        m = Memory(nc, stack, "pj_")
        w = m.sb("w", [P, 2, 3 * D])
        cos = m.sb("cos", [P, 2, DH])
        sin = m.sb("sin", [P, 2, DH])
        ident = m.sb("ident", [P, P])
        mhalf = m.sb("mhalf", [P, 2])
        eps = m.sb("eps", [P, 2])
        stats = m.sb("stats", [P, 2, 6])
        mv = m.sb("mv", [P, 2, 2])
        rstd = m.sb("rstd", [P, 2])
        xp = m.sb("xp", [P, 2, D])
        xT = m.sb("xT", [P, 2, 2 * P])
        straight = m.sb("straight", [P, 2, 2 * D])
        crossed = m.sb("crossed", [P, 2, 2 * D])
        kpad = m.sb("kpad", [P, AH, 32])

        ps_xT = m.ps("ps_xT", [P, 2, 2 * P])
        ps_p = m.ps("ps_p", [P, 2, 4, D])
        ps_kT = m.ps("ps_kT", [P, G, P])

        consts_in = m.sem("consts_in")
        consts = m.sem("consts")
        zeroed = m.sem("zeroed")
        ident_done = m.sem("ident_done")
        var_done = m.sem("var_done")
        rstd_done = m.sem("rstd_done")
        xp_done = m.sem("xp_done")
        xT_done = m.sem("xT_done")
        xT_copied = m.sem("xT_copied")
        p_done = m.sem("p_done")
        v_copied = m.sem("v_copied")
        turned = m.sem("turned")
        added = m.sem("added")
        kpad_done = m.sem("kpad_done")
        kT_done = m.sem("kT_done")
        keys_done = m.sem("keys_done")
        vcls_out = m.sem("vcls_out")
        PAIRS = NT // 2

        block = stack.enter_context(nc.Block())

        @block.sync
        def _(sp):
            sp.dma_start(w[:, :, :], args["att_w"].rearrange("(c p) n -> p c n", p=P)).then_inc(consts_in, 16)
            sp.dma_start(cos[:, :, :], args["rope_cos"].rearrange("(s p) j -> p s j", p=P)).then_inc(consts_in, 16)
            sp.dma_start(sin[:, :, :], args["rope_sin"].rearrange("(s p) j -> p s j", p=P)).then_inc(consts_in, 16)
            sp.wait_ge(v_copied, PAIRS + 1)
            sp.dma_start(vcls, qkv[0:NB, CLS, 2 * D:3 * D]).then_inc(vcls_out, 16)
            sp.wait_ge(vcls_out, 16)

        @block.gpsimd
        def _(pool):
            pool.sem_inc(added, 1)
            nc.gpsimd.memset(mhalf[:, :], -0.5).then_inc(consts, 1)
            nc.gpsimd.memset(eps[:, :], EPS).then_inc(consts, 1)
            nc.gpsimd.memset(ident[:, :], 0.0).then_inc(consts, 1)
            pool.wait_ge(consts, 3)
            nc.gpsimd.affine_select(out=ident[:, :], in_=ident[:, :], compare_op=ALU.not_equal, fill=1.0,
                                    base=0, pattern=[[-1, P]], channel_multiplier=1).then_inc(ident_done, 1)
            nc.gpsimd.memset(kpad[:, :, :], 0.0).then_inc(zeroed, 1)
            nc.gpsimd.memset(class_keys[:, :, :, :], 0.0).then_inc(zeroed, 1)
            steps = Steps(pool, m.sem("pool_rstd"), 1)

            def root(k):
                steps.round(k)
                pool.wait_ge(var_done, k + 1)
                steps.then_wait(nc.gpsimd.tensor_tensor(rstd[:, :], mv[:, :, 1], eps[:, :], ALU.add))
                nc.gpsimd.tensor_tensor(rstd[:, :], rstd[:, :], mhalf[:, :], ALU.pow).then_inc(rstd_done, 1)

            root(0)
            with pool.Fori(0, PAIRS - 1) as k:
                root(k + 1)
                pool.wait_ge(turned, k + 2)
                nc.gpsimd.tensor_tensor(qkv[:, bass.ds(2 * k, 2), 0:2 * D], straight[:, :, :], crossed[:, :, :],
                                        ALU.add).then_inc(added, 1)

        @block.tensor
        def _(pe):
            pe.wait_ge(ident_done, 1)
            pe.wait_ge(consts_in, 3 * 16)
            with pe.Fori(0, PAIRS) as k:
                pe.wait_ge(xp_done, k + 1)
                for c in range(2):
                    for s in range(2):
                        last = nc.tensor.transpose(ps_xT[:, c, s * P:(s + 1) * P],
                                                   xp[:, s, c * P:(c + 1) * P], ident[:, :])
                last.then_inc(xT_done, 1)
                pe.wait_ge(xT_copied, k + 1)
                pe.wait_ge(v_copied, k + 1)
                pe.wait_ge(turned, k + 1)
                for s in range(2):
                    for j in range(3):
                        for c in range(2):
                            last = nc.tensor.matmul(ps_p[:, s, j, :], xT[:, c, s * P:(s + 1) * P],
                                                    w[:, c, j * D:(j + 1) * D], start=c == 0, stop=c == 1)
                last.then_inc(p_done, 1)
            pe.wait_ge(kpad_done, 1)
            for g in range(G):
                last = nc.tensor.transpose(ps_kT[:, g, :], kpad[:, 4 * g:4 * g + 4, :], ident[:, :])
            last.then_inc(kT_done, 1)

        @block.scalar
        def _(act):
            act.sem_inc(v_copied, 1)
            with act.Fori(0, PAIRS) as k:
                act.wait_ge(xT_done, k + 1)
                nc.scalar.activation(xT[:, :, :], ps_xT[:, :, :], ACT.Copy).then_inc(xT_copied, 1)
                act.wait_ge(p_done, k + 1)
                for s in range(2):
                    last = nc.scalar.activation(qkv[:, bass.ds(2 * k + s, 1), 2 * D:3 * D], ps_p[:, s, 2:3, :],
                                                ACT.Copy)
                last.then_inc(v_copied, 1)
            nc.scalar.activation(qkv[:, CLS:NT, 0:D], ps_p[:, :, 2, :], ACT.Copy)
            act.wait_ge(zeroed, 1)
            nc.scalar.activation(kpad[:, :, 0:DH], ps_p[:, 0, 1, :].rearrange("p (h j) -> p h j", h=AH),
                                 ACT.Copy).then_inc(kpad_done, 1)
            act.wait_ge(kT_done, 1)
            act.wait_ge(zeroed, 2)
            for j in range(4):
                rows = slice(32 * j, 32 * j + 32)
                last = nc.scalar.activation(class_keys[rows, :, j, :], ps_kT[rows, :, 0:NB], ACT.Copy)
            last.then_inc(keys_done, 1)

        @block.vector
        def _(dve):
            stat_steps = Steps(dve, m.sem("dve_stat"), 1)
            dve.sem_inc(turned, 1)
            dve.wait_ge(consts_in, 3 * 16)

            def normalise(k):
                stat_steps.round(k)
                for s in range(2):
                    last = nc.vector.bn_stats(stats[:, s, :], H[:, bass.ds(2 * k + s, 1), :])
                stat_steps.then_wait(last, (consts_in, 3 * 16))
                for s in range(2):
                    last = nc.vector.bn_aggr(mv[:, s, :], stats[:, s, :])
                last.then_inc(var_done, 1)
                dve.wait_ge(rstd_done, k + 1)
                dve.wait_ge(xT_done, k)
                for s in range(2):
                    last = nc.vector.tensor_scalar(xp[:, s, :], H[:, bass.ds(2 * k + s, 1), :],
                                                   mv[:, s, 0:1], rstd[:, s:s + 1], ALU.subtract, ALU.mult)
                last.then_inc(xp_done, 1)

            normalise(0)
            with dve.Fori(0, PAIRS - 1) as k:
                normalise(k + 1)
                dve.wait_ge(p_done, k + 1)
                dve.wait_ge(added, k + 1)
                hd = DH // 2
                for s in range(2):
                    p = ps_p[:, s, 0:2, :].rearrange("p a (h j) -> p (a h) j", j=DH)
                    o = straight[:, s, :].rearrange("p (h j) -> p h j", j=DH)
                    x = crossed[:, s, :].rearrange("p (h j) -> p h j", j=DH)
                    nc.vector.tensor_tensor(o, p, over(cos[:, s, :], 1, 2 * AH), ALU.mult)
                    nc.vector.tensor_tensor(x[:, :, 0:hd], p[:, :, hd:DH], over(sin[:, s, 0:hd], 1, 2 * AH),
                                            ALU.mult)
                    last = nc.vector.tensor_tensor(x[:, :, hd:DH], p[:, :, 0:hd],
                                                   over(sin[:, s, hd:DH], 1, 2 * AH), ALU.mult)
                last.then_inc(turned, 1)


def attention(nc, qkv, class_keys, vcls, args):
    G = AH // 4
    R = AH // 2
    QK = 0.25
    with ExitStack() as stack:
        m = Memory(nc, stack, "at_")
        ident = m.sb("ident", [P, P])
        ident16 = m.sb("ident16", [P, P], BF16)
        hidden = m.sb("hidden", [P, P], BF16)
        pad = m.sb("pad", [P, 2, 2, AH, 32])
        v1 = m.sb("v1", [P, 2, AH, DH + 1])
        vc = m.sb("vc", [P, D])
        qkT = m.sb("qkT", [P, 2, G, 2, P])
        sc = m.sb("sc", [P, 2, AH])
        mx = m.sb("mx", [P, AH, 2])
        nmx = m.sb("nmx", [P, AH, 2])
        pr = [m.sb(f"pr{b}", [P, 2, 3 * P]) for b in range(2)]
        pT = [m.sb(f"pT{b}", [P, 2, 3 * P]) for b in range(2)]
        pc = m.sb("pc", [P, 2, AH])
        den = m.sb("den", [P, 2, AH])
        o = m.sb("o", [P, 2, AH, DH])

        ps_s = [m.ps(f"ps_s{b}", [P, 2, 512]) for b in range(2)]
        ps_t = m.ps("ps_t", [P, 2, 512])
        ps_o = m.ps("ps_o", [P, 2, 512])
        ps_v = ps_o[:, :, 0:AH * (DH + 1)].rearrange("p q (h j) -> p q h j", h=AH)
        ps_c = ps_o[:, :, 288:288 + AH]

        zeroed = m.sem("zeroed")
        ident_done = m.sem("ident_done")
        ident16_done = m.sem("ident16_done")
        padded = m.sem("padded")
        v1_done = m.sem("v1_done")
        vc_in = m.sem("vc_in")
        turned = m.sem("turned")
        q_copied = m.sem("q_copied")
        k_copied = m.sem("k_copied")
        sc_done = m.sem("sc_done")
        sc_copied = m.sem("sc_copied")
        s_done = m.sem("s_done")
        nmx_done = m.sem("nmx_done")
        exp_done = m.sem("exp_done")
        pT_done = m.sem("pT_done")
        pT_copied = m.sem("pT_copied")
        pv_done = m.sem("pv_done")
        sc_less = m.sem("sc_less")
        pc_done = m.sem("pc_done")
        o_read = m.sem("o_read")
        o_done = m.sem("o_done")

        block = stack.enter_context(nc.Block())

        @block.sync
        def _(sp):
            sp.dma_start(vc[:, :], vcls[0:1, :].broadcast_to([P, D])).then_inc(vc_in, 16)
            with sp.Fori(1, NB) as n:
                sp.wait_ge(o_read, n + 1)
                sp.dma_start(vc[:, :], vcls[bass.ds(n, 1), :].broadcast_to([P, D])).then_inc(vc_in, 16)

        @block.gpsimd
        def _(pool):
            nc.gpsimd.memset(ident[:, :], 0.0).then_inc(zeroed, 1)
            nc.gpsimd.memset(hidden[:, :], 0.0).then_inc(zeroed, 1)
            nc.gpsimd.memset(pad[:, :, :, :, :], 0.0).then_inc(zeroed, 1)
            nc.gpsimd.memset(v1[:, :, :, DH:DH + 1], 1.0).then_inc(zeroed, 1)
            pool.wait_ge(zeroed, 4)
            nc.gpsimd.affine_select(out=ident[:, :], in_=ident[:, :], compare_op=ALU.not_equal, fill=1.0,
                                    base=0, pattern=[[-1, P]], channel_multiplier=1).then_inc(ident_done, 1)
            nc.gpsimd.affine_select(out=hidden[:, :], in_=hidden[:, :], compare_op=ALU.is_ge, fill=-1e30,
                                    base=0, pattern=[[-1, P]], channel_multiplier=1).then_inc(ident_done, 1)
            pool.wait_ge(ident_done, 2)
            nc.gpsimd.tensor_copy(ident16[:, :], ident[:, :]).then_inc(ident16_done, 1)
            with pool.Fori(0, NB) as n:
                pool.wait_ge(pv_done, R * n + 1)
                nc.gpsimd.tensor_copy(v1[:, :, :, 0:DH], qkv[:, bass.ds(2 * n, 2), 2 * D:3 * D].rearrange(
                    "p s (h j) -> p s h j", h=AH)).then_inc(v1_done, 1)

        @block.tensor
        def _(pe):
            pe.wait_ge(ident16_done, 1)
            pe.sem_inc(pv_done, 1)

            def scores(n, r):
                b = r % 2
                if r >= 2:
                    pe.wait_ge(exp_done, R * n + r)
                for hh in range(2):
                    h = 2 * r + hh
                    g, rows = h // 4, slice(32 * (h % 4), 32 * (h % 4) + DH)
                    q, k = qkT[rows, 0, g], qkT[rows, 1, g]
                    nc.tensor.matmul(ps_s[b][:, hh, 0:P], q[:, 0, :], k[:, 0, :], start=True, stop=False)
                    nc.tensor.matmul(ps_s[b][:, hh, 0:P], ident16[:, :], hidden[:, :], start=False, stop=True)
                    nc.tensor.matmul(ps_s[b][:, hh, P:3 * P], q[:, 1, :], k.rearrange("p s t -> p (s t)"),
                                     start=True, stop=False)
                    last = nc.tensor.matmul(ps_s[b][:, hh, 2 * P:3 * P], ident16[:, :], hidden[:, :],
                                            start=False, stop=True)
                last.then_inc(s_done, 1)

            def turn(n, r):
                pe.wait_ge(exp_done, R * n + r + 2)
                pe.wait_ge(pT_copied, R * n + r + 1)
                for hh in range(2):
                    for c in range(3):
                        last = nc.tensor.transpose(ps_t[:, hh, c * P:(c + 1) * P],
                                                   pr[r % 2][:, hh, c * P:(c + 1) * P], ident[:, :])
                last.then_inc(pT_done, 1)

            def values(n, r):
                pe.wait_ge(pT_copied, R * n + r + 2)
                for hh in range(2):
                    h = 2 * r + hh
                    p = pT[r % 2]
                    nc.tensor.matmul(ps_v[:, 0, h, :], p[:, hh, 0:P], v1[:, 0, h, :], start=True, stop=True)
                    nc.tensor.matmul(ps_v[:, 1, h, :], p[:, hh, P:2 * P], v1[:, 0, h, :], start=True, stop=False)
                    last = nc.tensor.matmul(ps_v[:, 1, h, :], p[:, hh, 2 * P:3 * P], v1[:, 1, h, :],
                                            start=False, stop=True)
                last.then_inc(pv_done, 1)

            with pe.Fori(0, NB) as n:
                pe.wait_ge(padded, n + 1)
                pe.wait_ge(exp_done, R * n + 1)
                for a in range(2):
                    t = ps_s[a][:, :, :].rearrange("p a (g s t) -> p (a g) s t", g=2, s=2)
                    for g in range(G):
                        for s in range(2):
                            last = nc.tensor.transpose(t[:, g, s, :], pad[:, s, a, 4 * g:4 * g + 4, :], ident[:, :])
                last.then_inc(turned, 1)
                pe.wait_ge(q_copied, n + 1)
                pe.wait_ge(o_read, n + 1)
                for s in range(2):
                    for g in range(G):
                        last = nc.tensor.matmul(ps_c[:, s, 4 * g:4 * g + 4], qkT[:, 0, g, s, :],
                                                class_keys[:, g, :, bass.ds(n, 1)], start=True, stop=True)
                last.then_inc(sc_done, 1)
                pe.wait_ge(k_copied, n + 1)
                pe.wait_ge(v1_done, n + 1)
                scores(n, 0)
                for r in range(R):
                    if r + 1 < R:
                        scores(n, r + 1)
                    turn(n, r)
                    if r:
                        values(n, r - 1)
                values(n, R - 1)

        @block.scalar
        def _(act):
            act.wait_ge(zeroed, 4)
            act.sem_inc(exp_done, 1)

            def pads(n):
                act.wait_ge(turned, n)
                for s in range(2):
                    last = nc.scalar.activation(
                        pad[:, s, :, :, 0:DH].rearrange("p a h j -> p (a h) j"),
                        qkv[:, bass.ds(2 * n + s, 1), 0:2 * D].rearrange("p o (h j) -> p (o h) j", j=DH),
                        ACT.Copy)
                last.then_inc(padded, 1)

            def sequence(n):
                act.wait_ge(turned, n + 1)
                nc.scalar.activation(qkT[:, 0].rearrange("p g s t -> p (g s t)"),
                                     ps_s[0][:, :, :].rearrange("p a b -> p (a b)"), ACT.Copy).then_inc(q_copied, 1)
                for r in range(R):
                    act.wait_ge(nmx_done, R * n + r + 1)
                    if r >= 2:
                        act.wait_ge(pT_done, R * n + r - 1)
                    for hh in range(2):
                        h = 2 * r + hh
                        nc.scalar.activation(pr[r % 2][:, hh, 0:P], ps_s[r % 2][:, hh, 0:P], ACT.Exp,
                                             bias=nmx[:, h, 0:1], scale=QK)
                        last = nc.scalar.activation(pr[r % 2][:, hh, P:3 * P], ps_s[r % 2][:, hh, P:3 * P], ACT.Exp,
                                                    bias=nmx[:, h, 1:2], scale=QK)
                    last.then_inc(exp_done, 1)
                act.wait_ge(sc_less, n + 1)
                nc.scalar.activation(pc[:, :, :], pc[:, :, :], ACT.Exp, scale=QK).then_inc(pc_done, 1)

            pads(0)
            with act.Fori(0, NB - 1) as n:
                sequence(n)
                pads(n + 1)
            sequence(NB - 1)

        @block.vector
        def _(dve):
            mx_steps = Steps(dve, m.sem("dve_mx"), 2)
            out_steps = Steps(dve, m.sem("dve_out"), 1)
            dve.sem_inc(pT_copied, 1)
            dve.sem_inc(o_read, 1)

            def maxima(n, r):
                mx_steps.round(R * n + r)
                dve.wait_ge(s_done, R * n + r + 1)
                two = slice(2 * r, 2 * r + 2)
                nc.vector.tensor_reduce(mx[:, two, 0], ps_s[r % 2][:, :, 0:P], axis=AX.X, op=ALU.max)
                mx_steps.then_wait(nc.vector.tensor_reduce(mx[:, two, 1], ps_s[r % 2][:, :, P:3 * P],
                                                           axis=AX.X, op=ALU.max))
                mx_steps.then_wait(nc.vector.tensor_tensor(mx[:, two, :], mx[:, two, :],
                                                           sc[:, :, two].rearrange("p q h -> p h q"), ALU.max))
                nc.vector.tensor_scalar(nmx[:, two, :], mx[:, two, :], -QK, None, ALU.mult).then_inc(nmx_done, 1)

            def copy_pT(n, r):
                dve.wait_ge(pT_done, R * n + r + 1)
                if r >= 2:
                    dve.wait_ge(pv_done, R * n + r)
                nc.vector.tensor_copy(pT[r % 2][:, :, :], ps_t[:, :, 0:3 * P]).then_inc(pT_copied, 1)

            with dve.Fori(0, NB) as n:
                dve.wait_ge(turned, n + 1)
                nc.vector.tensor_copy(qkT[:, 1].rearrange("p g s t -> p (g s t)"),
                                      ps_s[1][:, :, :].rearrange("p a b -> p (a b)")).then_inc(k_copied, 1)
                dve.wait_ge(sc_done, n + 1)
                nc.vector.tensor_copy(sc[:, :, :], ps_c).then_inc(sc_copied, 1)
                dve.wait_ge(sc_copied, n + 1)
                maxima(n, 0)
                for r in range(R):
                    if r + 1 < R:
                        maxima(n, r + 1)
                    else:
                        dve.wait_ge(nmx_done, R * n + R)
                        nc.vector.tensor_tensor(pc[:, :, :], sc[:, :, :], mx[:, :, :].rearrange("p h q -> p q h"),
                                                ALU.subtract).then_inc(sc_less, 1)
                    copy_pT(n, r)
                out_steps.round(n)
                dve.wait_ge(pc_done, n + 1)
                dve.wait_ge(vc_in, 16 * n + 16)
                dve.wait_ge(pv_done, R * n + R + 1)
                for q in range(2):
                    nc.vector.tensor_tensor(o[:, q], over(pc[:, q, :], 2, DH),
                                            vc[:, :].rearrange("p (h j) -> p h j", h=AH), ALU.mult)
                out_steps.then_wait(nc.vector.tensor_tensor(den[:, :, :], ps_v[:, :, :, DH], pc[:, :, :], ALU.add))
                nc.vector.reciprocal(den[:, :, :], den[:, :, :])
                for q in range(2):
                    last = nc.vector.tensor_tensor(o[:, q], o[:, q], ps_v[:, q, :, 0:DH], ALU.add)
                last.then_inc(o_read, 1)
                dve.wait_ge(o_read, n + 2)
                for q in range(2):
                    last = nc.vector.tensor_tensor(
                        qkv[:, bass.ds(2 * n + q, 1), 0:D].rearrange("p o (h j) -> p (o h) j", h=AH), o[:, q],
                        over(den[:, q, :], 2, DH), ALU.mult)
                last.then_inc(o_done, 1)


def bitlinear_ffn(nc, H, att, args, out):
    F = 1024
    FC = F // P
    with ExitStack() as stack:
        m = Memory(nc, stack, "ff_")
        ident = m.sb("ident", [P, P])
        ident16 = m.sb("ident16", [P, P], BF16)
        ones = m.sb("ones", [P, P])
        mhalf = m.sb("mhalf", [P, 1])
        eps = m.sb("eps", [P, 1])
        wo = m.sb("wo", [P, 2, D])
        wf = m.sb("wf", [P, 2, 2 * F])
        wdf = m.sb("wdf", [P, FC, D])
        wq = m.sb("wq", [P, 2, 2 * F], BF16)
        wdq = m.sb("wdq", [P, FC, D], BF16)
        sums = m.sb("sums", [P, 3])
        wscale = m.sb("wscale", [P, 3])
        winv = m.sb("winv", [P, 3])
        winv2 = m.sb("winv2", [P, 2])
        ao = [m.sb(f"ao{b}", [P, D]) for b in range(2)]
        aoT = m.sb("aoT", [P, 2, P])
        h = [m.sb(f"h{b}", [P, D]) for b in range(2)]
        stats = m.sb("stats", [P, 6])
        mv = m.sb("mv", [P, 2])
        rstd = m.sb("rstd", [P, 1])
        xn = m.sb("xn", [P, D])
        xr = m.sb("xr", [P, D])
        xq = m.sb("xq", [P, D], BF16)
        xqT = m.sb("xqT", [P, 2, P], BF16)
        amax = m.sb("amax", [P, 1])
        ascale = m.sb("ascale", [P, 1])
        ainv = m.sb("ainv", [P, 1])
        half_gate = [m.sb(f"half_gate{b}", [P, 1]) for b in range(2)]
        prod = [m.sb(f"prod{b}", [P, 1]) for b in range(2)]
        th = m.sb("th", [P, F])
        z = m.sb("z", [P, F])
        zr = m.sb("zr", [P, F])
        zq = m.sb("zq", [P, F], BF16)
        zqT = m.sb("zqT", [P, FC, P], BF16)
        zmax = m.sb("zmax", [P, 1])
        zscale = m.sb("zscale", [P, 1])
        zmul = m.sb("zmul", [P, 1])
        down_scale = m.sb("down_scale", [P, 1])
        res = [m.sb(f"res{b}", [P, D]) for b in range(2)]

        ps_gu = m.ps("ps_gu", [P, 2, F])
        ps_tr = m.ps("ps_tr", [P, 4, P])
        ps_aoT = ps_tr[:, 0:2, :]
        ps_xqT = ps_tr[:, 2, :].bitcast(BF16).rearrange("p (c t) -> p c t", c=2)
        ps_h = m.ps("ps_h", [P, D])
        ps_d = m.ps("ps_d", [P, D])
        ps_zqT = m.ps("ps_zqT", [P, FC, P], BF16)

        w_in = m.sem("w_in")
        consts = m.sem("consts")
        ident_done = m.sem("ident_done")
        sums_done = m.sem("sums_done")
        total_done = m.sem("total_done")
        wq_done = m.sem("wq_done")
        ao_copied = m.sem("ao_copied")
        aoT_done = m.sem("aoT_done")
        aoT_copied = m.sem("aoT_copied")
        h_done = m.sem("h_done")
        var_done = m.sem("var_done")
        rstd_done = m.sem("rstd_done")
        xq_done = m.sem("xq_done")
        xqT_done = m.sem("xqT_done")
        xqT_copied = m.sem("xqT_copied")
        gu_done = m.sem("gu_done")
        th_done = m.sem("th_done")
        gu_read = m.sem("gu_read")
        zr_done = m.sem("zr_done")
        zq_done = m.sem("zq_done")
        zqT_done = m.sem("zqT_done")
        zqT_copied = m.sem("zqT_copied")
        down_done = m.sem("down_done")
        res_done = m.sem("res_done")
        stored = [m.sem(f"stored{b}") for b in range(2)]

        block = stack.enter_context(nc.Block())

        @block.sync
        def _(sp):
            sp.dma_start(wf[:, :, :], args["ffn_gu"].rearrange("(c p) n -> p c n", p=P)).then_inc(w_in, 16)
            sp.dma_start(wdf[:, :, :], args["ffn_down"].rearrange("(c p) n -> p c n", p=P)).then_inc(w_in, 16)
            sp.dma_start(wo[:, :, :], args["att_wo"].rearrange("(c p) n -> p c n", p=P)).then_inc(w_in, 16)
            for b in range(2):
                sp.sem_inc(stored[b], 16)
            with sp.Fori(0, NB) as i:
                for b in range(2):
                    sp.wait_ge(res_done, 2 * i + b + 1)
                    sp.dma_start(out[bass.ds(i, 1), 1 + b * P:1 + (b + 1) * P, :].rearrange("o p d -> (o p) d"),
                                 res[b][:, :]).then_inc(stored[b], 16)
            sp.wait_ge(res_done, 2 * NB + 1)
            sp.dma_start(out[:, 0, :], res[0][0:NB, :]).then_inc(stored[0], 16)
            sp.wait_ge(stored[0], 16 * (NB + 2))
            sp.wait_ge(stored[1], 16 * (NB + 1))

        @block.gpsimd
        def _(pool):
            nc.gpsimd.memset(mhalf[:, :], -0.5).then_inc(consts, 1)
            nc.gpsimd.memset(eps[:, :], EPS).then_inc(consts, 1)
            nc.gpsimd.memset(ones[:, :], 1.0).then_inc(consts, 1)
            nc.gpsimd.memset(ident[:, :], 0.0).then_inc(consts, 1)
            pool.wait_ge(consts, 4)
            nc.gpsimd.affine_select(out=ident[:, :], in_=ident[:, :], compare_op=ALU.not_equal, fill=1.0,
                                    base=0, pattern=[[-1, P]], channel_multiplier=1).then_inc(ident_done, 1)
            pool.wait_ge(ident_done, 1)
            nc.gpsimd.tensor_copy(ident16[:, :], ident[:, :]).then_inc(ident_done, 1)
            steps = Steps(pool, m.sem("pool_rstd"), 1)
            with pool.Fori(0, CLS + 1) as t:
                steps.round(t)
                pool.wait_ge(var_done, t + 1)
                steps.then_wait(nc.gpsimd.tensor_tensor(rstd[:, :], mv[:, 1:2], eps[:, :], ALU.add))
                nc.gpsimd.tensor_tensor(rstd[:, :], rstd[:, :], mhalf[:, :], ALU.pow).then_inc(rstd_done, 1)

        @block.tensor
        def _(pe):
            pe.wait_ge(consts, 4)
            pe.wait_ge(sums_done, 1)
            nc.tensor.matmul(ps_aoT[:, 0, 0:3], ones[:, :], sums[:, :], start=True, stop=True).then_inc(total_done, 1)
            pe.wait_ge(wq_done, 1)
            pe.wait_ge(ident_done, 2)
            pe.wait_ge(w_in, 3 * 16)

            def front(t, b):
                pe.wait_ge(ao_copied, t + 1)
                for c in range(2):
                    last = nc.tensor.transpose(ps_aoT[:, c, :], ao[b][:, c * P:(c + 1) * P], ident[:, :])
                last.then_inc(aoT_done, 1)
                pe.wait_ge(aoT_copied, t + 1)
                for c in range(2):
                    last = nc.tensor.matmul(ps_h[:, :], aoT[:, c, :], wo[:, c, :], start=c == 0, stop=c == 1)
                last.then_inc(h_done, 1)
                pe.wait_ge(xq_done, t + 1)
                for c in range(2):
                    last = nc.tensor.transpose(ps_xqT[:, c, :], xq[:, c * P:(c + 1) * P], ident16[:, :])
                last.then_inc(xqT_done, 1)

            def up(t):
                pe.wait_ge(xqT_copied, t + 1)
                pe.wait_ge(gu_read, t + 1)
                for j in range(4):
                    for c in range(2):
                        last = nc.tensor.matmul(ps_gu[:, j // 2, (j % 2) * 512:(j % 2) * 512 + 512], xqT[:, c, :],
                                                wq[:, c, j * 512:(j + 1) * 512], start=c == 0, stop=c == 1)
                last.then_inc(gu_done, 1)

            def down(t):
                pe.wait_ge(zq_done, t + 1)
                for c in range(FC):
                    last = nc.tensor.transpose(ps_zqT[:, c, :], zq[:, c * P:(c + 1) * P], ident16[:, :])
                last.then_inc(zqT_done, 1)
                pe.wait_ge(zqT_copied, t + 1)
                for c in range(FC):
                    last = nc.tensor.matmul(ps_d[:, :], zqT[:, c, :], wdq[:, c, :], start=c == 0, stop=c == FC - 1)
                last.then_inc(down_done, 1)

            front(0, 0)
            with pe.Fori(0, NB) as i:
                for b in range(2):
                    t = 2 * i + b
                    up(t)
                    front(t + 1, 1 - b)
                    down(t)
            up(CLS)
            down(CLS)

        @block.scalar
        def _(act):
            def take(t, b):
                act.wait_ge(aoT_done, t)
                nc.scalar.activation(ao[b][:, :], att[:, bass.ds(t, 1), 0:D], ACT.Copy).then_inc(ao_copied, 1)

            def front(t):
                act.wait_ge(aoT_done, t + 1)
                nc.scalar.activation(aoT[:, :, :], ps_aoT, ACT.Copy).then_inc(aoT_copied, 1)

            def copy_x(t):
                act.wait_ge(xqT_done, t + 1)
                nc.scalar.activation(xqT[:, :, :], ps_xqT, ACT.Copy).then_inc(xqT_copied, 1)

            def squash(t, b):
                act.wait_ge(gu_done, t + 1)
                act.wait_ge(gu_read, t + 1)
                nc.scalar.activation(th[:, :], ps_gu[:, 0, :], ACT.Tanh, scale=half_gate[b][:, :]).then_inc(th_done, 1)

            def down(t):
                act.wait_ge(zr_done, t + 1)
                nc.scalar.activation(zq[:, :], zr[:, :], ACT.Copy, bias=-MAGIC).then_inc(zq_done, 1)

            def copy_z(t):
                act.wait_ge(zqT_done, t + 1)
                nc.scalar.activation(zqT[:, :, :], ps_zqT[:, :, :], ACT.Copy).then_inc(zqT_copied, 1)

            take(0, 0)
            front(0)
            copy_x(0)
            with act.Fori(0, NB) as i:
                for b in range(2):
                    t = 2 * i + b
                    take(t + 1, 1 - b)
                    squash(t, b)
                    front(t + 1)
                    down(t)
                    copy_x(t + 1)
                    copy_z(t)
            squash(CLS, 0)
            down(CLS)
            copy_z(CLS)

        @block.vector
        def _(dve):
            v = nc.vector
            setup = Steps(dve, m.sem("dve_setup"), 100)
            go = setup.then_wait
            dve.wait_ge(w_in, 3 * 16)
            parts = [wf[:, :, 0:F], wf[:, :, F:2 * F], wdf[:, :, :]]
            rounded = [wq[:, :, 0:F], wq[:, :, F:2 * F], wdq[:, :, :]]
            for k, part in enumerate(parts):
                last = v.tensor_reduce(sums[:, k:k + 1], part, axis=AX.XY, op=ALU.add, apply_absolute_value=True)
            last.then_inc(sums_done, 1)
            dve.wait_ge(total_done, 1)
            go(v.tensor_scalar(winv[:, :], ps_aoT[:, 0, 0:3], 1.0 / (F * D), 1e-5, ALU.mult, ALU.max))
            go(v.reciprocal(wscale[:, :], winv[:, :]))
            go(v.reciprocal(winv[:, :], wscale[:, :]))
            v.tensor_scalar(winv2[:, 0:1], winv[:, 0:1], 0.5, None, ALU.mult)
            go(v.tensor_scalar(winv2[:, 1:2], winv[:, 0:1], winv[:, 1:2], 0.5, ALU.mult, ALU.mult))
            for k, part in enumerate(parts):
                last = v.tensor_scalar(part, part, wscale[:, k:k + 1], MAGIC, ALU.mult, ALU.add)
            go(last)
            for k, part in enumerate(parts):
                last = v.tensor_scalar(part, part, MAGIC - 1, MAGIC + 1, ALU.max, ALU.min)
            go(last)
            for k, part in enumerate(parts):
                last = v.tensor_scalar(rounded[k], part, MAGIC, None, ALU.subtract)
            last.then_inc(wq_done, 1)

            front_steps = Steps(dve, m.sem("dve_front"), 9)
            up_steps = Steps(dve, m.sem("dve_up"), 7)
            dve.sem_inc(gu_read, 1)

            def front(t, b):
                front_steps.round(t)
                go = front_steps.then_wait
                dve.wait_ge(h_done, t + 1)
                go(v.tensor_tensor(h[b][:, :], ps_h[:, :], H[:, bass.ds(t, 1), :], ALU.add))
                go(v.bn_stats(stats[:, :], h[b][:, :]), (w_in, 3 * 16))
                v.bn_aggr(mv[:, :], stats[:, :]).then_inc(var_done, 1)
                dve.wait_ge(rstd_done, t + 1)
                go(v.tensor_scalar(xn[:, :], h[b][:, :], mv[:, 0:1], rstd[:, :], ALU.subtract, ALU.mult))
                go(v.tensor_reduce(amax[:, :], xn[:, :], axis=AX.X, op=ALU.max, apply_absolute_value=True))
                go(v.tensor_scalar(amax[:, :], amax[:, :], 1e-5, 1.0 / 127.0, ALU.max, ALU.mult))
                go(v.reciprocal(ascale[:, :], amax[:, :]))
                go(v.tensor_scalar(xr[:, :], xn[:, :], ascale[:, :], MAGIC, ALU.mult, ALU.add))
                go(v.tensor_scalar(xr[:, :], xr[:, :], MAGIC - 128, MAGIC + 127, ALU.max, ALU.min))
                v.tensor_scalar(half_gate[b][:, :], amax[:, :], winv2[:, 0:1], None, ALU.mult)
                v.tensor_scalar(xq[:, :], xr[:, :], MAGIC, None, ALU.subtract).then_inc(xq_done, 1)
                go(v.tensor_scalar(prod[b][:, :], amax[:, :], amax[:, :], winv2[:, 1:2], ALU.mult, ALU.mult))

            def up(t, b):
                up_steps.round(t)
                go = up_steps.then_wait
                dve.wait_ge(th_done, t + 1)
                go(v.scalar_tensor_tensor(z[:, :], th[:, :], 1.0, ps_gu[:, 0, :], ALU.add, ALU.mult))
                v.tensor_tensor(z[:, :], z[:, :], ps_gu[:, 1, :], ALU.mult).then_inc(gu_read, 1)
                dve.wait_ge(gu_read, t + 2)
                go(v.tensor_reduce(zmax[:, :], z[:, :], axis=AX.X, op=ALU.max, apply_absolute_value=True))
                go(v.tensor_scalar(zmax[:, :], zmax[:, :], prod[b][:, :], 1e-5, ALU.mult, ALU.max))
                go(v.tensor_scalar(zmax[:, :], zmax[:, :], 1.0 / 127.0, None, ALU.mult))
                go(v.reciprocal(zscale[:, :], zmax[:, :]))
                v.tensor_scalar(down_scale[:, :], zmax[:, :], winv[:, 2:3], None, ALU.mult)
                go(v.tensor_scalar(zmul[:, :], zscale[:, :], prod[b][:, :], None, ALU.mult))
                go(v.tensor_scalar(zr[:, :], z[:, :], zmul[:, :], MAGIC, ALU.mult, ALU.add))
                v.tensor_scalar(zr[:, :], zr[:, :], MAGIC - 128, MAGIC + 127, ALU.max, ALU.min).then_inc(zr_done, 1)

            def final(i, b):
                t = 2 * i + b
                dve.wait_ge(down_done, t + 1)
                dve.wait_ge(stored[b], 16 * i + 16)
                v.scalar_tensor_tensor(res[b][:, :], ps_d[:, :], down_scale[:, :], h[b][:, :],
                                       ALU.mult, ALU.add).then_inc(res_done, 1)

            front(0, 0)
            with dve.Fori(0, NB) as i:
                for b in range(2):
                    t = 2 * i + b
                    up(t, b)
                    front(t + 1, 1 - b)
                    final(i, b)
            up(CLS, 0)
            final(NB, 0)


def build(nc, args, out):
    with ExitStack() as stack:
        H = stack.enter_context(nc.sbuf_tensor("H", [P, NT, D], F32))
        xs = nc.dram_tensor("xs_dram", (MTILES * MT, D), F32).ap()
        ys = nc.dram_tensor("ys_dram", (MTILES * MT, D), F32).ap()
        vcls = nc.dram_tensor("vcls_dram", (NB, D), F32).ap()
        with nc.cleanup_on_exit():
            tokenizer(nc, H, args)
            recurrence(nc, H, xs, args)
        with nc.cleanup_on_exit(), ExitStack() as moe:
            place = [moe.enter_context(nc.sbuf_tensor(f"place{k}", [P, NT, 1], U32)) for k in range(2)]
            share = [moe.enter_context(nc.sbuf_tensor(f"share{k}", [P, NT], F32)) for k in range(2)]
            whose = moe.enter_context(nc.sbuf_tensor("whose", [1, MTILES], I32))
            route(nc, H, xs, place, share, whose, args)
            experts(nc, xs, ys, whose, args)
            combine(nc, H, ys, place, share)
        with ExitStack() as att:
            qkv = att.enter_context(nc.sbuf_tensor("qkv", [P, NT, 3 * D], F32))
            class_keys = att.enter_context(nc.sbuf_tensor("class_keys", [P, AH // 4, 4, NB], F32))
            queries_keys_values(nc, H, qkv, class_keys, vcls, args)
            attention(nc, qkv, class_keys, vcls, args)
            bitlinear_ffn(nc, H, qkv, args, out)


def expert_rows(np, a):
    def up(w, sw):
        w = np.concatenate([w, sw[None]])
        return w.reshape(E + 1, 2, P, I, 2).transpose(0, 2, 1, 4, 3)

    def bias(b, sb):
        b = np.concatenate([b, sb[None]])
        return b.reshape(E + 1, I // P, P, 2).transpose(0, 2, 1, 3)

    w13 = np.stack([up(a["L0_ffn_w1"], a["L0_ffn_sw1"]), up(a["L0_ffn_w3"], a["L0_ffn_sw3"])], axis=3)
    w2 = np.concatenate([a["L0_ffn_w2"], a["L0_ffn_sw2"][None]]).reshape(E + 1, I // P, P, D).transpose(0, 2, 1, 3)
    b13 = np.stack([bias(a["L0_ffn_b1"], a["L0_ffn_sb1"]), bias(a["L0_ffn_b3"], a["L0_ffn_sb3"])], axis=3)
    return np.concatenate([w13.reshape(E + 1, P, -1), w2.reshape(E + 1, P, -1), b13.reshape(E + 1, P, -1)], axis=2)


def kernel(**inputs):
    import numpy as np
    import concourse.bacc as bacc
    from concourse.bass_utils import run_bass_kernel_spmd

    a = {k: np.asarray(v) for k, v in inputs.items()}
    x = a["x"]
    angle = np.outer(np.arange(1, L + 1, dtype=np.float32),
                     1.0 / 10000.0 ** (np.arange(0, DH, 2, dtype=np.float32) / DH)).astype(np.float32)
    laid = {
        "tok_x": np.concatenate([x.transpose(0, 1, 3, 2).reshape(NB, C, HT * L),
                                 np.ones((NB, 1, HT * L), np.float32)], axis=1),
        "tok_xr": x.transpose(0, 2, 3, 1).reshape(NB, L, D),
        "tok_wqkv": np.concatenate([
            np.concatenate([a[f"L0_tok_W{c}_w"].T for c in "qkv"], axis=1),
            np.concatenate([a[f"L0_tok_W{c}_b"] for c in "qkv"])[None]], axis=0),
        "tok_wbT": a["L0_tok_w_bias"].T,
        "tok_maskT": a["L0_tok_local_mask"].T,
        "L0_tok_out_w": a["L0_tok_out_w"], "L0_tok_out_b": a["L0_tok_out_b"],
        "L0_tok_ln_g": a["L0_tok_ln_g"], "L0_tok_ln_b": a["L0_tok_ln_b"],
        "cls_row": a["cls_tok"].reshape(D),
        "att_w": np.concatenate([a[f"L1_attn_W_{c}"].T for c in "QKV"], axis=1),
        "att_wo": a["L1_attn_W_O"].T,
        "ffn_gu": np.concatenate([a["L1_ffn_w_gate"].T, a["L1_ffn_w_up"].T], axis=1),
        "ffn_down": a["L1_ffn_w_down"].T,
        "rope_cos": np.concatenate([np.cos(angle), np.cos(angle)], axis=1),
        "rope_sin": np.concatenate([-np.sin(angle), np.sin(angle)], axis=1),
        "gate_wT": a["L0_ffn_gate_w"].T, "gate_b": a["L0_ffn_gate_b"],
        "experts": expert_rows(np, a), "experts_b2": np.concatenate([a["L0_ffn_b2"], a["L0_ffn_sb2"][None]]),
        "earlier": np.triu(np.ones((P, P), np.float32), 1),
        "first_wins": np.arange(E, 0, -1, dtype=np.float32),
        "is_token": np.concatenate([np.ones((P, CLS), np.float32), (np.arange(P)[:, None] < NB).astype(np.float32),
                                    np.zeros((P, 1), np.float32)], axis=1),
        "tile_no": np.arange(ROUTED, dtype=np.float32),
        "rec_w": np.concatenate([a[f"L0_attn_W_{c}"].T for c in "kvq"], axis=1),
    }
    nc = bacc.Bacc("TRN2", target_bir_lowering=False, num_devices=1)
    arrays, args = {}, {}
    for name, v in laid.items():
        arrays[name + "_dram"] = np.ascontiguousarray(v)
        args[name] = nc.dram_tensor(name + "_dram", v.shape, mybir.dt.from_np(v.dtype), kind="ExternalInput").ap()
    out = nc.dram_tensor("out_dram", (NB, L + 1, D), F32, kind="ExternalOutput").ap()
    build(nc, args, out)
    r = run_bass_kernel_spmd(nc, [arrays], core_ids=[0])
    return r.results[0]["out_dram"]
```

```python
from contextlib import ExitStack

import concourse.bass as bass
from concourse import mybir

P = 128
D = 256
NB = 16
L = 256
C = 64
HT = 4
NT = 2 * NB + 2
CLS = 2 * NB
EPS = 1e-5
E = 8
I = 512
MT = 256
ROUTED = 2 * NB * (L + 1) // MT + E
EXPERT_COLS = 2 * 2 * 2 * I + I // P * D + I // P * 4
AH = 16
DH = D // AH
MAGIC = 1.5 * 2 ** 23

F32 = mybir.dt.float32
BF16 = mybir.dt.bfloat16
I32 = mybir.dt.int32
U8 = mybir.dt.uint8
U32 = mybir.dt.uint32
ALU = mybir.AluOpType
ACT = mybir.ActivationFunctionType
AX = mybir.AxisListType


class Steps:

    def __init__(self, engine, sem, per):
        self.engine, self.sem, self.per, self.base, self.k = engine, sem, per, 0, 0

    def round(self, n):
        assert self.k in (0, self.per), (self.k, self.per)
        self.base, self.k = n * self.per, 0

    def then_wait(self, instruction, passed=None):
        instruction.then_inc(self.sem, 1)
        self.k += 1
        value = self.base + self.k
        if passed:
            if not isinstance(value, int):
                value = self.engine.to_reg(value)
            self.engine.wait_ge(*passed)
        self.engine.wait_ge(self.sem, value)


class Memory:

    def __init__(self, nc, stack, prefix):
        self.nc, self.stack, self.prefix = nc, stack, prefix

    def sb(self, name, shape, dt=F32):
        return self.stack.enter_context(self.nc.sbuf_tensor(self.prefix + name, shape, dt))

    def ps(self, name, shape, dt=F32):
        return self.stack.enter_context(self.nc.psum_tensor(self.prefix + name, shape, dt))

    def sem(self, name):
        return self.nc.alloc_semaphore(self.prefix + name)


def over(ap, axis, count):
    a = ap.unsqueeze(axis)
    shape = list(a.shape)
    shape[axis] = count
    return a.broadcast_to(shape)


def tokenizer(nc, H, args):
    with ExitStack() as stack:
        m = Memory(nc, stack, "tok_")
        wqkv = m.sb("wqkv", [C + 1, 3 * C])
        ew = m.sb("ew", [P, 2, L])
        mask8 = m.sb("mask8", [P, 2, L], U8)
        maskf = m.sb("maskf", [P, 2, L])
        outw = m.sb("outw", [P, 2, D])
        outb = m.sb("outb", [P, D])
        gain = m.sb("gain", [P, D])
        shift = m.sb("shift", [P, D])
        ident = m.sb("ident", [P, P])
        xa = [m.sb(f"xa{b}", [C + 1, HT, L]) for b in range(2)]
        xr = [m.sb(f"xr{b}", [P, 2, D]) for b in range(2)]
        mix = m.sb("mix", [P, 2, 2, D])
        eq = [m.sb(f"eq{b}", [P, 2, D]) for b in range(2)]
        den = m.sb("den", [P, 2, D])
        rec = m.sb("rec", [P, 2, D])
        y = m.sb("y", [P, 2, D])
        yT = m.sb("yT", [P, 2, L])
        hres = m.sb("hres", [P, 2, D])
        stats = m.sb("stats", [P, 2, 6])
        mv = m.sb("mv", [P, 2, 2])
        rstd = m.sb("rstd", [P, 2])
        mhalf = m.sb("mhalf", [P, 2])
        eps = m.sb("eps", [P, 2])
        hn = [m.sb(f"hn{b}", [P, 2, D]) for b in range(2)]

        ps_qkv = m.ps("ps_qkv", [P, 2, HT, 256])
        ps_nd = m.ps("ps_nd", [P, 2, 2, D])
        ps_yT = m.ps("ps_yT", [P, 2, L])
        ps_h = m.ps("ps_h", [P, 2, D])

        weights_in = m.sem("weights_in")
        class_in = m.sem("class_in")
        zeroed = m.sem("zeroed")
        ident_done = m.sem("ident_done")
        mask_steps = m.sem("mask_steps")
        ew_ready = m.sem("ew_ready")
        xa_in = [m.sem(f"xa_in{b}") for b in range(2)]
        xr_in = [m.sem(f"xr_in{b}") for b in range(2)]
        qkv_done = m.sem("qkv_done")
        exps_done = m.sem("exps_done")
        mix_done = m.sem("mix_done")
        nd_done = m.sem("nd_done")
        y_done = m.sem("y_done")
        yT_done = m.sem("yT_done")
        yT_copied = m.sem("yT_copied")
        hproj_done = m.sem("hproj_done")
        residual_ready = m.sem("residual_ready")
        var_done = m.sem("var_done")
        rstd_done = m.sem("rstd_done")
        normed = m.sem("normed")
        h_written = m.sem("h_written")
        y_steps = m.sem("y_steps")
        norm_steps = m.sem("norm_steps")
        pool_steps = m.sem("pool_steps")

        block = stack.enter_context(nc.Block())

        @block.sync
        def _(sp):
            sp.dma_start(wqkv[:, :], args["tok_wqkv"]).then_inc(weights_in, 16)
            sp.dma_start(ew[:, :, :], args["tok_wbT"].rearrange("(s p) t -> p s t", p=P)).then_inc(weights_in, 16)
            sp.dma_start(mask8[:, :, :], args["tok_maskT"].rearrange("(s p) t -> p s t", p=P)).then_inc(weights_in, 16)
            sp.dma_start(outw[:, :, :], args["L0_tok_out_w"].rearrange("(c p) n -> p c n", p=P)).then_inc(weights_in, 16)
            sp.dma_start(outb[:, :], args["L0_tok_out_b"].partition_broadcast(P)).then_inc(weights_in, 16)
            sp.dma_start(gain[:, :], args["L0_tok_ln_g"].partition_broadcast(P)).then_inc(weights_in, 16)
            sp.dma_start(shift[:, :], args["L0_tok_ln_b"].partition_broadcast(P)).then_inc(weights_in, 16)
            sp.wait_ge(zeroed, 1)
            sp.dma_start(H[0:NB, CLS, :], args["cls_row"].partition_broadcast(NB)).then_inc(class_in, 16)

            def load(i, b, first):
                n = 2 * i + b
                if not first:
                    sp.wait_ge(qkv_done, n - 1)
                    sp.wait_ge(normed, n - 1)
                sp.dma_start(xa[b][:, :, :], args["tok_x"][bass.ds(n, 1)].rearrange(
                    "o c (h l) -> (o c) h l", h=HT)).then_inc(xa_in[b], 16)
                sp.dma_start(xr[b][:, :, :], args["tok_xr"][bass.ds(n, 1)].rearrange(
                    "o (s p) d -> (o p) s d", p=P)).then_inc(xr_in[b], 16)

            load(0, 0, True)
            load(0, 1, True)
            with sp.Fori(1, NB // 2) as i:
                load(i, 0, False)
                load(i, 1, False)
            sp.wait_ge(class_in, 16)

        @block.gpsimd
        def _(pool):
            nc.gpsimd.memset(H[:, CLS:NT, :], 0.0).then_inc(zeroed, 1)
            nc.gpsimd.memset(mhalf[:, :], -0.5).then_inc(pool_steps, 1)
            nc.gpsimd.memset(eps[:, :], EPS).then_inc(pool_steps, 1)
            nc.gpsimd.memset(ident[:, :], 0.0).then_inc(pool_steps, 1)
            pool.wait_ge(pool_steps, 3)
            nc.gpsimd.affine_select(out=ident[:, :], in_=ident[:, :], compare_op=ALU.not_equal, fill=1.0,
                                    base=0, pattern=[[-1, P]], channel_multiplier=1).then_inc(ident_done, 1)
            pool.wait_ge(weights_in, 7 * 16)
            steps = Steps(pool, m.sem("pool_ln"), 2)
            with pool.Fori(0, NB // 2) as i:
                for b in range(2):
                    n = 2 * i + b
                    pool.wait_ge(xr_in[b], 16 * i + 16)
                    nc.gpsimd.tensor_tensor(xr[b][:, :, :], xr[b][:, :, :], over(outb[:, :], 1, 2), ALU.add)\
                        .then_inc(residual_ready, 1)
                    steps.round(n)
                    pool.wait_ge(var_done, n + 1)
                    steps.then_wait(nc.gpsimd.tensor_tensor(rstd[:, :], mv[:, :, 1], eps[:, :], ALU.add))
                    nc.gpsimd.tensor_tensor(rstd[:, :], rstd[:, :], mhalf[:, :], ALU.pow).then_inc(rstd_done, 1)
                    pool.wait_ge(normed, n + 1)
                    steps.then_wait(nc.gpsimd.tensor_tensor(
                        hn[b][:, :, :], hn[b][:, :, :], over(gain[:, :], 1, 2), ALU.mult))
                    nc.gpsimd.tensor_tensor(H[:, bass.ds(2 * n, 2), :], hn[b][:, :, :],
                                            over(shift[:, :], 1, 2), ALU.add).then_inc(h_written, 1)

        @block.tensor
        def _(pe):
            pe.wait_ge(weights_in, 7 * 16)

            def project(i, b, first):
                n = 2 * i + b
                pe.wait_ge(xa_in[b], 16 * i + 16)
                if not first:
                    pe.wait_ge(exps_done, n)
                    pe.wait_ge(mix_done, n)
                for s in range(2):
                    for h in range(HT):
                        last = nc.tensor.matmul(ps_qkv[:, s, h, 0:3 * C], xa[b][:, h, s * P:(s + 1) * P],
                                                wqkv[:, :], start=True, stop=True)
                last.then_inc(qkv_done, 1)

            def mixed(i, b):
                n = 2 * i + b
                pe.wait_ge(mix_done, n + 1)
                pe.wait_ge(exps_done, n + 1)
                for t in range(2):
                    for s in range(2):
                        last = nc.tensor.matmul(ps_nd[:, t, :, :], ew[:, s, t * P:(t + 1) * P],
                                                mix[:, s, :, :], start=s == 0, stop=s == 1)
                last.then_inc(nd_done, 1)

            def out(i, b):
                n = 2 * i + b
                pe.wait_ge(y_done, n + 1)
                for c in range(2):
                    for s in range(2):
                        last = nc.tensor.transpose(ps_yT[:, c, s * P:(s + 1) * P],
                                                   y[:, s, c * P:(c + 1) * P], ident[:, :])
                last.then_inc(yT_done, 1)
                pe.wait_ge(yT_copied, n + 1)
                for s in range(2):
                    for c in range(2):
                        last = nc.tensor.matmul(ps_h[:, s, :], yT[:, c, s * P:(s + 1) * P], outw[:, c, :],
                                                start=c == 0, stop=c == 1)
                last.then_inc(hproj_done, 1)

            project(0, 0, True)
            pe.wait_ge(ew_ready, 1)
            pe.wait_ge(ident_done, 1)
            with pe.Fori(0, NB // 2 - 1) as i:
                for b in range(2):
                    mixed(i, b)
                    project(i + b, 1 - b, False)
                    out(i, b)
            last_i = NB // 2 - 1
            mixed(last_i, 0)
            project(last_i, 1, False)
            out(last_i, 0)
            mixed(last_i, 1)
            out(last_i, 1)

        @block.scalar
        def _(act):
            act.wait_ge(mask_steps, 2)
            nc.scalar.activation(ew[:, :, :], ew[:, :, :], ACT.Exp).then_inc(ew_ready, 1)

            def exps(i, b, first):
                n = 2 * i + b
                act.wait_ge(qkv_done, n + 1)
                if not first:
                    act.wait_ge(nd_done, n)
                for s in range(2):
                    nc.scalar.activation(mix[:, s, 1, :].rearrange("p (h c) -> p h c", h=HT),
                                         ps_qkv[:, s, :, C:2 * C], ACT.Exp)
                    last = nc.scalar.activation(eq[b][:, s, :].rearrange("p (h c) -> p h c", h=HT),
                                                ps_qkv[:, s, :, 0:C], ACT.Exp, scale=-1.0)
                last.then_inc(exps_done, 1)

            def copy(i, b):
                n = 2 * i + b
                act.wait_ge(yT_done, n + 1)
                nc.scalar.activation(yT[:, :, :], ps_yT[:, :, :], ACT.Copy).then_inc(yT_copied, 1)

            exps(0, 0, True)
            with act.Fori(0, NB // 2 - 1) as i:
                for b in range(2):
                    exps(i + b, 1 - b, False)
                    copy(i, b)
            last_i = NB // 2 - 1
            exps(last_i, 1, False)
            copy(last_i, 0)
            copy(last_i, 1)

        @block.vector
        def _(dve):
            dve.wait_ge(weights_in, 7 * 16)
            nc.vector.tensor_copy(maskf[:, :, :], mask8[:, :, :]).then_inc(mask_steps, 1)
            dve.wait_ge(mask_steps, 1)
            nc.vector.tensor_tensor(ew[:, :, :], ew[:, :, :], maskf[:, :, :], ALU.mult).then_inc(mask_steps, 1)
            y_chain = Steps(dve, y_steps, 2)
            norm_chain = Steps(dve, norm_steps, 2)

            def weigh(i, b):
                n = 2 * i + b
                dve.wait_ge(exps_done, n + 1)
                for s in range(2):
                    last = nc.vector.tensor_tensor(
                        mix[:, s, 0, :].rearrange("p (h c) -> p h c", h=HT), ps_qkv[:, s, :, 2 * C:3 * C],
                        mix[:, s, 1, :].rearrange("p (h c) -> p h c", h=HT), ALU.mult)
                last.then_inc(mix_done, 1)

            def gate(i, b):
                n = 2 * i + b
                y_chain.round(n)
                dve.wait_ge(nd_done, n + 1)
                y_chain.then_wait(nc.vector.scalar_tensor_tensor(
                    den[:, :, :], eq[b][:, :, :], 1.0, ps_nd[:, :, 1, :], ALU.add, ALU.mult))
                y_chain.then_wait(nc.vector.reciprocal(rec[:, :, :], den[:, :, :]))
                nc.vector.tensor_tensor(y[:, :, :], ps_nd[:, :, 0, :], rec[:, :, :], ALU.mult).then_inc(y_done, 1)

            def norm(i, b):
                n = 2 * i + b
                norm_chain.round(n)
                dve.wait_ge(hproj_done, n + 1)
                dve.wait_ge(residual_ready, n + 1)
                norm_chain.then_wait(nc.vector.tensor_tensor(hres[:, :, :], ps_h[:, :, :], xr[b][:, :, :], ALU.add))
                for s in range(2):
                    last = nc.vector.bn_stats(stats[:, s, :], hres[:, s, :])
                norm_chain.then_wait(last, (weights_in, 7 * 16))
                for s in range(2):
                    last = nc.vector.bn_aggr(mv[:, s, :], stats[:, s, :])
                last.then_inc(var_done, 1)
                dve.wait_ge(rstd_done, n + 1)
                for s in range(2):
                    last = nc.vector.tensor_scalar(hn[b][:, s, :], hres[:, s, :], mv[:, s, 0:1], rstd[:, s:s + 1],
                                                   ALU.subtract, ALU.mult)
                last.then_inc(normed, 1)

            weigh(0, 0)
            with dve.Fori(0, NB // 2 - 1) as i:
                for b in range(2):
                    gate(i, b)
                    weigh(i + b, 1 - b)
                    norm(i, b)
            last_i = NB // 2 - 1
            gate(last_i, 0)
            weigh(last_i, 1)
            norm(last_i, 0)
            gate(last_i, 1)
            norm(last_i, 1)


def recurrence(nc, H, xs, args):
    NBLK, BW = 32, 8
    U = 2 * NBLK + 1
    GROUPS = [(0, 33), (33, U)]
    HALF_COLS = 512
    with ExitStack() as stack:
        m = Memory(nc, stack, "rec_")
        w = m.sb("w", [P, 2, 3 * D])
        ident = m.sb("ident", [P, P])
        mhalf = m.sb("mhalf", [P, 2])
        eps = m.sb("eps", [P, 2])
        half = m.sb("half", [P, U])
        stats = m.sb("stats", [P, 2, 6])
        mv = m.sb("mv", [P, 2, 2])
        rstd = m.sb("rstd", [P, 2])
        xn = m.sb("xn", [P, 2, D])
        xT = m.sb("xT", [P, 2, 2 * P])
        kvq = [m.sb(f"kvq{b}", [P, 3, U, BW]) for b in range(2)]
        kn = [m.sb(f"kn{b}", [P, U, BW]) for b in range(2)]
        ksq = m.sb("ksq", [P, U, BW])
        ss = m.sb("ss", [P, U])
        nrm = m.sb("nrm", [P, U])
        rn = m.sb("rn", [P, U])
        row = m.sb("row", [1, 3 * D])
        S = m.sb("S", [P, U, BW, BW])
        T = m.sb("T", [P, U, BW, BW])
        Tq = m.sb("Tq", [P, U, BW, BW])
        delta = m.sb("delta", [P, U, BW])
        sq = [m.sb(f"sq{b}", [P, U, BW]) for b in range(2)]
        th = [m.sb(f"th{b}", [P, U, BW]) for b in range(2)]
        sqh = [m.sb(f"sqh{b}", [P, U, BW]) for b in range(2)]
        o = m.sb("o", [P, U, BW])
        ocls = m.sb("ocls", [NBLK, NB, BW])
        ocls_rows = m.sb("ocls_rows", [NB, D])
        zero_rows = m.sb("zero_rows", [P, 8 * D])
        row_dram = nc.dram_tensor("rec_row_dram", (3 * D,), F32).ap()
        ocls_dram = nc.dram_tensor("rec_ocls_dram", (NB, D), F32).ap()

        ps_xT = m.ps("ps_xT", [P, 2, 2 * P])
        ps_kvq = m.ps("ps_kvq", [P, 2, 3, D])
        ps_sk = [m.ps(f"ps_sk{g}", [P, HALF_COLS]) for g in range(2)]
        ps_sq = [m.ps(f"ps_sq{g}", [P, HALF_COLS]) for g in range(2)]

        weights_in = m.sem("weights_in")
        zero_ready = m.sem("zero_ready")
        xs_zeroed = m.sem("xs_zeroed")
        consts = m.sem("consts")
        ident_done = m.sem("ident_done")
        row_copied = m.sem("row_copied")
        row_out = m.sem("row_out")
        row_in = m.sem("row_in")
        state_zero = m.sem("state_zero")
        var_done = m.sem("var_done")
        rstd_done = m.sem("rstd_done")
        xn_done = m.sem("xn_done")
        xT_done = m.sem("xT_done")
        xT_copied = m.sem("xT_copied")
        kvq_done = m.sem("kvq_done")
        kvq_copied = m.sem("kvq_copied")
        ss_done = m.sem("ss_done")
        nrm_done = m.sem("nrm_done")
        pre_done = [m.sem(f"pre_done{g}") for g in range(2)]
        tanh_done = [m.sem(f"tanh_done{g}") for g in range(2)]
        k_product = [m.sem(f"k_product{g}") for g in range(2)]
        q_product = [m.sem(f"q_product{g}") for g in range(2)]
        sk_done = [m.sem(f"sk_done{g}") for g in range(2)]
        sq_done = [m.sem(f"sq_done{g}") for g in range(2)]
        gate_done = [m.sem(f"gate_done{g}") for g in range(2)]
        out_done = m.sem("out_done")
        ocls_out = m.sem("ocls_out")
        ocls_in = m.sem("ocls_in")

        def exists(n, last=NB - 1):
            return not isinstance(n, int) or 0 <= n <= last

        def all_turns(engine, turn):
            turn(0, 0)
            pairs = (NB - 4) // 2
            with engine.Fori(0, pairs) as i:
                turn(2 * i + 1, 1)
                turn(2 * i + 2, 0)
            for n in range(2 * pairs + 1, NB + 1):
                turn(n, n % 2)

        block = stack.enter_context(nc.Block())

        @block.sync
        def _(sp):
            sp.dma_start(w[:, :, :], args["rec_w"].rearrange("(c p) n -> p c n", p=P)).then_inc(weights_in, 16)
            sp.wait_ge(row_copied, 1)
            sp.dma_start(row_dram.unsqueeze(0), row[:, :]).then_inc(row_out, 16)
            sp.wait_ge(row_out, 16)
            sp.wait_ge(consts, 6)
            for b in range(2):
                sp.dma_start(kvq[b][0:NBLK, :, U - 1, :],
                             row_dram.rearrange("(c b j) -> b c j", c=3, j=BW)).then_inc(row_in, 16)
            sp.wait_ge(zero_ready, 1)
            xs_v = xs[0:ROUTED * MT, :].rearrange("(p g r) d -> g p (r d)", p=P, r=8)
            chunks = ROUTED * MT // P // 8
            with sp.Fori(0, chunks) as g:
                sp.dma_start(xs_v[bass.ds(g, 1)].rearrange("o p d -> (o p) d"), zero_rows[:, :])\
                    .then_inc(xs_zeroed, 16)
            sp.wait_ge(out_done, NB + 2)
            sp.dma_start(ocls_dram.rearrange("n (b j) -> b n j", j=BW), ocls[:, :, :]).then_inc(ocls_out, 16)
            sp.wait_ge(ocls_out, 16)
            sp.dma_start(ocls_rows[:, :], ocls_dram).then_inc(ocls_in, 16)
            sp.wait_ge(ocls_in, 16)
            sp.wait_ge(xs_zeroed, 16 * chunks)

        @block.gpsimd
        def _(pool):
            pool.sem_inc(out_done, 2)
            nc.gpsimd.memset(mhalf[:, :], -0.5).then_inc(consts, 1)
            nc.gpsimd.memset(eps[:, :], EPS).then_inc(consts, 1)
            nc.gpsimd.memset(half[:, :], 0.5).then_inc(consts, 1)
            nc.gpsimd.memset(ident[:, :], 0.0).then_inc(consts, 1)
            for b in range(2):
                nc.gpsimd.memset(kvq[b][:, :, U - 1, :], 0.0).then_inc(consts, 1)
            pool.wait_ge(consts, 6)
            nc.gpsimd.affine_select(out=ident[:, :], in_=ident[:, :], compare_op=ALU.not_equal, fill=1.0,
                                    base=0, pattern=[[-1, P]], channel_multiplier=1).then_inc(ident_done, 1)
            nc.gpsimd.memset(zero_rows[:, :], 0.0).then_inc(zero_ready, 1)
            rstd_steps = Steps(pool, m.sem("pool_rstd"), 1)
            out_steps = Steps(pool, m.sem("pool_out"), 4)

            def root(k):
                rstd_steps.round(k)
                pool.wait_ge(var_done, k + 1)
                rstd_steps.then_wait(nc.gpsimd.tensor_tensor(rstd[:, :], mv[:, :, 1], eps[:, :], ALU.add))
                nc.gpsimd.tensor_tensor(rstd[:, :], rstd[:, :], mhalf[:, :], ALU.pow).then_inc(rstd_done, 1)

            def norm(n):
                pool.wait_ge(ss_done, n + 1)
                nc.gpsimd.tensor_tensor(nrm[:, :], ss[:, :], half[:, :], ALU.pow).then_inc(nrm_done, 1)

            def gate(n, b):
                out_steps.round(n)
                for g in range(2):
                    pool.wait_ge(gate_done[g], n + 1)
                out_steps.then_wait(nc.gpsimd.tensor_tensor(o[:, :, :], th[b][:, :, :], sqh[b][:, :, :], ALU.mult))
                out_steps.then_wait(nc.gpsimd.tensor_tensor(o[:, :, :], o[:, :, :], sqh[b][:, :, :], ALU.add))
                out_steps.then_wait(nc.gpsimd.tensor_tensor(o[:, :, :], o[:, :, :], sq[b][:, :, :], ALU.mult))
                tiles = H[:, bass.ds(2 * n, 2), :]
                out_steps.then_wait(nc.gpsimd.tensor_tensor(
                    tiles, tiles, o[:, 0:U - 1, :].rearrange("p (s u) j -> p s (u j)", s=2), ALU.add))
                nc.gpsimd.tensor_copy(ocls[:, bass.ds(n, 1), :], o[0:NBLK, U - 1:U, :]).then_inc(out_done, 1)
                pool.wait_ge(out_done, n + 3)

            def turn(n, b):
                if exists(n + 3, NB):
                    root(n + 3)
                if exists(n + 1):
                    norm(n + 1)
                if exists(n - 1):
                    gate(n - 1, 1 - b)

            root(0)
            root(1)
            root(2)
            norm(0)
            all_turns(pool, turn)
            pool.wait_ge(ocls_in, 16)
            nc.gpsimd.tensor_tensor(H[0:NB, CLS, :], H[0:NB, CLS, :], ocls_rows[:, :], ALU.add)

        @block.tensor
        def _(pe):
            pe.wait_ge(ident_done, 1)
            pe.wait_ge(weights_in, 16)

            def turn_x(k):
                pe.wait_ge(xn_done, k + 1)
                for c in range(2):
                    for t in range(2):
                        last = nc.tensor.transpose(ps_xT[:, c, t * P:(t + 1) * P],
                                                   xn[:, t, c * P:(c + 1) * P], ident[:, :])
                last.then_inc(xT_done, 1)

            def project(k, t):
                if t == 0:
                    pe.wait_ge(xT_copied, k + 1)
                    if exists(k - 1):
                        pe.wait_ge(kvq_copied, k)
                for j in range(3):
                    for c in range(2):
                        last = nc.tensor.matmul(ps_kvq[:, t, j, :], xT[:, c, t * P:(t + 1) * P],
                                                w[:, c, j * D:(j + 1) * D], start=c == 0, stop=c == 1)
                if t == 1:
                    last.then_inc(kvq_done, 1)

            def add_up(out, product, g, done):
                lo, hi = GROUPS[g]
                for j in range(BW):
                    last = nc.tensor.matmul(out[:, 0:(hi - lo) * BW], ident[:, :], product[:, lo:hi, :, j],
                                            start=j == 0, stop=j == BW - 1)
                last.then_inc(done, 1)

            def sum_sq(n, g):
                pe.wait_ge(q_product[g], n + 1)
                if not isinstance(n, int) or n > 0:
                    pe.wait_ge(gate_done[g], n)
                add_up(ps_sq[g], Tq, g, sq_done[g])

            def turn(n, b):
                for g in range(2):
                    if exists(n):
                        pe.wait_ge(k_product[g], n + 1)
                        add_up(ps_sk[g], T, g, sk_done[g])
                if exists(n + 3, NB):
                    turn_x(n + 3)
                if exists(n - 1):
                    sum_sq(n - 1, 0)
                if exists(n + 3, NB):
                    project(n + 3, 0)
                if exists(n - 1):
                    sum_sq(n - 1, 1)
                if exists(n + 3, NB):
                    project(n + 3, 1)

            for k in range(3):
                turn_x(k)
                project(k, 0)
                project(k, 1)
            all_turns(pe, turn)

        @block.scalar
        def _(act):
            def copy_xT(k):
                act.wait_ge(xT_done, k + 1)
                nc.scalar.activation(xT[:, :, :], ps_xT[:, :, :], ACT.Copy).then_inc(xT_copied, 1)

            def copy_kvq(k, b):
                act.wait_ge(kvq_done, k + 1)
                for s in range(2):
                    nc.scalar.activation(
                        ksq[:, s * NBLK:(s + 1) * NBLK, :].rearrange("p u j -> p (u j)"), ps_kvq[:, s, 0, :],
                        ACT.Square)
                for s in range(2):
                    last = nc.scalar.activation(
                        kvq[b][:, :, s * NBLK:(s + 1) * NBLK, :].rearrange("p c u j -> p c (u j)"),
                        ps_kvq[:, s, :, :], ACT.Copy)
                last.then_inc(kvq_copied, 1)

            def squash(n, g):
                lo, hi = GROUPS[g]
                act.wait_ge(pre_done[g], n + 1)
                nc.scalar.activation(S[:, lo:hi], S[:, lo:hi], ACT.Tanh).then_inc(tanh_done[g], 1)

            def read_out(n, b, g):
                lo, hi = GROUPS[g]
                sums = ps_sq[g][:, 0:(hi - lo) * BW].rearrange("p (u j) -> p u j", j=BW)
                act.wait_ge(sq_done[g], n + 1)
                act.wait_ge(out_done, n + 1)
                nc.scalar.activation(th[b][:, lo:hi], sums, ACT.Tanh, scale=0.5)
                nc.scalar.activation(sqh[b][:, lo:hi], sums, ACT.Copy, scale=0.5)
                nc.scalar.activation(sq[b][:, lo:hi], sums, ACT.Copy).then_inc(gate_done[g], 1)

            def turn(n, b):
                if exists(n + 1):
                    if not isinstance(n, int) or n > 0:
                        act.wait_ge(q_product[1], n)
                    else:
                        act.wait_ge(ss_done, 1)
                    copy_kvq(n + 2, 1 - b)
                if exists(n + 3, NB):
                    copy_xT(n + 3)
                for g in range(2):
                    if exists(n):
                        squash(n, g)
                for g in range(2):
                    if exists(n - 1):
                        read_out(n - 1, 1 - b, g)

            copy_xT(0)
            act.wait_ge(kvq_done, 1)
            nc.scalar.activation(row[:, :].rearrange("p (c d) -> p c d", c=3), ps_kvq[0:1, 0, :, :],
                                 ACT.Copy).then_inc(row_copied, 1)
            act.wait_ge(row_copied, 1)
            act.sem_inc(kvq_copied, 1)
            copy_xT(1)
            copy_kvq(1, 0)
            copy_xT(2)
            all_turns(act, turn)

        @block.vector
        def _(dve):
            stat_steps = Steps(dve, m.sem("dve_stat"), 1)
            cls_squared = m.sem("dve_cls_squared")
            kn_steps = Steps(dve, m.sem("dve_kn"), 3)
            change_steps = [Steps(dve, m.sem(f"dve_change{g}"), 2) for g in range(2)]

            def moments(k, tiles):
                stat_steps.round(k)
                for s in range(2):
                    last = nc.vector.bn_stats(stats[:, s, :], tiles(s))
                stat_steps.then_wait(last, (state_zero, 1))
                for s in range(2):
                    last = nc.vector.bn_aggr(mv[:, s, :], stats[:, s, :])
                last.then_inc(var_done, 1)

            def normalise(k, tiles):
                if not isinstance(k, int) or k > 0:
                    dve.wait_ge(xT_done, k)
                dve.wait_ge(rstd_done, k + 1)
                for s in range(2):
                    last = nc.vector.tensor_scalar(xn[:, s, :], tiles(s), mv[:, s, 0:1], rstd[:, s:s + 1],
                                                   ALU.subtract, ALU.mult)
                last.then_inc(xn_done, 1)

            def sums(n, b):
                dve.wait_ge(kvq_copied, n + 2)
                nc.vector.tensor_reduce(ss[:, :], ksq[:, :, :], axis=AX.X, op=ALU.add).then_inc(ss_done, 1)

            def unit(n, b):
                kn_steps.round(n)
                dve.wait_ge(nrm_done, n + 1)
                kn_steps.then_wait(nc.vector.tensor_scalar(nrm[:, :], nrm[:, :], 1e-6, None, ALU.add))
                kn_steps.then_wait(nc.vector.reciprocal(rn[:, :], nrm[:, :]))
                kn_steps.then_wait(nc.vector.tensor_tensor(kn[b][:, :, :], kvq[b][:, 0], over(rn[:, :], 2, BW),
                                                           ALU.mult))

            def multiply_k(n, b, g):
                lo, hi = GROUPS[g]
                nc.vector.tensor_tensor(T[:, lo:hi], S[:, lo:hi], over(kn[b][:, lo:hi], 2, BW), ALU.mult)\
                    .then_inc(k_product[g], 1)

            def change(n, b, g):
                lo, hi = GROUPS[g]
                steps = change_steps[g]
                steps.round(n)
                s, t = S[:, lo:hi], T[:, lo:hi]
                dve.wait_ge(sk_done[g], n + 1)
                sk = ps_sk[g][:, 0:(hi - lo) * BW].rearrange("p (u j) -> p u j", j=BW)
                steps.then_wait(nc.vector.tensor_tensor(delta[:, lo:hi], kvq[b][:, 1, lo:hi], sk, ALU.subtract))
                steps.then_wait(nc.vector.tensor_tensor(t, over(delta[:, lo:hi], 3, BW), over(kn[b][:, lo:hi], 2, BW),
                                                        ALU.mult))
                nc.vector.tensor_tensor(s, s, t, ALU.add).then_inc(pre_done[g], 1)

            def multiply_q(n, b, g):
                lo, hi = GROUPS[g]
                dve.wait_ge(tanh_done[g], n + 1)
                if not isinstance(n, int) or n > 0:
                    dve.wait_ge(sq_done[g], n)
                nc.vector.tensor_tensor(Tq[:, lo:hi], S[:, lo:hi], over(kvq[b][:, 2, lo:hi], 2, BW), ALU.mult)\
                    .then_inc(q_product[g], 1)

            def tiles_of(k):
                if isinstance(k, int) and k == 0:
                    return lambda s: H[:, CLS + s, :]
                return lambda s: H[:, bass.ds(2 * k - 2 + s, 1), :]

            def turn(n, b):
                if exists(n):
                    multiply_k(n, b, 0)
                if exists(n + 3, NB):
                    moments(n + 3, tiles_of(n + 3))
                if exists(n - 1):
                    multiply_q(n - 1, 1 - b, 1)
                if exists(n):
                    multiply_k(n, b, 1)
                if exists(n + 1):
                    sums(n + 1, 1 - b)
                if exists(n + 3, NB):
                    normalise(n + 3, tiles_of(n + 3))
                if exists(n):
                    change(n, b, 0)
                    change(n, b, 1)
                    multiply_q(n, b, 0)
                if exists(n + 1):
                    unit(n + 1, 1 - b)

            nc.vector.memset(S[:, :, :, :], 0.0).then_inc(state_zero, 1)
            dve.wait_ge(consts, 3)
            for k in range(3):
                moments(k, tiles_of(k))
                normalise(k, tiles_of(k))
            dve.wait_ge(row_in, 32)
            k = kvq[0][:, 0, U - 1]
            nc.vector.tensor_tensor(ksq[:, U - 1], k, k, ALU.mult).then_inc(cls_squared, 1)
            dve.wait_ge(cls_squared, 1)
            sums(0, 0)
            unit(0, 0)
            all_turns(dve, turn)


def route(nc, H, xn, place, share, whose, shared_w, args):
    with ExitStack() as stack:
        m = Memory(nc, stack, "rt_")
        ident = m.sb("ident", [P, P])
        mhalf = m.sb("mhalf", [P, 2])
        eps = m.sb("eps", [P, 2])
        ones = m.sb("ones", [P, P])
        earlier = m.sb("earlier", [P, P])
        gw = m.sb("gw", [P, 2, E])
        gb = m.sb("gb", [P, E])
        first_wins = m.sb("first_wins", [P, E])
        is_token = m.sb("is_token", [P, NT])
        tile_no = m.sb("tile_no", [P, ROUTED])
        xp = m.sb("xp", [P, 2, D])
        xT = m.sb("xT", [P, 2, 2 * P])
        stats = m.sb("stats", [P, 2, 6])
        mv = m.sb("mv", [P, 2, 2])
        rstd = m.sb("rstd", [P, 2])
        logits = m.sb("logits", [P, NT, E])
        top = m.sb("top", [P, NT])
        scores = m.sb("scores", [P, NT, E])
        biased = m.sb("biased", [P, NT, E])
        tied = m.sb("tied", [P, NT, E])
        chosen = [m.sb(f"chosen{k}", [P, NT, E]) for k in range(2)]
        taken = m.sb("taken", [P, NT, E])
        upto = m.sb("upto", [P, E, NT])
        one_row = m.sb("one_row", [P, NT])
        tiles_of = m.sb("tiles_of", [P, E])
        ends = m.sb("ends", [P, E])
        start = m.sb("start", [P, E])
        row = m.sb("row", [P, NT, E])
        tmp = m.sb("tmp", [P, NT, E])
        ended = m.sb("ended", [P, ROUTED, E])
        owner = m.sb("owner", [P, ROUTED])
        placef = m.sb("placef", [P, NT])

        ps_xT = m.ps("ps_xT", [P, 2, 2 * P])
        ps_lg = m.ps("ps_lg", [P, 2, E])
        ps_rank = m.ps("ps_rank", [P, NT, E])
        ps_total = m.ps("ps_total", [P, NT, E])

        consts_in = m.sem("consts_in")
        consts = m.sem("consts")
        ident_done = m.sem("ident_done")
        var_done = m.sem("var_done")
        rstd_done = m.sem("rstd_done")
        xn_done = m.sem("xn_done")
        xT_done = m.sem("xT_done")
        xT_copied = m.sem("xT_copied")
        lg_done = m.sem("lg_done")
        lg_copied = m.sem("lg_copied")
        less_max = m.sem("less_max")
        exp_done = m.sem("exp_done")
        taken_done = m.sem("taken_done")
        ranks_done = m.sem("ranks_done")
        shared_w_in = m.sem("shared_w_in")
        PAIRS = NT // 2

        block = stack.enter_context(nc.Block())

        @block.sync
        def _(sp):
            sp.dma_start(gw[:, :, :], args["gate_wT"].rearrange("(c p) e -> p c e", p=P)).then_inc(consts_in, 16)
            sp.dma_start(gb[:, :], args["gate_b"].partition_broadcast(P)).then_inc(consts_in, 16)
            sp.dma_start(earlier[:, :], args["earlier"]).then_inc(consts_in, 16)
            sp.dma_start(first_wins[:, :], args["first_wins"].partition_broadcast(P)).then_inc(consts_in, 16)
            sp.dma_start(is_token[:, :], args["is_token"]).then_inc(consts_in, 16)
            sp.dma_start(tile_no[:, :], args["tile_no"].partition_broadcast(P)).then_inc(consts_in, 16)
            sp.dma_start(shared_w[:, :], args["experts"][E]).then_inc(shared_w_in, 16)
            sp.wait_ge(shared_w_in, 16)

        @block.gpsimd
        def _(pool):
            nc.gpsimd.memset(mhalf[:, :], -0.5).then_inc(consts, 1)
            nc.gpsimd.memset(eps[:, :], EPS).then_inc(consts, 1)
            nc.gpsimd.memset(ones[:, :], 1.0).then_inc(consts, 1)
            nc.gpsimd.memset(one_row[:, :], 1.0).then_inc(consts, 1)
            nc.gpsimd.memset(ident[:, :], 0.0).then_inc(consts, 1)
            pool.wait_ge(consts, 5)
            nc.gpsimd.affine_select(out=ident[:, :], in_=ident[:, :], compare_op=ALU.not_equal, fill=1.0,
                                    base=0, pattern=[[-1, P]], channel_multiplier=1).then_inc(ident_done, 1)
            steps = Steps(pool, m.sem("pool_rstd"), 1)
            with pool.Fori(0, PAIRS) as k:
                steps.round(k)
                pool.wait_ge(var_done, k + 1)
                steps.then_wait(nc.gpsimd.tensor_tensor(rstd[:, :], mv[:, :, 1], eps[:, :], ALU.add))
                nc.gpsimd.tensor_tensor(rstd[:, :], rstd[:, :], mhalf[:, :], ALU.pow).then_inc(rstd_done, 1)

        @block.tensor
        def _(pe):
            pe.wait_ge(ident_done, 1)
            pe.wait_ge(consts_in, 6 * 16)
            with pe.Fori(0, PAIRS) as k:
                pe.wait_ge(xn_done, k + 1)
                for c in range(2):
                    for s in range(2):
                        last = nc.tensor.transpose(ps_xT[:, c, s * P:(s + 1) * P],
                                                   xp[:, s, c * P:(c + 1) * P], ident[:, :])
                last.then_inc(xT_done, 1)
                pe.wait_ge(xT_copied, k + 1)
                pe.wait_ge(lg_copied, k + 1)
                for s in range(2):
                    for c in range(2):
                        last = nc.tensor.matmul(ps_lg[:, s, :], xT[:, c, s * P:(s + 1) * P], gw[:, c, :],
                                                start=c == 0, stop=c == 1)
                last.then_inc(lg_done, 1)
            pe.wait_ge(taken_done, 1)
            nc.tensor.matmul(ps_rank[:, :, :], earlier[:, :], taken[:, :, :], start=True, stop=True)
            nc.tensor.matmul(ps_total[:, :, :], ones[:, :], taken[:, :, :], start=True, stop=True)\
                .then_inc(ranks_done, 1)

        @block.scalar
        def _(act):
            with act.Fori(0, PAIRS) as k:
                act.wait_ge(xn_done, k + 1)
                nc.scalar.activation(xn[:, bass.ds(2 * k, 2), :], xp[:, :, :], ACT.Copy)
                act.wait_ge(xT_done, k + 1)
                nc.scalar.activation(xT[:, :, :], ps_xT[:, :, :], ACT.Copy).then_inc(xT_copied, 1)
            act.wait_ge(less_max, 1)
            nc.scalar.activation(scores[:, :, :], scores[:, :, :], ACT.Exp).then_inc(exp_done, 1)

        @block.vector
        def _(dve):
            stat_steps = Steps(dve, m.sem("dve_stat"), 1)
            dve.sem_inc(lg_copied, 1)
            dve.wait_ge(consts_in, 6 * 16)
            with dve.Fori(0, PAIRS) as k:
                stat_steps.round(k)
                for s in range(2):
                    last = nc.vector.bn_stats(stats[:, s, :], H[:, bass.ds(2 * k + s, 1), :])
                stat_steps.then_wait(last, (consts_in, 6 * 16))
                for s in range(2):
                    last = nc.vector.bn_aggr(mv[:, s, :], stats[:, s, :])
                last.then_inc(var_done, 1)
                dve.wait_ge(rstd_done, k + 1)
                for s in range(2):
                    last = nc.vector.tensor_scalar(xp[:, s, :], H[:, bass.ds(2 * k + s, 1), :],
                                                   mv[:, s, 0:1], rstd[:, s:s + 1], ALU.subtract, ALU.mult)
                last.then_inc(xn_done, 1)
                dve.wait_ge(lg_done, k + 1)
                nc.vector.tensor_copy(logits[:, bass.ds(2 * k, 2), :], ps_lg[:, :, :]).then_inc(lg_copied, 1)

            one = Steps(dve, m.sem("dve_route"), 100)
            dve.wait_ge(lg_copied, PAIRS + 1)
            go = one.then_wait
            v = nc.vector
            go(v.tensor_reduce(top[:, :], logits[:, :, :], axis=AX.X, op=ALU.max))
            v.tensor_tensor(scores[:, :, :], logits[:, :, :], over(top[:, :], 2, E), ALU.subtract)\
                .then_inc(less_max, 1)
            dve.wait_ge(exp_done, 1)
            go(v.tensor_reduce(top[:, :], scores[:, :, :], axis=AX.X, op=ALU.add))
            go(v.reciprocal(top[:, :], top[:, :]))
            go(v.tensor_tensor(scores[:, :, :], scores[:, :, :], over(top[:, :], 2, E), ALU.mult))
            go(v.tensor_tensor(biased[:, :, :], scores[:, :, :], over(gb[:, :], 1, NT), ALU.add))
            for k in range(2):
                go(v.tensor_reduce(top[:, :], biased[:, :, :], axis=AX.X, op=ALU.max))
                go(v.tensor_tensor(tied[:, :, :], biased[:, :, :], over(top[:, :], 2, E), ALU.is_equal))
                go(v.tensor_tensor(tied[:, :, :], tied[:, :, :], over(first_wins[:, :], 1, NT), ALU.mult))
                go(v.tensor_reduce(top[:, :], tied[:, :, :], axis=AX.X, op=ALU.max))
                go(v.tensor_tensor(chosen[k][:, :, :], tied[:, :, :], over(top[:, :], 2, E), ALU.is_equal))
                go(v.tensor_tensor(tmp[:, :, :], chosen[k][:, :, :], scores[:, :, :], ALU.mult))
                go(v.tensor_reduce(share[k][:, :], tmp[:, :, :], axis=AX.X, op=ALU.add))
                if k == 0:
                    go(v.tensor_scalar(tmp[:, :, :], chosen[k][:, :, :], -1e30, None, ALU.mult))
                    go(v.tensor_tensor(biased[:, :, :], biased[:, :, :], tmp[:, :, :], ALU.add))
            go(v.tensor_tensor(taken[:, :, :], chosen[0][:, :, :], chosen[1][:, :, :], ALU.add))
            v.tensor_tensor(taken[:, :, :], taken[:, :, :], over(is_token[:, :], 2, E), ALU.mult)\
                .then_inc(taken_done, 1)
            dve.wait_ge(ranks_done, 1)
            for e in range(E):
                last = v.tensor_tensor_scan(upto[:, e, :], one_row[:, :], ps_total[:, :, e], 0.0, ALU.mult, ALU.add)
            go(last)
            go(v.tensor_scalar(tiles_of[:, :], upto[:, :, NT - 1], 1.0 / MT, (MT - 1) / MT - 0.5 + 0.25 / MT,
                               ALU.mult, ALU.add))
            go(v.tensor_scalar(tiles_of[:, :], tiles_of[:, :], MAGIC, None, ALU.add))
            go(v.tensor_scalar(tiles_of[:, :], tiles_of[:, :], MAGIC, None, ALU.subtract))
            go(v.tensor_tensor_scan(ends[:, :], one_row[:, 0:E], tiles_of[:, :], 0.0, ALU.mult, ALU.add))
            go(v.tensor_tensor(start[:, :], ends[:, :], tiles_of[:, :], ALU.subtract))
            go(v.tensor_scalar(start[:, :], start[:, :], float(MT), None, ALU.mult))
            go(v.tensor_tensor(row[:, :, :], upto[:, :, :].rearrange("p e t -> p t e"), ps_total[:, :, :],
                               ALU.subtract))
            go(v.tensor_tensor(row[:, :, :], row[:, :, :], ps_rank[:, :, :], ALU.add))
            go(v.tensor_tensor(row[:, :, :], row[:, :, :], over(start[:, :], 1, NT), ALU.add))
            for k in range(2):
                go(v.tensor_tensor(tmp[:, :, :], row[:, :, :], chosen[k][:, :, :], ALU.mult))
                go(v.tensor_reduce(placef[:, :], tmp[:, :, :], axis=AX.X, op=ALU.add))
                go(v.tensor_copy(place[k][:, :, 0], placef[:, :]))
            go(v.tensor_tensor(ended[:, :, :], over(tile_no[:, :], 2, E), over(ends[:, :], 1, ROUTED), ALU.is_ge))
            go(v.tensor_reduce(owner[:, :], ended[:, :, :], axis=AX.X, op=ALU.add))
            go(v.tensor_scalar(owner[:, :], owner[:, :], float(E - 1), None, ALU.min))
            v.tensor_copy(whose[:, :], owner[0:1, :])


class Tile:

    def __init__(self, n, b, g=None, u=None, i=None, gap=None):
        self.n, self.b, self.g, self.i, self.gap = n, b, g, i, gap
        self.shared = i is not None
        self.w = 2 if self.shared else u
        self.row = None if self.shared else 2 * g + u


def experts(nc, H, xn, xs, ys, place, share, whose, shared_w, args):
    SHARED = NT // 2
    MIXED = 8
    GROUPS = ROUTED // 2
    LEAD = 4
    TRAIL = SHARED - LEAD - MIXED
    assert ROUTED % 2 == 0 and MIXED % 2 == 0 and LEAD % 2 == 0 and TRAIL > 1
    TOKEN_TILES = CLS + 1
    RING = 8

    def lead(i):
        return Tile(i, i % 2, i=i)

    def mixed(q):
        tiles = []
        for half in range(2):
            n, g = LEAD + 6 * q + 3 * half, 2 * q + half
            tiles += [Tile(n, half, g=g, u=0, gap=3), Tile(n + 1, 1 - half, g=g, u=1, gap=3),
                      Tile(n + 2, half, i=LEAD + g)]
        return tiles

    def plain(g, gap=2):
        n = LEAD + MIXED + 2 * g
        return [Tile(n, 0, g=g, u=0, gap=gap), Tile(n + 1, 1, g=g, u=1, gap=gap)]

    def trail(k):
        n = LEAD + MIXED + 2 * GROUPS + k
        return Tile(n, k % 2, i=LEAD + MIXED + k)

    def all_tiles(engine, tile):
        def run(tiles, before, after):
            tiles = [before] + tiles + [after]
            for k in range(1, len(tiles) - 1):
                tile(tiles[k - 1], tiles[k], tiles[k + 1])

        run([lead(i) for i in range(LEAD)], None, mixed(0)[0])
        run(mixed(0), lead(LEAD - 1), mixed(1)[0])
        with engine.Fori(1, MIXED // 2) as q:
            run(mixed(q), mixed(q - 1)[-1], mixed(q + 1)[0])
        run(plain(MIXED, 3), mixed(MIXED // 2 - 1)[-1], plain(MIXED + 1)[0])
        with engine.Fori(MIXED + 1, GROUPS - 1) as g:
            run(plain(g), plain(g - 1)[-1], plain(g + 1)[0])
        run(plain(GROUPS - 1), plain(GROUPS - 2)[-1], trail(0))
        run([trail(k) for k in range(TRAIL)], plain(GROUPS - 1)[-1], None)

    CH = I // P
    W13 = 2 * 2 * 2 * I
    with ExitStack() as stack:
        m = Memory(nc, stack, "ex_")
        ident = m.sb("ident", [P, P])
        wt = [m.sb(f"wt{u}", [P, EXPERT_COLS]) for u in range(2)] + [shared_w]
        w13 = [w[:, 0:W13].rearrange("p (c w g i) -> p c w g i", c=2, w=2, g=2) for w in wt]
        w2 = [w[:, W13:W13 + CH * D].rearrange("p (h d) -> p h d", h=CH) for w in wt]
        b13 = [w[:, W13 + CH * D:EXPERT_COLS].rearrange("p (h w g) -> p h w g", h=CH, w=2) for w in wt]
        b2 = [m.sb(f"b2{u}", [P, D]) for u in range(3)]
        xrow = [m.sb(f"xrow{b}", [P, 2, D]) for b in range(2)]
        xT = [m.sb(f"xT{b}", [P, 2, MT]) for b in range(2)]
        x3 = m.sb("x3", [P, 2, MT])
        gl = m.sb("gl", [P, 2, MT])
        glc = m.sb("glc", [P, 2, MT])
        th = m.sb("th", [P, MT])
        gate = m.sb("gate", [P, MT])
        hT = [m.sb(f"hT{b}", [P, CH, MT]) for b in range(2)]
        yrow = [m.sb(f"yrow{b}", [P, 2, D]) for b in range(2)]
        routed = m.sb("routed", [P, RING, 2, D])

        ps_xT = m.ps("ps_xT", [P, 2, MT])
        ps_up = [m.ps(f"ps_up{b}", [P, 2, 2, MT]) for b in range(2)]
        ps_y = m.ps("ps_y", [P, 2, D])

        ident_done = m.sem("ident_done")
        rows_out = m.sem("rows_out")
        shared_b2_in = m.sem("shared_b2_in")
        w_in = [m.sem(f"w_in{u}") for u in range(2)]
        x_in = [m.sem(f"x_in{b}") for b in range(2)]
        x_taken = m.sem("x_taken")
        xT_done = m.sem("xT_done")
        xT_copied = m.sem("xT_copied")
        up_done = m.sem("up_done")
        x3_done = m.sem("x3_done")
        half_gate = m.sem("half_gate")
        th_done = m.sem("th_done")
        h_done = m.sem("h_done")
        down_done = m.sem("down_done")
        y_copied = m.sem("y_copied")
        y_out = [m.sem(f"y_out{b}") for b in range(2)]
        gathered = [m.sem(f"gathered{s}") for s in range(RING)]
        added = m.sem("added")

        xs_v = xs.rearrange("(j s p) d -> j p s d", s=2, p=P)
        ys_v = ys.rearrange("(j s p) d -> j p s d", s=2, p=P)

        block = stack.enter_context(nc.Block())

        @block.sync
        def _(sp):
            sp.dma_start(b2[2][:, :], args["experts_b2"][E:E + 1, :].broadcast_to([P, D])).then_inc(shared_b2_in, 16)

            def load(before, t, after):
                if t.shared:
                    return
                first = isinstance(t.g, int) and t.g == 0
                e = sp.value_load(whose[0:1, bass.ds(t.row, 1)], min_val=0, max_val=E - 1)
                sp.wait_ge(xT_done, t.n - 1)
                sp.dma_start(xrow[t.b][:, :, :], xs_v[bass.ds(t.row, 1)].rearrange("o p s d -> (o p) s d"))\
                    .then_inc(x_in[t.b], 16)
                if not first:
                    sp.wait_ge(down_done, t.n - t.gap + 1)
                sp.dma_start(wt[t.w][:, :], args["experts"][bass.ds(e, 1)].rearrange("o p n -> (o p) n"))\
                    .then_inc(w_in[t.w], 16)
                if not first:
                    sp.wait_ge(y_copied, t.n - t.gap + 2)
                sp.dma_start(b2[t.w][:, :], args["experts_b2"][bass.ds(e, 1), :].broadcast_to([P, D]))\
                    .then_inc(w_in[t.w], 16)

            sp.wait_ge(rows_out, 16 * 2 * TOKEN_TILES)
            all_tiles(sp, load)

        @block.gpsimd
        def _(pool):
            zeroed = m.sem("zeroed")
            nc.gpsimd.memset(ident[:, :], 0.0).then_inc(zeroed, 1)
            pool.wait_ge(zeroed, 1)
            nc.gpsimd.affine_select(out=ident[:, :], in_=ident[:, :], compare_op=ALU.not_equal, fill=1.0,
                                    base=0, pattern=[[-1, P]], channel_multiplier=1).then_inc(ident_done, 1)
            for t in range(TOKEN_TILES):
                n = P if t < CLS else NB
                for k in range(2):
                    pool.indirect_dma_start(
                        out=xs, out_offset=bass.IndirectOffsetOnAxis(ap=place[k][0:n, t, :], axis=0),
                        in_=xn[0:n, t, :], in_offset=None).then_inc(rows_out, 16)
            for b in range(2):
                pool.wait_ge(y_out[b], 16 * (GROUPS + 1))
            for t in range(TOKEN_TILES):
                n = P if t < CLS else NB
                if t >= RING:
                    pool.wait_ge(added, t - RING + 1)
                for k in range(2):
                    pool.indirect_dma_start(
                        out=routed[0:n, t % RING, k, :], out_offset=None, in_=ys,
                        in_offset=bass.IndirectOffsetOnAxis(ap=place[k][0:n, t, :], axis=0))\
                        .then_inc(gathered[t % RING], 16)

        @block.tensor
        def _(pe):
            def turn(t):
                if t.shared:
                    pe.wait_ge(x_taken, t.i + 1)
                else:
                    pe.wait_ge(x_in[t.b], 16 * t.g + 16)
                for c in range(2):
                    for s in range(2):
                        last = nc.tensor.transpose(ps_xT[:, c, s * P:(s + 1) * P],
                                                   xrow[t.b][:, s, c * P:(c + 1) * P], ident[:, :])
                last.then_inc(xT_done, 1)

            def up(t, h, first):
                if h == 0:
                    if not t.shared:
                        pe.wait_ge(w_in[t.w], 32 * t.g + 32)
                    pe.wait_ge(xT_copied, t.n + 1)
                if not first:
                    pe.wait_ge(half_gate, 4 * t.n + h - 1)
                for w in range(2):
                    for k in range(2):
                        for c in range(2):
                            last = nc.tensor.matmul(ps_up[h % 2][:, w, k, :],
                                                    w13[t.w][:, c, w, k, h * P:(h + 1) * P], xT[t.b][:, c, :],
                                                    start=c == 0, stop=c == 1)
                last.then_inc(up_done, 1)

            def down(t):
                pe.wait_ge(h_done, 4 * t.n + 4)
                pe.wait_ge(y_copied, t.n + 1)
                for s in range(2):
                    for h in range(CH):
                        last = nc.tensor.matmul(ps_y[:, s, :], hT[t.b][:, h, s * P:(s + 1) * P], w2[t.w][:, h, :],
                                                start=h == 0, stop=h == CH - 1)
                last.then_inc(down_done, 1)

            def tile(before, t, after):
                up(t, 0, before is None)
                if before:
                    down(before)
                up(t, 1, before is None)
                if after:
                    turn(after)
                up(t, 2, False)
                up(t, 3, False)

            pe.wait_ge(ident_done, 1)
            turn(lead(0))
            all_tiles(pe, tile)
            down(trail(TRAIL - 1))

        @block.scalar
        def _(act):
            def copy(t):
                act.wait_ge(xT_done, t.n + 1)
                nc.scalar.activation(xT[t.b][:, :, :], ps_xT[:, :, :], ACT.Copy).then_inc(xT_copied, 1)

            def chunk(t, h, first):
                q = 4 * t.n + h
                act.wait_ge(up_done, q + 1)
                if not first:
                    act.wait_ge(half_gate, q)
                for k in range(2):
                    last = nc.scalar.activation(x3[:, k, :], ps_up[h % 2][:, 1, k, :], ACT.Identity,
                                                bias=b13[t.w][:, h, 1, k:k + 1])
                last.then_inc(x3_done, 1)
                act.wait_ge(half_gate, q + 1)
                nc.scalar.activation(th[:, :], glc[:, 0, :], ACT.Tanh, scale=1.702).then_inc(th_done, 1)

            def store(t):
                act.wait_ge(y_copied, t.n + 2)
                act.dma_start(ys_v[bass.ds(t.row, 1)].rearrange("o p s d -> (o p) s d"), yrow[t.b][:, :, :])\
                    .then_inc(y_out[t.b], 16)

            def take(t):
                nc.scalar.activation(xrow[t.b][:, :, :], xn[:, bass.ds(2 * t.i, 2), :], ACT.Copy).then_inc(x_taken, 1)

            def tile(before, t, after):
                for h in range(CH):
                    chunk(t, h, before is None and h == 0)
                    if h == 0 and after and after.shared:
                        take(after)
                    if h == 1 and after:
                        copy(after)
                    if h == 2 and before and not before.shared:
                        store(before)

            for b in range(2):
                act.sem_inc(y_out[b], 16)
            take(lead(0))
            copy(lead(0))
            all_tiles(act, tile)

        @block.vector
        def _(dve):
            head_steps = Steps(dve, m.sem("dve_head"), 1)
            tail_steps = Steps(dve, m.sem("dve_tail"), 1)
            shared_added = m.sem("shared_added")
            routed_added = m.sem("routed_added")
            dve.sem_inc(y_copied, 1)
            dve.wait_ge(shared_b2_in, 16)

            def chunk(t, h):
                q = 4 * t.n + h
                head_steps.round(q)
                tail_steps.round(q)
                dve.wait_ge(x3_done, q + 1)
                for k in range(2):
                    last = nc.vector.scalar_tensor_tensor(gl[:, k, :], ps_up[h % 2][:, 0, k, :],
                                                          b13[t.w][:, h, 0, k:k + 1], x3[:, k, :], ALU.add, ALU.mult)
                head_steps.then_wait(last)
                nc.vector.tensor_scalar(glc[:, 0, :], gl[:, 0, :], 7.0, 0.5, ALU.min, ALU.mult)
                nc.vector.tensor_scalar(glc[:, 1, :], gl[:, 1, :], -7.0, 7.0, ALU.max, ALU.min)\
                    .then_inc(half_gate, 1)
                dve.wait_ge(th_done, q + 1)
                tail_steps.then_wait(nc.vector.scalar_tensor_tensor(gate[:, :], th[:, :], 1.0, glc[:, 0, :],
                                                                    ALU.add, ALU.mult))
                nc.vector.scalar_tensor_tensor(hT[t.b][:, h, :], glc[:, 1, :], 1.0, gate[:, :],
                                               ALU.add, ALU.mult).then_inc(h_done, 1)

            def copy_y(t):
                dve.wait_ge(down_done, t.n + 1)
                if not t.shared:
                    dve.wait_ge(y_out[t.b], 16 * t.g + 16)
                    nc.vector.tensor_tensor(yrow[t.b][:, :, :], ps_y[:, :, :], over(b2[t.w][:, :], 1, 2), ALU.add)\
                        .then_inc(y_copied, 1)
                    return
                n, s = (NB, 1) if isinstance(t.i, int) and 2 * t.i == CLS else (P, 2)
                h = H[0:n, bass.ds(2 * t.i, s), :]
                nc.vector.tensor_tensor(h, h, ps_y[0:n, 0:s, :], ALU.add).then_inc(y_copied, 1)
                dve.wait_ge(y_copied, t.n + 2)
                nc.vector.tensor_tensor(h, h, over(b2[2][0:n, :], 1, s), ALU.add).then_inc(shared_added, 1)

            def add_routed(t):
                n = P if t < CLS else NB
                h = H[0:n, t, :]
                dve.wait_ge(gathered[t % RING], 32 * (t // RING + 1))
                dve.wait_ge(shared_added, t // 2 + 1)
                nc.vector.scalar_tensor_tensor(h, routed[0:n, t % RING, 0, :], share[0][0:n, t:t + 1], h,
                                               ALU.mult, ALU.add).then_inc(routed_added, 1)
                dve.wait_ge(routed_added, t + 1)
                nc.vector.scalar_tensor_tensor(h, routed[0:n, t % RING, 1, :], share[1][0:n, t:t + 1], h,
                                               ALU.mult, ALU.add).then_inc(added, 1)

            tokens = iter(range(TOKEN_TILES))
            each = -(-TOKEN_TILES // (4 * (TRAIL - 1) + 1))

            def tile(before, t, after):
                ending = t.shared and isinstance(t.i, int) and t.i > SHARED - TRAIL
                for h in range(CH):
                    chunk(t, h)
                    if h == 1 and before:
                        copy_y(before)
                    if ending:
                        for _, token_tile in zip(range(each), tokens):
                            add_routed(token_tile)

            all_tiles(dve, tile)
            copy_y(trail(TRAIL - 1))
            for token_tile in tokens:
                add_routed(token_tile)


def queries_keys_values(nc, H, qkv, class_keys, vcls, args):
    G = AH // 4
    with ExitStack() as stack:
        m = Memory(nc, stack, "pj_")
        w = m.sb("w", [P, 2, 3 * D])
        cos = m.sb("cos", [P, 2, DH])
        sin = m.sb("sin", [P, 2, DH])
        ident = m.sb("ident", [P, P])
        mhalf = m.sb("mhalf", [P, 2])
        eps = m.sb("eps", [P, 2])
        stats = m.sb("stats", [P, 2, 6])
        mv = m.sb("mv", [P, 2, 2])
        rstd = m.sb("rstd", [P, 2])
        xp = m.sb("xp", [P, 2, D])
        xT = m.sb("xT", [P, 2, 2 * P])
        straight = m.sb("straight", [P, 2, 2 * D])
        crossed = m.sb("crossed", [P, 2, 2 * D])
        kpad = m.sb("kpad", [P, AH, 32])

        ps_xT = m.ps("ps_xT", [P, 2, 2 * P])
        ps_p = m.ps("ps_p", [P, 2, 4, D])
        ps_kT = m.ps("ps_kT", [P, G, P])

        consts_in = m.sem("consts_in")
        consts = m.sem("consts")
        zeroed = m.sem("zeroed")
        ident_done = m.sem("ident_done")
        var_done = m.sem("var_done")
        rstd_done = m.sem("rstd_done")
        xp_done = m.sem("xp_done")
        xT_done = m.sem("xT_done")
        xT_copied = m.sem("xT_copied")
        p_done = m.sem("p_done")
        v_copied = m.sem("v_copied")
        turned = m.sem("turned")
        added = m.sem("added")
        kpad_done = m.sem("kpad_done")
        kT_done = m.sem("kT_done")
        keys_done = m.sem("keys_done")
        vcls_out = m.sem("vcls_out")
        PAIRS = NT // 2

        block = stack.enter_context(nc.Block())

        @block.sync
        def _(sp):
            sp.dma_start(w[:, :, :], args["att_w"].rearrange("(c p) n -> p c n", p=P)).then_inc(consts_in, 16)
            sp.dma_start(cos[:, :, :], args["rope_cos"].rearrange("(s p) j -> p s j", p=P)).then_inc(consts_in, 16)
            sp.dma_start(sin[:, :, :], args["rope_sin"].rearrange("(s p) j -> p s j", p=P)).then_inc(consts_in, 16)
            sp.wait_ge(v_copied, PAIRS + 1)
            sp.dma_start(vcls, qkv[0:NB, CLS, 2 * D:3 * D]).then_inc(vcls_out, 16)
            sp.wait_ge(vcls_out, 16)

        @block.gpsimd
        def _(pool):
            pool.sem_inc(added, 1)
            nc.gpsimd.memset(mhalf[:, :], -0.5).then_inc(consts, 1)
            nc.gpsimd.memset(eps[:, :], EPS).then_inc(consts, 1)
            nc.gpsimd.memset(ident[:, :], 0.0).then_inc(consts, 1)
            pool.wait_ge(consts, 3)
            nc.gpsimd.affine_select(out=ident[:, :], in_=ident[:, :], compare_op=ALU.not_equal, fill=1.0,
                                    base=0, pattern=[[-1, P]], channel_multiplier=1).then_inc(ident_done, 1)
            nc.gpsimd.memset(kpad[:, :, :], 0.0).then_inc(zeroed, 1)
            nc.gpsimd.memset(class_keys[:, :, :, :], 0.0).then_inc(zeroed, 1)
            steps = Steps(pool, m.sem("pool_rstd"), 1)

            def root(k):
                steps.round(k)
                pool.wait_ge(var_done, k + 1)
                steps.then_wait(nc.gpsimd.tensor_tensor(rstd[:, :], mv[:, :, 1], eps[:, :], ALU.add))
                nc.gpsimd.tensor_tensor(rstd[:, :], rstd[:, :], mhalf[:, :], ALU.pow).then_inc(rstd_done, 1)

            root(0)
            with pool.Fori(0, PAIRS - 1) as k:
                root(k + 1)
                pool.wait_ge(turned, k + 2)
                nc.gpsimd.tensor_tensor(qkv[:, bass.ds(2 * k, 2), 0:2 * D], straight[:, :, :], crossed[:, :, :],
                                        ALU.add).then_inc(added, 1)

        @block.tensor
        def _(pe):
            pe.wait_ge(ident_done, 1)
            pe.wait_ge(consts_in, 3 * 16)
            with pe.Fori(0, PAIRS) as k:
                pe.wait_ge(xp_done, k + 1)
                for c in range(2):
                    for s in range(2):
                        last = nc.tensor.transpose(ps_xT[:, c, s * P:(s + 1) * P],
                                                   xp[:, s, c * P:(c + 1) * P], ident[:, :])
                last.then_inc(xT_done, 1)
                pe.wait_ge(xT_copied, k + 1)
                pe.wait_ge(v_copied, k + 1)
                pe.wait_ge(turned, k + 1)
                for s in range(2):
                    for j in range(3):
                        for c in range(2):
                            last = nc.tensor.matmul(ps_p[:, s, j, :], xT[:, c, s * P:(s + 1) * P],
                                                    w[:, c, j * D:(j + 1) * D], start=c == 0, stop=c == 1)
                last.then_inc(p_done, 1)
            pe.wait_ge(kpad_done, 1)
            for g in range(G):
                last = nc.tensor.transpose(ps_kT[:, g, :], kpad[:, 4 * g:4 * g + 4, :], ident[:, :])
            last.then_inc(kT_done, 1)

        @block.scalar
        def _(act):
            act.sem_inc(v_copied, 1)
            with act.Fori(0, PAIRS) as k:
                act.wait_ge(xT_done, k + 1)
                nc.scalar.activation(xT[:, :, :], ps_xT[:, :, :], ACT.Copy).then_inc(xT_copied, 1)
                act.wait_ge(p_done, k + 1)
                for s in range(2):
                    last = nc.scalar.activation(qkv[:, bass.ds(2 * k + s, 1), 2 * D:3 * D], ps_p[:, s, 2:3, :],
                                                ACT.Copy)
                last.then_inc(v_copied, 1)
            nc.scalar.activation(qkv[:, CLS:NT, 0:D], ps_p[:, :, 2, :], ACT.Copy)
            act.wait_ge(zeroed, 1)
            nc.scalar.activation(kpad[:, :, 0:DH], ps_p[:, 0, 1, :].rearrange("p (h j) -> p h j", h=AH),
                                 ACT.Copy).then_inc(kpad_done, 1)
            act.wait_ge(kT_done, 1)
            act.wait_ge(zeroed, 2)
            for j in range(4):
                rows = slice(32 * j, 32 * j + 32)
                last = nc.scalar.activation(class_keys[rows, :, j, :], ps_kT[rows, :, 0:NB], ACT.Copy)
            last.then_inc(keys_done, 1)

        @block.vector
        def _(dve):
            stat_steps = Steps(dve, m.sem("dve_stat"), 1)
            dve.sem_inc(turned, 1)
            dve.wait_ge(consts_in, 3 * 16)

            def normalise(k):
                stat_steps.round(k)
                for s in range(2):
                    last = nc.vector.bn_stats(stats[:, s, :], H[:, bass.ds(2 * k + s, 1), :])
                stat_steps.then_wait(last, (consts_in, 3 * 16))
                for s in range(2):
                    last = nc.vector.bn_aggr(mv[:, s, :], stats[:, s, :])
                last.then_inc(var_done, 1)
                dve.wait_ge(rstd_done, k + 1)
                dve.wait_ge(xT_done, k)
                for s in range(2):
                    last = nc.vector.tensor_scalar(xp[:, s, :], H[:, bass.ds(2 * k + s, 1), :],
                                                   mv[:, s, 0:1], rstd[:, s:s + 1], ALU.subtract, ALU.mult)
                last.then_inc(xp_done, 1)

            normalise(0)
            with dve.Fori(0, PAIRS - 1) as k:
                normalise(k + 1)
                dve.wait_ge(p_done, k + 1)
                dve.wait_ge(added, k + 1)
                hd = DH // 2
                for s in range(2):
                    p = ps_p[:, s, 0:2, :].rearrange("p a (h j) -> p (a h) j", j=DH)
                    o = straight[:, s, :].rearrange("p (h j) -> p h j", j=DH)
                    x = crossed[:, s, :].rearrange("p (h j) -> p h j", j=DH)
                    nc.vector.tensor_tensor(o, p, over(cos[:, s, :], 1, 2 * AH), ALU.mult)
                    nc.vector.tensor_tensor(x[:, :, 0:hd], p[:, :, hd:DH], over(sin[:, s, 0:hd], 1, 2 * AH),
                                            ALU.mult)
                    last = nc.vector.tensor_tensor(x[:, :, hd:DH], p[:, :, 0:hd],
                                                   over(sin[:, s, hd:DH], 1, 2 * AH), ALU.mult)
                last.then_inc(turned, 1)


def attention(nc, qkv, class_keys, vcls, args):
    G = AH // 4
    R = AH // 2
    QK = 0.25
    with ExitStack() as stack:
        m = Memory(nc, stack, "at_")
        ident = m.sb("ident", [P, P])
        ident16 = m.sb("ident16", [P, P], BF16)
        hidden = m.sb("hidden", [P, P], BF16)
        pad = m.sb("pad", [P, 2, 2, AH, 32])
        v1 = m.sb("v1", [P, 2, AH, DH + 1])
        vc = m.sb("vc", [P, D])
        qkT = m.sb("qkT", [P, 2, G, 2, P])
        sc = m.sb("sc", [P, 2, AH])
        mx = m.sb("mx", [P, AH, 2])
        nmx = m.sb("nmx", [P, AH, 2])
        pr = [m.sb(f"pr{b}", [P, 2, 3 * P]) for b in range(2)]
        pT = [m.sb(f"pT{b}", [P, 2, 3 * P]) for b in range(2)]
        pc = m.sb("pc", [P, 2, AH])
        den = m.sb("den", [P, 2, AH])
        o = m.sb("o", [P, 2, AH, DH])

        ps_s = [m.ps(f"ps_s{b}", [P, 2, 512]) for b in range(2)]
        ps_t = m.ps("ps_t", [P, 2, 512])
        ps_o = m.ps("ps_o", [P, 2, 512])
        ps_v = ps_o[:, :, 0:AH * (DH + 1)].rearrange("p q (h j) -> p q h j", h=AH)
        ps_c = ps_o[:, :, 288:288 + AH]

        zeroed = m.sem("zeroed")
        ident_done = m.sem("ident_done")
        ident16_done = m.sem("ident16_done")
        padded = m.sem("padded")
        v1_done = m.sem("v1_done")
        vc_in = m.sem("vc_in")
        turned = m.sem("turned")
        q_copied = m.sem("q_copied")
        k_copied = m.sem("k_copied")
        sc_done = m.sem("sc_done")
        sc_copied = m.sem("sc_copied")
        s_done = m.sem("s_done")
        nmx_done = m.sem("nmx_done")
        exp_done = m.sem("exp_done")
        pT_done = m.sem("pT_done")
        pT_copied = m.sem("pT_copied")
        pv_done = m.sem("pv_done")
        sc_less = m.sem("sc_less")
        pc_done = m.sem("pc_done")
        o_read = m.sem("o_read")
        o_done = m.sem("o_done")

        block = stack.enter_context(nc.Block())

        @block.sync
        def _(sp):
            sp.dma_start(vc[:, :], vcls[0:1, :].broadcast_to([P, D])).then_inc(vc_in, 16)
            with sp.Fori(1, NB) as n:
                sp.wait_ge(o_read, n + 1)
                sp.dma_start(vc[:, :], vcls[bass.ds(n, 1), :].broadcast_to([P, D])).then_inc(vc_in, 16)

        @block.gpsimd
        def _(pool):
            nc.gpsimd.memset(ident[:, :], 0.0).then_inc(zeroed, 1)
            nc.gpsimd.memset(hidden[:, :], 0.0).then_inc(zeroed, 1)
            nc.gpsimd.memset(pad[:, :, :, :, :], 0.0).then_inc(zeroed, 1)
            nc.gpsimd.memset(v1[:, :, :, DH:DH + 1], 1.0).then_inc(zeroed, 1)
            pool.wait_ge(zeroed, 4)
            nc.gpsimd.affine_select(out=ident[:, :], in_=ident[:, :], compare_op=ALU.not_equal, fill=1.0,
                                    base=0, pattern=[[-1, P]], channel_multiplier=1).then_inc(ident_done, 1)
            nc.gpsimd.affine_select(out=hidden[:, :], in_=hidden[:, :], compare_op=ALU.is_ge, fill=-1e30,
                                    base=0, pattern=[[-1, P]], channel_multiplier=1).then_inc(ident_done, 1)
            pool.wait_ge(ident_done, 2)
            nc.gpsimd.tensor_copy(ident16[:, :], ident[:, :]).then_inc(ident16_done, 1)
            with pool.Fori(0, NB) as n:
                pool.wait_ge(pv_done, R * n + 1)
                nc.gpsimd.tensor_copy(v1[:, :, :, 0:DH], qkv[:, bass.ds(2 * n, 2), 2 * D:3 * D].rearrange(
                    "p s (h j) -> p s h j", h=AH)).then_inc(v1_done, 1)

        @block.tensor
        def _(pe):
            pe.wait_ge(ident16_done, 1)
            pe.sem_inc(pv_done, 1)

            def scores(n, r):
                b = r % 2
                if r >= 2:
                    pe.wait_ge(exp_done, R * n + r)
                for hh in range(2):
                    h = 2 * r + hh
                    g, rows = h // 4, slice(32 * (h % 4), 32 * (h % 4) + DH)
                    q, k = qkT[rows, 0, g], qkT[rows, 1, g]
                    nc.tensor.matmul(ps_s[b][:, hh, 0:P], q[:, 0, :], k[:, 0, :], start=True, stop=False)
                    nc.tensor.matmul(ps_s[b][:, hh, 0:P], ident16[:, :], hidden[:, :], start=False, stop=True)
                    nc.tensor.matmul(ps_s[b][:, hh, P:3 * P], q[:, 1, :], k.rearrange("p s t -> p (s t)"),
                                     start=True, stop=False)
                    last = nc.tensor.matmul(ps_s[b][:, hh, 2 * P:3 * P], ident16[:, :], hidden[:, :],
                                            start=False, stop=True)
                last.then_inc(s_done, 1)

            def turn(n, r):
                pe.wait_ge(exp_done, R * n + r + 2)
                pe.wait_ge(pT_copied, R * n + r + 1)
                for hh in range(2):
                    for c in range(3):
                        last = nc.tensor.transpose(ps_t[:, hh, c * P:(c + 1) * P],
                                                   pr[r % 2][:, hh, c * P:(c + 1) * P], ident[:, :])
                last.then_inc(pT_done, 1)

            def values(n, r):
                pe.wait_ge(pT_copied, R * n + r + 2)
                for hh in range(2):
                    h = 2 * r + hh
                    p = pT[r % 2]
                    nc.tensor.matmul(ps_v[:, 0, h, :], p[:, hh, 0:P], v1[:, 0, h, :], start=True, stop=True)
                    nc.tensor.matmul(ps_v[:, 1, h, :], p[:, hh, P:2 * P], v1[:, 0, h, :], start=True, stop=False)
                    last = nc.tensor.matmul(ps_v[:, 1, h, :], p[:, hh, 2 * P:3 * P], v1[:, 1, h, :],
                                            start=False, stop=True)
                last.then_inc(pv_done, 1)

            with pe.Fori(0, NB) as n:
                pe.wait_ge(padded, n + 1)
                pe.wait_ge(exp_done, R * n + 1)
                for a in range(2):
                    t = ps_s[a][:, :, :].rearrange("p a (g s t) -> p (a g) s t", g=2, s=2)
                    for g in range(G):
                        for s in range(2):
                            last = nc.tensor.transpose(t[:, g, s, :], pad[:, s, a, 4 * g:4 * g + 4, :], ident[:, :])
                last.then_inc(turned, 1)
                pe.wait_ge(q_copied, n + 1)
                pe.wait_ge(o_read, n + 1)
                for s in range(2):
                    for g in range(G):
                        last = nc.tensor.matmul(ps_c[:, s, 4 * g:4 * g + 4], qkT[:, 0, g, s, :],
                                                class_keys[:, g, :, bass.ds(n, 1)], start=True, stop=True)
                last.then_inc(sc_done, 1)
                pe.wait_ge(k_copied, n + 1)
                pe.wait_ge(v1_done, n + 1)
                scores(n, 0)
                for r in range(R):
                    if r + 1 < R:
                        scores(n, r + 1)
                    turn(n, r)
                    if r:
                        values(n, r - 1)
                values(n, R - 1)

        @block.scalar
        def _(act):
            act.wait_ge(zeroed, 4)
            act.sem_inc(exp_done, 1)

            def pads(n):
                act.wait_ge(turned, n)
                for s in range(2):
                    last = nc.scalar.activation(
                        pad[:, s, :, :, 0:DH].rearrange("p a h j -> p (a h) j"),
                        qkv[:, bass.ds(2 * n + s, 1), 0:2 * D].rearrange("p o (h j) -> p (o h) j", j=DH),
                        ACT.Copy)
                last.then_inc(padded, 1)

            def sequence(n):
                act.wait_ge(turned, n + 1)
                nc.scalar.activation(qkT[:, 0].rearrange("p g s t -> p (g s t)"),
                                     ps_s[0][:, :, :].rearrange("p a b -> p (a b)"), ACT.Copy).then_inc(q_copied, 1)
                for r in range(R):
                    act.wait_ge(nmx_done, R * n + r + 1)
                    if r >= 2:
                        act.wait_ge(pT_done, R * n + r - 1)
                    for hh in range(2):
                        h = 2 * r + hh
                        nc.scalar.activation(pr[r % 2][:, hh, 0:P], ps_s[r % 2][:, hh, 0:P], ACT.Exp,
                                             bias=nmx[:, h, 0:1], scale=QK)
                        last = nc.scalar.activation(pr[r % 2][:, hh, P:3 * P], ps_s[r % 2][:, hh, P:3 * P], ACT.Exp,
                                                    bias=nmx[:, h, 1:2], scale=QK)
                    last.then_inc(exp_done, 1)
                act.wait_ge(sc_less, n + 1)
                nc.scalar.activation(pc[:, :, :], pc[:, :, :], ACT.Exp, scale=QK).then_inc(pc_done, 1)

            pads(0)
            with act.Fori(0, NB - 1) as n:
                sequence(n)
                pads(n + 1)
            sequence(NB - 1)

        @block.vector
        def _(dve):
            mx_steps = Steps(dve, m.sem("dve_mx"), 2)
            out_steps = Steps(dve, m.sem("dve_out"), 1)
            dve.sem_inc(pT_copied, 1)
            dve.sem_inc(o_read, 1)

            def maxima(n, r):
                mx_steps.round(R * n + r)
                dve.wait_ge(s_done, R * n + r + 1)
                two = slice(2 * r, 2 * r + 2)
                nc.vector.tensor_reduce(mx[:, two, 0], ps_s[r % 2][:, :, 0:P], axis=AX.X, op=ALU.max)
                mx_steps.then_wait(nc.vector.tensor_reduce(mx[:, two, 1], ps_s[r % 2][:, :, P:3 * P],
                                                           axis=AX.X, op=ALU.max))
                mx_steps.then_wait(nc.vector.tensor_tensor(mx[:, two, :], mx[:, two, :],
                                                           sc[:, :, two].rearrange("p q h -> p h q"), ALU.max))
                nc.vector.tensor_scalar(nmx[:, two, :], mx[:, two, :], -QK, None, ALU.mult).then_inc(nmx_done, 1)

            def copy_pT(n, r):
                dve.wait_ge(pT_done, R * n + r + 1)
                if r >= 2:
                    dve.wait_ge(pv_done, R * n + r)
                nc.vector.tensor_copy(pT[r % 2][:, :, :], ps_t[:, :, 0:3 * P]).then_inc(pT_copied, 1)

            with dve.Fori(0, NB) as n:
                dve.wait_ge(turned, n + 1)
                nc.vector.tensor_copy(qkT[:, 1].rearrange("p g s t -> p (g s t)"),
                                      ps_s[1][:, :, :].rearrange("p a b -> p (a b)")).then_inc(k_copied, 1)
                dve.wait_ge(sc_done, n + 1)
                nc.vector.tensor_copy(sc[:, :, :], ps_c).then_inc(sc_copied, 1)
                dve.wait_ge(sc_copied, n + 1)
                maxima(n, 0)
                for r in range(R):
                    if r + 1 < R:
                        maxima(n, r + 1)
                    else:
                        dve.wait_ge(nmx_done, R * n + R)
                        nc.vector.tensor_tensor(pc[:, :, :], sc[:, :, :], mx[:, :, :].rearrange("p h q -> p q h"),
                                                ALU.subtract).then_inc(sc_less, 1)
                    copy_pT(n, r)
                out_steps.round(n)
                dve.wait_ge(pc_done, n + 1)
                dve.wait_ge(vc_in, 16 * n + 16)
                dve.wait_ge(pv_done, R * n + R + 1)
                for q in range(2):
                    nc.vector.tensor_tensor(o[:, q], over(pc[:, q, :], 2, DH),
                                            vc[:, :].rearrange("p (h j) -> p h j", h=AH), ALU.mult)
                out_steps.then_wait(nc.vector.tensor_tensor(den[:, :, :], ps_v[:, :, :, DH], pc[:, :, :], ALU.add))
                nc.vector.reciprocal(den[:, :, :], den[:, :, :])
                for q in range(2):
                    last = nc.vector.tensor_tensor(o[:, q], o[:, q], ps_v[:, q, :, 0:DH], ALU.add)
                last.then_inc(o_read, 1)
                dve.wait_ge(o_read, n + 2)
                for q in range(2):
                    last = nc.vector.tensor_tensor(
                        qkv[:, bass.ds(2 * n + q, 1), 0:D].rearrange("p o (h j) -> p (o h) j", h=AH), o[:, q],
                        over(den[:, q, :], 2, DH), ALU.mult)
                last.then_inc(o_done, 1)


def bitlinear_ffn(nc, H, att, args, out):
    F = 1024
    FC = F // P
    HALF = F // 2
    T = CLS + 1
    with ExitStack() as stack:
        m = Memory(nc, stack, "ff_")
        ident = m.sb("ident", [P, P])
        ident16 = m.sb("ident16", [P, P], BF16)
        ones = m.sb("ones", [P, P])
        mhalf = m.sb("mhalf", [P, 1])
        eps = m.sb("eps", [P, 1])
        wo = m.sb("wo", [P, 2, D])
        wf = m.sb("wf", [P, 2, 2 * F])
        wdf = m.sb("wdf", [P, FC, D])
        wq = m.sb("wq", [P, 2, 2 * F], BF16)
        wdq = m.sb("wdq", [P, FC, D], BF16)
        sums = m.sb("sums", [P, 3])
        wscale = m.sb("wscale", [P, 3])
        winv = m.sb("winv", [P, 3])
        ao = [m.sb(f"ao{b}", [P, D]) for b in range(2)]
        aoT = m.sb("aoT", [P, 2, P])
        stats = m.sb("stats", [P, 6])
        mv = m.sb("mv", [P, 2])
        rstd = m.sb("rstd", [P, 1])
        xn = m.sb("xn", [P, D])
        xr = m.sb("xr", [P, D])
        xq = m.sb("xq", [P, D], BF16)
        xqT = m.sb("xqT", [P, 2, P], BF16)
        amax = m.sb("amax", [P, 1])
        ascale = m.sb("ascale", [P, 1])
        gate_scale = [m.sb(f"gate_scale{b}", [P, 1]) for b in range(2)]
        up_scale = [m.sb(f"up_scale{b}", [P, 1]) for b in range(2)]
        silu = m.sb("silu", [P, F])
        z = [m.sb(f"z{b}", [P, F]) for b in range(2)]
        zq = m.sb("zq", [P, F], BF16)
        zqT = m.sb("zqT", [P, FC, P], BF16)
        zmax = m.sb("zmax", [P, 1])
        zscale = m.sb("zscale", [P, 1])
        zmul = m.sb("zmul", [P, 1])
        down_scale = [m.sb(f"down_scale{b}", [P, 1]) for b in range(2)]
        res = [m.sb(f"res{b}", [P, D]) for b in range(2)]

        ps_gu = m.ps("ps_gu", [P, 2, 2, HALF])
        ps_tr = m.ps("ps_tr", [P, 4, P])
        ps_aoT = ps_tr[:, 0:2, :]
        ps_xqT = ps_tr[:, 2, :].bitcast(BF16).rearrange("p (c t) -> p c t", c=2)
        ps_h = m.ps("ps_h", [P, D])
        ps_d = m.ps("ps_d", [P, D])
        ps_zqT = m.ps("ps_zqT", [P, FC, P], BF16)

        w_in = m.sem("w_in")
        consts = m.sem("consts")
        ident_done = m.sem("ident_done")
        sums_done = m.sem("sums_done")
        total_done = m.sem("total_done")
        wq_done = m.sem("wq_done")
        ao_copied = m.sem("ao_copied")
        aoT_done = m.sem("aoT_done")
        aoT_copied = m.sem("aoT_copied")
        h_done = m.sem("h_done")
        var_done = m.sem("var_done")
        rstd_done = m.sem("rstd_done")
        xq_done = m.sem("xq_done")
        xqT_done = m.sem("xqT_done")
        xqT_copied = m.sem("xqT_copied")
        gu_done = m.sem("gu_done")
        silu_done = m.sem("silu_done")
        gu_read = m.sem("gu_read")
        zr_done = m.sem("zr_done")
        zq_done = m.sem("zq_done")
        zqT_done = m.sem("zqT_done")
        zqT_copied = m.sem("zqT_copied")
        down_done = m.sem("down_done")
        res_done = m.sem("res_done")
        stored = [m.sem(f"stored{b}") for b in range(2)]

        def exists(t):
            return not isinstance(t, int) or 0 <= t < T

        def all_turns(engine, turn):
            turn(0, 0)
            pairs = (T - 4) // 2
            with engine.Fori(0, pairs) as i:
                turn(2 * i + 1, 1)
                turn(2 * i + 2, 0)
            for t in range(2 * pairs + 1, T + 1):
                turn(t, t % 2)

        block = stack.enter_context(nc.Block())

        @block.sync
        def _(sp):
            sp.dma_start(wf[:, :, :], args["ffn_gu"].rearrange("(c p) n -> p c n", p=P)).then_inc(w_in, 16)
            sp.dma_start(wdf[:, :, :], args["ffn_down"].rearrange("(c p) n -> p c n", p=P)).then_inc(w_in, 16)
            sp.dma_start(wo[:, :, :], args["att_wo"].rearrange("(c p) n -> p c n", p=P)).then_inc(w_in, 16)
            for b in range(2):
                sp.sem_inc(stored[b], 16)
            with sp.Fori(0, NB) as i:
                for b in range(2):
                    sp.wait_ge(res_done, 2 * i + b + 1)
                    sp.dma_start(out[bass.ds(i, 1), 1 + b * P:1 + (b + 1) * P, :].rearrange("o p d -> (o p) d"),
                                 res[b][:, :]).then_inc(stored[b], 16)
            sp.wait_ge(res_done, 2 * NB + 1)
            sp.dma_start(out[:, 0, :], res[0][0:NB, :]).then_inc(stored[0], 16)
            sp.wait_ge(stored[0], 16 * (NB + 2))
            sp.wait_ge(stored[1], 16 * (NB + 1))

        @block.gpsimd
        def _(pool):
            nc.gpsimd.memset(mhalf[:, :], -0.5).then_inc(consts, 1)
            nc.gpsimd.memset(eps[:, :], EPS).then_inc(consts, 1)
            nc.gpsimd.memset(ones[:, :], 1.0).then_inc(consts, 1)
            nc.gpsimd.memset(ident[:, :], 0.0).then_inc(consts, 1)
            pool.wait_ge(consts, 4)
            nc.gpsimd.affine_select(out=ident[:, :], in_=ident[:, :], compare_op=ALU.not_equal, fill=1.0,
                                    base=0, pattern=[[-1, P]], channel_multiplier=1).then_inc(ident_done, 1)
            pool.wait_ge(ident_done, 1)
            nc.gpsimd.tensor_copy(ident16[:, :], ident[:, :]).then_inc(ident_done, 1)
            steps = Steps(pool, m.sem("pool_rstd"), 1)

            def take(t, b):
                if not isinstance(t, int) or t >= 2:
                    pool.wait_ge(aoT_done, t - 1)
                nc.gpsimd.tensor_copy(ao[b][:, :], att[:, bass.ds(t, 1), 0:D]).then_inc(ao_copied, 1)

            def root(t):
                steps.round(t)
                pool.wait_ge(var_done, t + 1)
                steps.then_wait(nc.gpsimd.tensor_tensor(rstd[:, :], mv[:, 1:2], eps[:, :], ALU.add))
                nc.gpsimd.tensor_tensor(rstd[:, :], rstd[:, :], mhalf[:, :], ALU.pow).then_inc(rstd_done, 1)

            def turn(t, b):
                if exists(t + 3):
                    take(t + 3, 1 - b)
                if exists(t + 2):
                    root(t + 2)

            for t in range(3):
                take(t, t % 2)
            for t in range(2):
                root(t)
            all_turns(pool, turn)

        @block.tensor
        def _(pe):
            pe.wait_ge(consts, 4)
            pe.wait_ge(sums_done, 1)
            nc.tensor.matmul(ps_aoT[:, 0, 0:3], ones[:, :], sums[:, :], start=True, stop=True).then_inc(total_done, 1)
            pe.wait_ge(wq_done, 1)
            pe.wait_ge(ident_done, 2)
            pe.wait_ge(w_in, 3 * 16)

            def turn_ao(t, b):
                pe.wait_ge(ao_copied, t + 1)
                for c in range(2):
                    last = nc.tensor.transpose(ps_aoT[:, c, :], ao[b][:, c * P:(c + 1) * P], ident[:, :])
                last.then_inc(aoT_done, 1)

            def project(t):
                pe.wait_ge(aoT_copied, t + 1)
                for c in range(2):
                    last = nc.tensor.matmul(ps_h[:, :], aoT[:, c, :], wo[:, c, :], start=c == 0, stop=c == 1)
                last.then_inc(h_done, 1)

            def turn_x(t):
                pe.wait_ge(xq_done, t + 1)
                pe.wait_ge(aoT_copied, t + 2 if not isinstance(t, int) else max(3, min(t + 2, T)))
                for c in range(2):
                    last = nc.tensor.transpose(ps_xqT[:, c, :], xq[:, c * P:(c + 1) * P], ident16[:, :])
                last.then_inc(xqT_done, 1)

            def up(t, half):
                if half == 0:
                    pe.wait_ge(xqT_copied, t + 1)
                if not isinstance(t, int) or t > 0:
                    pe.wait_ge(gu_read, 2 * t - 1 + half)
                for k in range(2):
                    for c in range(2):
                        cols = slice(k * F + half * HALF, k * F + (half + 1) * HALF)
                        last = nc.tensor.matmul(ps_gu[:, half, k, :], xqT[:, c, :], wq[:, c, cols],
                                                start=c == 0, stop=c == 1)
                last.then_inc(gu_done, 1)

            def turn_z(t):
                pe.wait_ge(zq_done, t + 1)
                for c in range(FC):
                    last = nc.tensor.transpose(ps_zqT[:, c, :], zq[:, c * P:(c + 1) * P], ident16[:, :])
                last.then_inc(zqT_done, 1)

            def down(t):
                pe.wait_ge(zqT_copied, t + 1)
                for c in range(FC):
                    last = nc.tensor.matmul(ps_d[:, :], zqT[:, c, :], wdq[:, c, :], start=c == 0, stop=c == FC - 1)
                last.then_inc(down_done, 1)

            def turn(t, b):
                if exists(t + 2):
                    pe.wait_ge(var_done, t + 2)
                    project(t + 2)
                if exists(t - 1):
                    turn_z(t - 1)
                if exists(t + 1):
                    turn_x(t + 1)
                if exists(t - 1):
                    if not isinstance(t, int) or t > 1:
                        pe.wait_ge(res_done, t - 1)
                    down(t - 1)
                if exists(t + 1):
                    up(t + 1, 0)
                    up(t + 1, 1)
                if exists(t + 3):
                    turn_ao(t + 3, 1 - b)

            turn_ao(0, 0)
            project(0)
            turn_ao(1, 1)
            pe.wait_ge(var_done, 1)
            project(1)
            turn_ao(2, 0)
            turn_x(0)
            up(0, 0)
            up(0, 1)
            all_turns(pe, turn)

        @block.scalar
        def _(act):
            def copy_ao(t):
                act.wait_ge(aoT_done, t + 1)
                nc.scalar.activation(aoT[:, :, :], ps_aoT, ACT.Copy).then_inc(aoT_copied, 1)

            def copy_x(t):
                act.wait_ge(xqT_done, t + 1)
                nc.scalar.activation(xqT[:, :, :], ps_xqT, ACT.Copy).then_inc(xqT_copied, 1)

            def gate(t, b, half):
                act.wait_ge(gu_done, 2 * t + half + 1)
                nc.scalar.activation(silu[:, half * HALF:(half + 1) * HALF], ps_gu[:, half, 0, :], ACT.Silu,
                                     scale=gate_scale[b][:, :]).then_inc(silu_done, 1)

            def round_z(t, b):
                act.wait_ge(zr_done, t + 1)
                nc.scalar.activation(zq[:, :], z[b][:, :], ACT.Copy, bias=-MAGIC).then_inc(zq_done, 1)

            def copy_z(t):
                act.wait_ge(zqT_done, t + 1)
                nc.scalar.activation(zqT[:, :, :], ps_zqT[:, :, :], ACT.Copy).then_inc(zqT_copied, 1)

            def turn(t, b):
                if exists(t + 1):
                    copy_x(t + 1)
                if exists(t - 1):
                    copy_z(t - 1)
                if exists(t + 1):
                    gate(t + 1, 1 - b, 0)
                    gate(t + 1, 1 - b, 1)
                if exists(t):
                    round_z(t, b)
                if exists(t + 3):
                    copy_ao(t + 3)

            for t in range(3):
                copy_ao(t)
            copy_x(0)
            gate(0, 0, 0)
            gate(0, 0, 1)
            all_turns(act, turn)

        @block.vector
        def _(dve):
            v = nc.vector
            setup = Steps(dve, m.sem("dve_setup"), 100)
            go = setup.then_wait
            dve.wait_ge(w_in, 3 * 16)
            parts = [wf[:, :, 0:F], wf[:, :, F:2 * F], wdf[:, :, :]]
            rounded = [wq[:, :, 0:F], wq[:, :, F:2 * F], wdq[:, :, :]]
            for k, part in enumerate(parts):
                last = v.tensor_reduce(sums[:, k:k + 1], part, axis=AX.XY, op=ALU.add, apply_absolute_value=True)
            last.then_inc(sums_done, 1)
            dve.wait_ge(total_done, 1)
            go(v.tensor_scalar(winv[:, :], ps_aoT[:, 0, 0:3], 1.0 / (F * D), 1e-5, ALU.mult, ALU.max))
            go(v.reciprocal(wscale[:, :], winv[:, :]))
            go(v.reciprocal(winv[:, :], wscale[:, :]))
            for k, part in enumerate(parts):
                last = v.tensor_scalar(part, part, wscale[:, k:k + 1], MAGIC, ALU.mult, ALU.add)
            go(last)
            for k, part in enumerate(parts):
                last = v.tensor_scalar(part, part, MAGIC - 1, MAGIC + 1, ALU.max, ALU.min)
            go(last)
            for k, part in enumerate(parts):
                last = v.tensor_scalar(rounded[k], part, MAGIC, None, ALU.subtract)
            last.then_inc(wq_done, 1)

            add_steps = Steps(dve, m.sem("dve_add"), 2)
            round_steps = Steps(dve, m.sem("dve_round"), 6)
            z_steps = Steps(dve, m.sem("dve_z"), 7)

            def add_projection(t):
                add_steps.round(t)
                go = add_steps.then_wait
                h = H[:, bass.ds(t, 1), :]
                dve.wait_ge(h_done, t + 1)
                go(v.tensor_tensor(h, ps_h[:, :], h, ALU.add), (w_in, 3 * 16))
                go(v.bn_stats(stats[:, :], h), (w_in, 3 * 16))
                v.bn_aggr(mv[:, :], stats[:, :]).then_inc(var_done, 1)

            def round_x(t, b):
                round_steps.round(t)
                go = round_steps.then_wait
                dve.wait_ge(rstd_done, t + 1)
                go(v.tensor_scalar(xn[:, :], H[:, bass.ds(t, 1), :], mv[:, 0:1], rstd[:, :],
                                   ALU.subtract, ALU.mult))
                go(v.tensor_reduce(amax[:, :], xn[:, :], axis=AX.X, op=ALU.max, apply_absolute_value=True))
                go(v.tensor_scalar(amax[:, :], amax[:, :], 1e-5, 1.0 / 127.0, ALU.max, ALU.mult))
                go(v.reciprocal(ascale[:, :], amax[:, :]))
                go(v.tensor_scalar(xr[:, :], xn[:, :], ascale[:, :], MAGIC, ALU.mult, ALU.add))
                v.tensor_scalar(gate_scale[b][:, :], amax[:, :], winv[:, 0:1], None, ALU.mult)
                v.tensor_scalar(up_scale[b][:, :], amax[:, :], winv[:, 1:2], None, ALU.mult)
                go(v.tensor_scalar(xr[:, :], xr[:, :], MAGIC - 128, MAGIC + 127, ALU.max, ALU.min))
                if not isinstance(t, int) or t > 0:
                    dve.wait_ge(xqT_done, t)
                v.tensor_scalar(xq[:, :], xr[:, :], MAGIC, None, ALU.subtract).then_inc(xq_done, 1)

            def multiply(t, b):
                z_steps.round(t)
                go = z_steps.then_wait
                for half in range(2):
                    cols = slice(half * HALF, (half + 1) * HALF)
                    dve.wait_ge(silu_done, 2 * t + half + 1)
                    v.tensor_tensor(z[b][:, cols], silu[:, cols], ps_gu[:, half, 1, :], ALU.mult)\
                        .then_inc(gu_read, 1)
                dve.wait_ge(gu_read, 2 * t + 2)
                go(v.tensor_reduce(zmax[:, :], z[b][:, :], axis=AX.X, op=ALU.max, apply_absolute_value=True))
                go(v.tensor_scalar(zmax[:, :], zmax[:, :], up_scale[b][:, :], 1e-5, ALU.mult, ALU.max))
                go(v.tensor_scalar(zmax[:, :], zmax[:, :], 1.0 / 127.0, None, ALU.mult))
                go(v.reciprocal(zscale[:, :], zmax[:, :]))
                go(v.tensor_scalar(zmul[:, :], zscale[:, :], up_scale[b][:, :], None, ALU.mult))
                go(v.tensor_scalar(z[b][:, :], z[b][:, :], zmul[:, :], MAGIC, ALU.mult, ALU.add))
                v.tensor_scalar(z[b][:, :], z[b][:, :], MAGIC - 128, MAGIC + 127, ALU.max, ALU.min)\
                    .then_inc(zr_done, 1)
                go(v.tensor_scalar(down_scale[b][:, :], zmax[:, :], winv[:, 2:3], None, ALU.mult))

            def finish(t, b):
                dve.wait_ge(down_done, t + 1)
                dve.wait_ge(stored[b], 16 * (t // 2 + 1) if isinstance(t, int) else 8 * (t - b) + 16)
                v.scalar_tensor_tensor(res[b][:, :], ps_d[:, :], down_scale[b][:, :], H[:, bass.ds(t, 1), :],
                                       ALU.mult, ALU.add).then_inc(res_done, 1)

            def turn(t, b):
                if exists(t + 1):
                    round_x(t + 1, 1 - b)
                if exists(t):
                    multiply(t, b)
                if exists(t + 2):
                    add_projection(t + 2)
                if exists(t - 1):
                    finish(t - 1, 1 - b)

            add_projection(0)
            round_x(0, 0)
            add_projection(1)
            all_turns(dve, turn)


def build(nc, args, out):
    with ExitStack() as stack:
        H = stack.enter_context(nc.sbuf_tensor("H", [P, NT, D], F32))
        xs = nc.dram_tensor("xs_dram", (ROUTED * MT, D), F32).ap()
        ys = nc.dram_tensor("ys_dram", (ROUTED * MT, D), F32).ap()
        vcls = nc.dram_tensor("vcls_dram", (NB, D), F32).ap()
        with nc.cleanup_on_exit():
            tokenizer(nc, H, args)
            recurrence(nc, H, xs, args)
        with nc.cleanup_on_exit(), ExitStack() as moe:
            place = [moe.enter_context(nc.sbuf_tensor(f"place{k}", [P, NT, 1], U32)) for k in range(2)]
            share = [moe.enter_context(nc.sbuf_tensor(f"share{k}", [P, NT], F32)) for k in range(2)]
            whose = moe.enter_context(nc.sbuf_tensor("whose", [1, ROUTED], I32))
            xn = moe.enter_context(nc.sbuf_tensor("xn", [P, NT, D], F32))
            shared_w = moe.enter_context(nc.sbuf_tensor("shared_w", [P, EXPERT_COLS], F32))
            route(nc, H, xn, place, share, whose, shared_w, args)
            experts(nc, H, xn, xs, ys, place, share, whose, shared_w, args)
        with ExitStack() as att:
            qkv = att.enter_context(nc.sbuf_tensor("qkv", [P, NT, 3 * D], F32))
            class_keys = att.enter_context(nc.sbuf_tensor("class_keys", [P, AH // 4, 4, NB], F32))
            queries_keys_values(nc, H, qkv, class_keys, vcls, args)
            attention(nc, qkv, class_keys, vcls, args)
            bitlinear_ffn(nc, H, qkv, args, out)


def expert_rows(np, a):
    def up(w, sw):
        w = np.concatenate([w, sw[None]])
        return w.reshape(E + 1, 2, P, I, 2).transpose(0, 2, 1, 4, 3)

    def bias(b, sb):
        b = np.concatenate([b, sb[None]])
        return b.reshape(E + 1, I // P, P, 2).transpose(0, 2, 1, 3)

    w13 = np.stack([up(a["L0_ffn_w1"], a["L0_ffn_sw1"]), up(a["L0_ffn_w3"], a["L0_ffn_sw3"])], axis=3)
    w2 = np.concatenate([a["L0_ffn_w2"], a["L0_ffn_sw2"][None]]).reshape(E + 1, I // P, P, D).transpose(0, 2, 1, 3)
    b13 = np.stack([bias(a["L0_ffn_b1"], a["L0_ffn_sb1"]), bias(a["L0_ffn_b3"], a["L0_ffn_sb3"])], axis=3)
    return np.concatenate([w13.reshape(E + 1, P, -1), w2.reshape(E + 1, P, -1), b13.reshape(E + 1, P, -1)], axis=2)


def kernel(**inputs):
    import numpy as np
    import concourse.bacc as bacc
    from concourse.bass_utils import run_bass_kernel_spmd

    a = {k: np.asarray(v) for k, v in inputs.items()}
    x = a["x"]
    angle = np.outer(np.arange(1, L + 1, dtype=np.float32),
                     1.0 / 10000.0 ** (np.arange(0, DH, 2, dtype=np.float32) / DH)).astype(np.float32)
    laid = {
        "tok_x": np.concatenate([x.transpose(0, 1, 3, 2).reshape(NB, C, HT * L),
                                 np.ones((NB, 1, HT * L), np.float32)], axis=1),
        "tok_xr": x.transpose(0, 2, 3, 1).reshape(NB, L, D),
        "tok_wqkv": np.concatenate([
            np.concatenate([a[f"L0_tok_W{c}_w"].T for c in "qkv"], axis=1),
            np.concatenate([a[f"L0_tok_W{c}_b"] for c in "qkv"])[None]], axis=0),
        "tok_wbT": a["L0_tok_w_bias"].T,
        "tok_maskT": a["L0_tok_local_mask"].T,
        "L0_tok_out_w": a["L0_tok_out_w"], "L0_tok_out_b": a["L0_tok_out_b"],
        "L0_tok_ln_g": a["L0_tok_ln_g"], "L0_tok_ln_b": a["L0_tok_ln_b"],
        "cls_row": a["cls_tok"].reshape(D),
        "att_w": np.concatenate([a[f"L1_attn_W_{c}"].T for c in "QKV"], axis=1),
        "att_wo": a["L1_attn_W_O"].T,
        "ffn_gu": np.concatenate([a["L1_ffn_w_gate"].T, a["L1_ffn_w_up"].T], axis=1),
        "ffn_down": a["L1_ffn_w_down"].T,
        "rope_cos": np.concatenate([np.cos(angle), np.cos(angle)], axis=1),
        "rope_sin": np.concatenate([-np.sin(angle), np.sin(angle)], axis=1),
        "gate_wT": a["L0_ffn_gate_w"].T, "gate_b": a["L0_ffn_gate_b"],
        "experts": expert_rows(np, a), "experts_b2": np.concatenate([a["L0_ffn_b2"], a["L0_ffn_sb2"][None]]),
        "earlier": np.triu(np.ones((P, P), np.float32), 1),
        "first_wins": np.arange(E, 0, -1, dtype=np.float32),
        "is_token": np.concatenate([np.ones((P, CLS), np.float32), (np.arange(P)[:, None] < NB).astype(np.float32),
                                    np.zeros((P, 1), np.float32)], axis=1),
        "tile_no": np.arange(ROUTED, dtype=np.float32),
        "rec_w": np.concatenate([a[f"L0_attn_W_{c}"].T for c in "kvq"], axis=1),
    }
    nc = bacc.Bacc("TRN2", target_bir_lowering=False, num_devices=1)
    arrays, args = {}, {}
    for name, v in laid.items():
        arrays[name + "_dram"] = np.ascontiguousarray(v)
        args[name] = nc.dram_tensor(name + "_dram", v.shape, mybir.dt.from_np(v.dtype), kind="ExternalInput").ap()
    out = nc.dram_tensor("out_dram", (NB, L + 1, D), F32, kind="ExternalOutput").ap()
    build(nc, args, out)
    r = run_bass_kernel_spmd(nc, [arrays], core_ids=[0])
    return r.results[0]["out_dram"]
```

```python
from contextlib import ExitStack

import concourse.bass as bass
from concourse import mybir

P = 128
D = 256
NB = 16
L = 256
C = 64
HT = 4
NT = 2 * NB + 2
CLS = 2 * NB
EPS = 1e-5
E = 8
I = 512
MT = 256
ROUTED = 2 * NB * (L + 1) // MT + E
EXPERT_COLS = 2 * 2 * 2 * I + I // P * D + I // P * 4
AH = 16
DH = D // AH
MAGIC = 1.5 * 2 ** 23

F32 = mybir.dt.float32
BF16 = mybir.dt.bfloat16
I32 = mybir.dt.int32
U8 = mybir.dt.uint8
U32 = mybir.dt.uint32
F32R = mybir.dt.float32r
ALU = mybir.AluOpType
ACT = mybir.ActivationFunctionType
AX = mybir.AxisListType


class Steps:

    def __init__(self, engine, sem, per):
        self.engine, self.sem, self.per, self.base, self.k = engine, sem, per, 0, 0

    def round(self, n):
        assert self.k in (0, self.per), (self.k, self.per)
        self.base, self.k = n * self.per, 0

    def then_wait(self, instruction, passed=None):
        instruction.then_inc(self.sem, 1)
        self.k += 1
        value = self.base + self.k
        if passed:
            if not isinstance(value, int):
                value = self.engine.to_reg(value)
            self.engine.wait_ge(*passed)
        self.engine.wait_ge(self.sem, value)


class Memory:

    def __init__(self, nc, stack, prefix):
        self.nc, self.stack, self.prefix = nc, stack, prefix

    def sb(self, name, shape, dt=F32):
        return self.stack.enter_context(self.nc.sbuf_tensor(self.prefix + name, shape, dt))

    def ps(self, name, shape, dt=F32):
        return self.stack.enter_context(self.nc.psum_tensor(self.prefix + name, shape, dt))

    def sem(self, name):
        return self.nc.alloc_semaphore(self.prefix + name)


def over(ap, axis, count):
    a = ap.unsqueeze(axis)
    shape = list(a.shape)
    shape[axis] = count
    return a.broadcast_to(shape)


def tokenizer(nc, H, args):
    with ExitStack() as stack:
        m = Memory(nc, stack, "tok_")
        wqkv = m.sb("wqkv", [C + 1, 3 * C])
        ew = m.sb("ew", [P, 2, L])
        mask8 = m.sb("mask8", [P, 2, L], U8)
        maskf = m.sb("maskf", [P, 2, L])
        outw = m.sb("outw", [P, 2, D])
        outb = m.sb("outb", [P, D])
        gain = m.sb("gain", [P, D])
        shift = m.sb("shift", [P, D])
        ident = m.sb("ident", [P, P])
        xa = [m.sb(f"xa{b}", [C + 1, HT, L]) for b in range(2)]
        xr = [m.sb(f"xr{b}", [P, 2, D]) for b in range(2)]
        mix = m.sb("mix", [P, 2, 2, D])
        eq = [m.sb(f"eq{b}", [P, 2, D]) for b in range(2)]
        den = m.sb("den", [P, 2, D])
        rec = m.sb("rec", [P, 2, D])
        y = [m.sb(f"y{b}", [P, 2, D]) for b in range(2)]
        yT = m.sb("yT", [P, 2, L])
        hres = m.sb("hres", [P, 2, D])
        stats = m.sb("stats", [P, 2, 6])
        mv = m.sb("mv", [P, 2, 2])
        rstd = m.sb("rstd", [P, 2])
        mhalf = m.sb("mhalf", [P, 2])
        eps = m.sb("eps", [P, 2])
        hn = [m.sb(f"hn{b}", [P, 2, D]) for b in range(2)]

        ps_qkv = m.ps("ps_qkv", [P, 2, HT, 256])
        ps_nd = m.ps("ps_nd", [P, 2, 2, D])
        ps_yT = m.ps("ps_yT", [P, 2, L])
        ps_h = m.ps("ps_h", [P, 2, D])

        weights_in = m.sem("weights_in")
        class_in = m.sem("class_in")
        zeroed = m.sem("zeroed")
        ident_done = m.sem("ident_done")
        mask_steps = m.sem("mask_steps")
        ew_ready = m.sem("ew_ready")
        xa_in = [m.sem(f"xa_in{b}") for b in range(2)]
        xr_in = [m.sem(f"xr_in{b}") for b in range(2)]
        qkv_done = m.sem("qkv_done")
        exps_done = m.sem("exps_done")
        mix_done = m.sem("mix_done")
        nd_done = m.sem("nd_done")
        y_done = m.sem("y_done")
        yT_done = m.sem("yT_done")
        yT_copied = m.sem("yT_copied")
        hproj_done = m.sem("hproj_done")
        residual_ready = m.sem("residual_ready")
        var_done = m.sem("var_done")
        rstd_done = m.sem("rstd_done")
        normed = m.sem("normed")
        h_written = m.sem("h_written")
        y_steps = m.sem("y_steps")
        norm_steps = m.sem("norm_steps")
        pool_steps = m.sem("pool_steps")

        def exists(n):
            return not isinstance(n, int) or 0 <= n < NB

        def all_turns(engine, turn):
            turn(0, 0)
            pairs = (NB - 2) // 2
            with engine.Fori(0, pairs) as i:
                turn(2 * i + 1, 1)
                turn(2 * i + 2, 0)
            turn(NB - 1, 1)
            turn(NB, 0)

        block = stack.enter_context(nc.Block())

        @block.sync
        def _(sp):
            sp.dma_start(wqkv[:, :], args["tok_wqkv"]).then_inc(weights_in, 16)
            sp.dma_start(ew[:, :, :], args["tok_wbT"].rearrange("(s p) t -> p s t", p=P)).then_inc(weights_in, 16)
            sp.dma_start(mask8[:, :, :], args["tok_maskT"].rearrange("(s p) t -> p s t", p=P)).then_inc(weights_in, 16)
            sp.dma_start(outw[:, :, :], args["L0_tok_out_w"].rearrange("(c p) n -> p c n", p=P)).then_inc(weights_in, 16)
            sp.dma_start(outb[:, :], args["L0_tok_out_b"].partition_broadcast(P)).then_inc(weights_in, 16)
            sp.dma_start(gain[:, :], args["L0_tok_ln_g"].partition_broadcast(P)).then_inc(weights_in, 16)
            sp.dma_start(shift[:, :], args["L0_tok_ln_b"].partition_broadcast(P)).then_inc(weights_in, 16)
            sp.wait_ge(zeroed, 1)
            sp.dma_start(H[0:NB, CLS, :], args["cls_row"].partition_broadcast(NB)).then_inc(class_in, 16)

            def load_channels(n, b):
                if not isinstance(n, int) or n >= 2:
                    sp.wait_ge(qkv_done, n - 1)
                sp.dma_start(xa[b][:, :, :], args["tok_x"][bass.ds(n, 1)].rearrange(
                    "o c (h l) -> (o c) h l", h=HT)).then_inc(xa_in[b], 16)

            def load_residual(n, b):
                if not isinstance(n, int) or n >= 2:
                    sp.wait_ge(normed, n - 1)
                sp.dma_start(xr[b][:, :, :], args["tok_xr"][bass.ds(n, 1)].rearrange(
                    "o (s p) d -> (o p) s d", p=P)).then_inc(xr_in[b], 16)

            load_channels(0, 0)
            load_channels(1, 1)
            load_residual(0, 0)
            load_channels(2, 0)
            load_residual(1, 1)
            with sp.Fori(1, NB // 2 - 1) as i:
                for b in range(2):
                    load_channels(2 * i + b + 1, 1 - b)
                    load_residual(2 * i + b, b)
            load_channels(NB - 1, 1)
            load_residual(NB - 2, 0)
            load_residual(NB - 1, 1)
            sp.wait_ge(class_in, 16)

        @block.gpsimd
        def _(pool):
            nc.gpsimd.memset(H[:, CLS:NT, :], 0.0).then_inc(zeroed, 1)
            nc.gpsimd.memset(mhalf[:, :], -0.5).then_inc(pool_steps, 1)
            nc.gpsimd.memset(eps[:, :], EPS).then_inc(pool_steps, 1)
            nc.gpsimd.memset(ident[:, :], 0.0).then_inc(pool_steps, 1)
            pool.wait_ge(pool_steps, 3)
            nc.gpsimd.affine_select(out=ident[:, :], in_=ident[:, :], compare_op=ALU.not_equal, fill=1.0,
                                    base=0, pattern=[[-1, P]], channel_multiplier=1).then_inc(ident_done, 1)
            pool.wait_ge(weights_in, 7 * 16)
            pool.sem_inc(h_written, 2)
            steps = Steps(pool, m.sem("pool_ln"), 2)
            with pool.Fori(0, NB // 2) as i:
                for b in range(2):
                    n = 2 * i + b
                    pool.wait_ge(xr_in[b], 16 * i + 16)
                    nc.gpsimd.tensor_tensor(xr[b][:, :, :], xr[b][:, :, :], over(outb[:, :], 1, 2), ALU.add)\
                        .then_inc(residual_ready, 1)
                    steps.round(n)
                    pool.wait_ge(var_done, n + 1)
                    steps.then_wait(nc.gpsimd.tensor_tensor(rstd[:, :], mv[:, :, 1], eps[:, :], ALU.add))
                    nc.gpsimd.tensor_tensor(rstd[:, :], rstd[:, :], mhalf[:, :], ALU.pow).then_inc(rstd_done, 1)
                    pool.wait_ge(normed, n + 1)
                    steps.then_wait(nc.gpsimd.tensor_tensor(
                        hn[b][:, :, :], hn[b][:, :, :], over(gain[:, :], 1, 2), ALU.mult))
                    nc.gpsimd.tensor_tensor(H[:, bass.ds(2 * n, 2), :], hn[b][:, :, :],
                                            over(shift[:, :], 1, 2), ALU.add).then_inc(h_written, 1)

        @block.tensor
        def _(pe):
            pe.wait_ge(weights_in, 7 * 16)

            def project(n, b):
                pe.wait_ge(xa_in[b], 8 * (n - b) + 16)
                if not isinstance(n, int) or n > 0:
                    pe.wait_ge(exps_done, n)
                    pe.wait_ge(mix_done, n)
                for s in range(2):
                    for h in range(HT):
                        last = nc.tensor.matmul(ps_qkv[:, s, h, 0:3 * C], xa[b][:, h, s * P:(s + 1) * P],
                                                wqkv[:, :], start=True, stop=True)
                last.then_inc(qkv_done, 1)

            def mixed(n):
                pe.wait_ge(mix_done, n + 1)
                if not isinstance(n, int) or n > 0:
                    pe.wait_ge(y_done, n)
                for t in range(2):
                    for s in range(2):
                        last = nc.tensor.matmul(ps_nd[:, t, :, :], ew[:, s, t * P:(t + 1) * P],
                                                mix[:, s, :, :], start=s == 0, stop=s == 1)
                last.then_inc(nd_done, 1)

            def turn_y(n, b):
                pe.wait_ge(y_done, n + 1)
                for c in range(2):
                    for s in range(2):
                        last = nc.tensor.transpose(ps_yT[:, c, s * P:(s + 1) * P],
                                                   y[b][:, s, c * P:(c + 1) * P], ident[:, :])
                last.then_inc(yT_done, 1)

            def put_out(n):
                pe.wait_ge(yT_copied, n + 1)
                if not isinstance(n, int) or n > 0:
                    pe.wait_ge(var_done, n)
                for s in range(2):
                    for c in range(2):
                        last = nc.tensor.matmul(ps_h[:, s, :], yT[:, c, s * P:(s + 1) * P], outw[:, c, :],
                                                start=c == 0, stop=c == 1)
                last.then_inc(hproj_done, 1)

            def turn(n, b):
                if exists(n):
                    mixed(n)
                if exists(n - 1):
                    turn_y(n - 1, 1 - b)
                if exists(n + 1):
                    project(n + 1, 1 - b)
                if exists(n - 1):
                    put_out(n - 1)

            project(0, 0)
            pe.wait_ge(ew_ready, 1)
            pe.wait_ge(ident_done, 1)
            all_turns(pe, turn)

        @block.scalar
        def _(act):
            act.wait_ge(mask_steps, 2)
            nc.scalar.activation(ew[:, :, :], ew[:, :, :], ACT.Exp).then_inc(ew_ready, 1)

            def exps(n, b):
                act.wait_ge(qkv_done, n + 1)
                if not isinstance(n, int) or n > 0:
                    act.wait_ge(nd_done, n)
                for s in range(2):
                    nc.scalar.activation(mix[:, s, 1, :].rearrange("p (h c) -> p h c", h=HT),
                                         ps_qkv[:, s, :, C:2 * C], ACT.Exp)
                    last = nc.scalar.activation(eq[b][:, s, :].rearrange("p (h c) -> p h c", h=HT),
                                                ps_qkv[:, s, :, 0:C], ACT.Exp, scale=-1.0)
                last.then_inc(exps_done, 1)

            def copy(n):
                act.wait_ge(yT_done, n + 1)
                nc.scalar.activation(yT[:, :, :], ps_yT[:, :, :], ACT.Copy).then_inc(yT_copied, 1)

            def turn(n, b):
                if exists(n - 1):
                    copy(n - 1)
                if exists(n + 1):
                    exps(n + 1, 1 - b)

            exps(0, 0)
            all_turns(act, turn)

        @block.vector
        def _(dve):
            dve.wait_ge(weights_in, 7 * 16)
            nc.vector.tensor_copy(maskf[:, :, :], mask8[:, :, :]).then_inc(mask_steps, 1)
            dve.wait_ge(mask_steps, 1)
            nc.vector.tensor_tensor(ew[:, :, :], ew[:, :, :], maskf[:, :, :], ALU.mult).then_inc(mask_steps, 1)
            y_chain = Steps(dve, y_steps, 2)
            norm_chain = Steps(dve, norm_steps, 2)

            def weigh(n):
                dve.wait_ge(exps_done, n + 1)
                for s in range(2):
                    last = nc.vector.tensor_tensor(
                        mix[:, s, 0, :].rearrange("p (h c) -> p h c", h=HT), ps_qkv[:, s, :, 2 * C:3 * C],
                        mix[:, s, 1, :].rearrange("p (h c) -> p h c", h=HT), ALU.mult)
                last.then_inc(mix_done, 1)

            def gate(n, b):
                y_chain.round(n)
                dve.wait_ge(nd_done, n + 1)
                y_chain.then_wait(nc.vector.scalar_tensor_tensor(
                    den[:, :, :], eq[b][:, :, :], 1.0, ps_nd[:, :, 1, :], ALU.add, ALU.mult))
                y_chain.then_wait(nc.vector.reciprocal(rec[:, :, :], den[:, :, :]))
                nc.vector.tensor_tensor(y[b][:, :, :], ps_nd[:, :, 0, :], rec[:, :, :], ALU.mult).then_inc(y_done, 1)

            def moments(n, b):
                norm_chain.round(n)
                dve.wait_ge(hproj_done, n + 1)
                dve.wait_ge(residual_ready, n + 1)
                norm_chain.then_wait(nc.vector.tensor_tensor(hres[:, :, :], ps_h[:, :, :], xr[b][:, :, :], ALU.add))
                for s in range(2):
                    last = nc.vector.bn_stats(stats[:, s, :], hres[:, s, :])
                norm_chain.then_wait(last, (weights_in, 7 * 16))
                for s in range(2):
                    last = nc.vector.bn_aggr(mv[:, s, :], stats[:, s, :])
                last.then_inc(var_done, 1)

            def norm(n, b):
                dve.wait_ge(rstd_done, n + 1)
                dve.wait_ge(h_written, n + 1)
                for s in range(2):
                    last = nc.vector.tensor_scalar(hn[b][:, s, :], hres[:, s, :], mv[:, s, 0:1], rstd[:, s:s + 1],
                                                   ALU.subtract, ALU.mult)
                last.then_inc(normed, 1)

            def turn(n, b):
                if exists(n):
                    gate(n, b)
                if exists(n + 1):
                    weigh(n + 1)
                if exists(n - 1):
                    moments(n - 1, 1 - b)
                    norm(n - 1, 1 - b)

            weigh(0)
            all_turns(dve, turn)


def recurrence(nc, H, xs, args):
    NBLK, BW = 32, 8
    U = 2 * NBLK + 1
    GROUPS = [(0, 33), (33, U)]
    HALF_COLS = 512
    with ExitStack() as stack:
        m = Memory(nc, stack, "rec_")
        w = m.sb("w", [P, 2, 3 * D])
        ident = m.sb("ident", [P, P])
        mhalf = m.sb("mhalf", [P, 2])
        eps = m.sb("eps", [P, 2])
        half = m.sb("half", [P, U])
        stats = m.sb("stats", [P, 2, 6])
        mv = m.sb("mv", [P, 2, 2])
        rstd = m.sb("rstd", [P, 2])
        xn = m.sb("xn", [P, 2, D])
        xT = m.sb("xT", [P, 2, 2 * P])
        kvq = [m.sb(f"kvq{b}", [P, 3, U, BW]) for b in range(2)]
        kn = [m.sb(f"kn{b}", [P, U, BW]) for b in range(2)]
        ksq = m.sb("ksq", [P, U, BW])
        ss = m.sb("ss", [P, U])
        nrm = m.sb("nrm", [P, U])
        rn = m.sb("rn", [P, U])
        row = m.sb("row", [1, 3 * D])
        S = m.sb("S", [P, U, BW, BW])
        T = m.sb("T", [P, U, BW, BW])
        Tq = m.sb("Tq", [P, U, BW, BW])
        delta = m.sb("delta", [P, U, BW])
        sq = [m.sb(f"sq{b}", [P, U, BW]) for b in range(2)]
        th = [m.sb(f"th{b}", [P, U, BW]) for b in range(2)]
        sqh = [m.sb(f"sqh{b}", [P, U, BW]) for b in range(2)]
        o = m.sb("o", [P, U, BW])
        ocls = m.sb("ocls", [NBLK, NB, BW])
        ocls_rows = m.sb("ocls_rows", [NB, D])
        zero_rows = m.sb("zero_rows", [P, 8 * D])
        row_dram = nc.dram_tensor("rec_row_dram", (3 * D,), F32).ap()
        ocls_dram = nc.dram_tensor("rec_ocls_dram", (NB, D), F32).ap()

        ps_xT = m.ps("ps_xT", [P, 2, 2 * P])
        ps_kvq = m.ps("ps_kvq", [P, 2, 3, D])
        ps_sk = [m.ps(f"ps_sk{g}", [P, HALF_COLS]) for g in range(2)]
        ps_sq = [m.ps(f"ps_sq{g}", [P, HALF_COLS]) for g in range(2)]

        weights_in = m.sem("weights_in")
        zero_ready = m.sem("zero_ready")
        xs_zeroed = m.sem("xs_zeroed")
        consts = m.sem("consts")
        ident_done = m.sem("ident_done")
        row_copied = m.sem("row_copied")
        row_out = m.sem("row_out")
        row_in = m.sem("row_in")
        state_zero = m.sem("state_zero")
        var_done = m.sem("var_done")
        rstd_done = m.sem("rstd_done")
        xn_done = m.sem("xn_done")
        xT_done = m.sem("xT_done")
        xT_copied = m.sem("xT_copied")
        kvq_done = m.sem("kvq_done")
        kvq_copied = m.sem("kvq_copied")
        ss_done = m.sem("ss_done")
        nrm_done = m.sem("nrm_done")
        pre_done = [m.sem(f"pre_done{g}") for g in range(2)]
        tanh_done = [m.sem(f"tanh_done{g}") for g in range(2)]
        k_product = [m.sem(f"k_product{g}") for g in range(2)]
        q_product = [m.sem(f"q_product{g}") for g in range(2)]
        sk_done = [m.sem(f"sk_done{g}") for g in range(2)]
        sq_done = [m.sem(f"sq_done{g}") for g in range(2)]
        gate_done = [m.sem(f"gate_done{g}") for g in range(2)]
        out_done = m.sem("out_done")
        ocls_out = m.sem("ocls_out")
        ocls_in = m.sem("ocls_in")

        def exists(n, last=NB - 1):
            return not isinstance(n, int) or 0 <= n <= last

        def all_turns(engine, turn):
            turn(0, 0)
            pairs = (NB - 4) // 2
            with engine.Fori(0, pairs) as i:
                turn(2 * i + 1, 1)
                turn(2 * i + 2, 0)
            for n in range(2 * pairs + 1, NB + 1):
                turn(n, n % 2)

        block = stack.enter_context(nc.Block())

        @block.sync
        def _(sp):
            sp.dma_start(w[:, :, :], args["rec_w"].rearrange("(c p) n -> p c n", p=P)).then_inc(weights_in, 16)
            sp.wait_ge(row_copied, 1)
            sp.dma_start(row_dram.unsqueeze(0), row[:, :]).then_inc(row_out, 16)
            sp.wait_ge(row_out, 16)
            sp.wait_ge(consts, 6)
            for b in range(2):
                sp.dma_start(kvq[b][0:NBLK, :, U - 1, :],
                             row_dram.rearrange("(c b j) -> b c j", c=3, j=BW)).then_inc(row_in, 16)
            sp.wait_ge(zero_ready, 1)
            xs_v = xs[0:ROUTED * MT, :].rearrange("(p g r) d -> g p (r d)", p=P, r=8)
            chunks = ROUTED * MT // P // 8
            with sp.Fori(0, chunks) as g:
                sp.dma_start(xs_v[bass.ds(g, 1)].rearrange("o p d -> (o p) d"), zero_rows[:, :])\
                    .then_inc(xs_zeroed, 16)
            sp.wait_ge(out_done, NB + 2)
            sp.dma_start(ocls_dram.rearrange("n (b j) -> b n j", j=BW), ocls[:, :, :]).then_inc(ocls_out, 16)
            sp.wait_ge(ocls_out, 16)
            sp.dma_start(ocls_rows[:, :], ocls_dram).then_inc(ocls_in, 16)
            sp.wait_ge(ocls_in, 16)
            sp.wait_ge(xs_zeroed, 16 * chunks)

        @block.gpsimd
        def _(pool):
            pool.sem_inc(out_done, 2)
            nc.gpsimd.memset(mhalf[:, :], -0.5).then_inc(consts, 1)
            nc.gpsimd.memset(eps[:, :], EPS).then_inc(consts, 1)
            nc.gpsimd.memset(half[:, :], 0.5).then_inc(consts, 1)
            nc.gpsimd.memset(ident[:, :], 0.0).then_inc(consts, 1)
            for b in range(2):
                nc.gpsimd.memset(kvq[b][:, :, U - 1, :], 0.0).then_inc(consts, 1)
            pool.wait_ge(consts, 6)
            nc.gpsimd.affine_select(out=ident[:, :], in_=ident[:, :], compare_op=ALU.not_equal, fill=1.0,
                                    base=0, pattern=[[-1, P]], channel_multiplier=1).then_inc(ident_done, 1)
            nc.gpsimd.memset(zero_rows[:, :], 0.0).then_inc(zero_ready, 1)
            rstd_steps = Steps(pool, m.sem("pool_rstd"), 1)
            out_steps = Steps(pool, m.sem("pool_out"), 4)

            def root(k):
                rstd_steps.round(k)
                pool.wait_ge(var_done, k + 1)
                rstd_steps.then_wait(nc.gpsimd.tensor_tensor(rstd[:, :], mv[:, :, 1], eps[:, :], ALU.add))
                nc.gpsimd.tensor_tensor(rstd[:, :], rstd[:, :], mhalf[:, :], ALU.pow).then_inc(rstd_done, 1)

            def norm(n):
                pool.wait_ge(ss_done, n + 1)
                nc.gpsimd.tensor_tensor(nrm[:, :], ss[:, :], half[:, :], ALU.pow).then_inc(nrm_done, 1)

            def gate(n, b):
                out_steps.round(n)
                for g in range(2):
                    pool.wait_ge(gate_done[g], n + 1)
                out_steps.then_wait(nc.gpsimd.tensor_tensor(o[:, :, :], th[b][:, :, :], sqh[b][:, :, :], ALU.mult))
                out_steps.then_wait(nc.gpsimd.tensor_tensor(o[:, :, :], o[:, :, :], sqh[b][:, :, :], ALU.add))
                out_steps.then_wait(nc.gpsimd.tensor_tensor(o[:, :, :], o[:, :, :], sq[b][:, :, :], ALU.mult))
                tiles = H[:, bass.ds(2 * n, 2), :]
                out_steps.then_wait(nc.gpsimd.tensor_tensor(
                    tiles, tiles, o[:, 0:U - 1, :].rearrange("p (s u) j -> p s (u j)", s=2), ALU.add))
                nc.gpsimd.tensor_copy(ocls[:, bass.ds(n, 1), :], o[0:NBLK, U - 1:U, :]).then_inc(out_done, 1)
                pool.wait_ge(out_done, n + 3)

            def turn(n, b):
                if exists(n + 3, NB):
                    root(n + 3)
                if exists(n + 1):
                    norm(n + 1)
                if exists(n - 1):
                    gate(n - 1, 1 - b)

            root(0)
            root(1)
            root(2)
            norm(0)
            all_turns(pool, turn)
            pool.wait_ge(ocls_in, 16)
            nc.gpsimd.tensor_tensor(H[0:NB, CLS, :], H[0:NB, CLS, :], ocls_rows[:, :], ALU.add)

        @block.tensor
        def _(pe):
            pe.wait_ge(ident_done, 1)
            pe.wait_ge(weights_in, 16)

            def turn_x(k):
                pe.wait_ge(xn_done, k + 1)
                for c in range(2):
                    for t in range(2):
                        last = nc.tensor.transpose(ps_xT[:, c, t * P:(t + 1) * P],
                                                   xn[:, t, c * P:(c + 1) * P], ident[:, :])
                last.then_inc(xT_done, 1)

            def project(k, t):
                if t == 0:
                    pe.wait_ge(xT_copied, k + 1)
                    if exists(k - 1):
                        pe.wait_ge(kvq_copied, k)
                for j in range(3):
                    for c in range(2):
                        last = nc.tensor.matmul(ps_kvq[:, t, j, :], xT[:, c, t * P:(t + 1) * P],
                                                w[:, c, j * D:(j + 1) * D], start=c == 0, stop=c == 1)
                if t == 1:
                    last.then_inc(kvq_done, 1)

            def add_up(out, product, g, done):
                lo, hi = GROUPS[g]
                for j in range(BW):
                    last = nc.tensor.matmul(out[:, 0:(hi - lo) * BW], ident[:, :], product[:, lo:hi, :, j],
                                            start=j == 0, stop=j == BW - 1)
                last.then_inc(done, 1)

            def sum_sq(n, g):
                pe.wait_ge(q_product[g], n + 1)
                if not isinstance(n, int) or n > 0:
                    pe.wait_ge(gate_done[g], n)
                add_up(ps_sq[g], Tq, g, sq_done[g])

            def turn(n, b):
                for g in range(2):
                    if exists(n):
                        pe.wait_ge(k_product[g], n + 1)
                        add_up(ps_sk[g], T, g, sk_done[g])
                if exists(n + 3, NB):
                    turn_x(n + 3)
                if exists(n - 1):
                    sum_sq(n - 1, 0)
                if exists(n + 3, NB):
                    project(n + 3, 0)
                if exists(n - 1):
                    sum_sq(n - 1, 1)
                if exists(n + 3, NB):
                    project(n + 3, 1)

            for k in range(3):
                turn_x(k)
                project(k, 0)
                project(k, 1)
            all_turns(pe, turn)

        @block.scalar
        def _(act):
            def copy_xT(k):
                act.wait_ge(xT_done, k + 1)
                nc.scalar.activation(xT[:, :, :], ps_xT[:, :, :], ACT.Copy).then_inc(xT_copied, 1)

            def copy_kvq(k, b):
                act.wait_ge(kvq_done, k + 1)
                for s in range(2):
                    nc.scalar.activation(
                        ksq[:, s * NBLK:(s + 1) * NBLK, :].rearrange("p u j -> p (u j)"), ps_kvq[:, s, 0, :],
                        ACT.Square)
                for s in range(2):
                    last = nc.scalar.activation(
                        kvq[b][:, :, s * NBLK:(s + 1) * NBLK, :].rearrange("p c u j -> p c (u j)"),
                        ps_kvq[:, s, :, :], ACT.Copy)
                last.then_inc(kvq_copied, 1)

            def squash(n, g):
                lo, hi = GROUPS[g]
                act.wait_ge(pre_done[g], n + 1)
                nc.scalar.activation(S[:, lo:hi], S[:, lo:hi], ACT.Tanh).then_inc(tanh_done[g], 1)

            def read_out(n, b, g):
                lo, hi = GROUPS[g]
                sums = ps_sq[g][:, 0:(hi - lo) * BW].rearrange("p (u j) -> p u j", j=BW)
                act.wait_ge(sq_done[g], n + 1)
                act.wait_ge(out_done, n + 1)
                nc.scalar.activation(th[b][:, lo:hi], sums, ACT.Tanh, scale=0.5)
                nc.scalar.activation(sqh[b][:, lo:hi], sums, ACT.Copy, scale=0.5)
                nc.scalar.activation(sq[b][:, lo:hi], sums, ACT.Copy).then_inc(gate_done[g], 1)

            def turn(n, b):
                if exists(n + 1):
                    if not isinstance(n, int) or n > 0:
                        act.wait_ge(q_product[1], n)
                    else:
                        act.wait_ge(ss_done, 1)
                    copy_kvq(n + 2, 1 - b)
                if exists(n + 3, NB):
                    copy_xT(n + 3)
                for g in range(2):
                    if exists(n):
                        squash(n, g)
                for g in range(2):
                    if exists(n - 1):
                        read_out(n - 1, 1 - b, g)

            copy_xT(0)
            act.wait_ge(kvq_done, 1)
            nc.scalar.activation(row[:, :].rearrange("p (c d) -> p c d", c=3), ps_kvq[0:1, 0, :, :],
                                 ACT.Copy).then_inc(row_copied, 1)
            act.wait_ge(row_copied, 1)
            act.sem_inc(kvq_copied, 1)
            copy_xT(1)
            copy_kvq(1, 0)
            copy_xT(2)
            all_turns(act, turn)

        @block.vector
        def _(dve):
            stat_steps = Steps(dve, m.sem("dve_stat"), 1)
            cls_squared = m.sem("dve_cls_squared")
            kn_steps = Steps(dve, m.sem("dve_kn"), 3)
            change_steps = [Steps(dve, m.sem(f"dve_change{g}"), 2) for g in range(2)]

            def moments(k, tiles):
                stat_steps.round(k)
                for s in range(2):
                    last = nc.vector.bn_stats(stats[:, s, :], tiles(s))
                stat_steps.then_wait(last, (state_zero, 1))
                for s in range(2):
                    last = nc.vector.bn_aggr(mv[:, s, :], stats[:, s, :])
                last.then_inc(var_done, 1)

            def normalise(k, tiles):
                if not isinstance(k, int) or k > 0:
                    dve.wait_ge(xT_done, k)
                dve.wait_ge(rstd_done, k + 1)
                for s in range(2):
                    last = nc.vector.tensor_scalar(xn[:, s, :], tiles(s), mv[:, s, 0:1], rstd[:, s:s + 1],
                                                   ALU.subtract, ALU.mult)
                last.then_inc(xn_done, 1)

            def sums(n, b):
                dve.wait_ge(kvq_copied, n + 2)
                nc.vector.tensor_reduce(ss[:, :], ksq[:, :, :], axis=AX.X, op=ALU.add).then_inc(ss_done, 1)

            def unit(n, b):
                kn_steps.round(n)
                dve.wait_ge(nrm_done, n + 1)
                kn_steps.then_wait(nc.vector.tensor_scalar(nrm[:, :], nrm[:, :], 1e-6, None, ALU.add))
                kn_steps.then_wait(nc.vector.reciprocal(rn[:, :], nrm[:, :]))
                kn_steps.then_wait(nc.vector.tensor_tensor(kn[b][:, :, :], kvq[b][:, 0], over(rn[:, :], 2, BW),
                                                           ALU.mult))

            def multiply_k(n, b, g):
                lo, hi = GROUPS[g]
                nc.vector.tensor_tensor(T[:, lo:hi], S[:, lo:hi], over(kn[b][:, lo:hi], 2, BW), ALU.mult)\
                    .then_inc(k_product[g], 1)

            def change(n, b, g):
                lo, hi = GROUPS[g]
                steps = change_steps[g]
                steps.round(n)
                s, t = S[:, lo:hi], T[:, lo:hi]
                dve.wait_ge(sk_done[g], n + 1)
                sk = ps_sk[g][:, 0:(hi - lo) * BW].rearrange("p (u j) -> p u j", j=BW)
                steps.then_wait(nc.vector.tensor_tensor(delta[:, lo:hi], kvq[b][:, 1, lo:hi], sk, ALU.subtract))
                steps.then_wait(nc.vector.tensor_tensor(t, over(delta[:, lo:hi], 3, BW), over(kn[b][:, lo:hi], 2, BW),
                                                        ALU.mult))
                nc.vector.tensor_tensor(s, s, t, ALU.add).then_inc(pre_done[g], 1)

            def multiply_q(n, b, g):
                lo, hi = GROUPS[g]
                dve.wait_ge(tanh_done[g], n + 1)
                if not isinstance(n, int) or n > 0:
                    dve.wait_ge(sq_done[g], n)
                nc.vector.tensor_tensor(Tq[:, lo:hi], S[:, lo:hi], over(kvq[b][:, 2, lo:hi], 2, BW), ALU.mult)\
                    .then_inc(q_product[g], 1)

            def tiles_of(k):
                if isinstance(k, int) and k == 0:
                    return lambda s: H[:, CLS + s, :]
                return lambda s: H[:, bass.ds(2 * k - 2 + s, 1), :]

            def turn(n, b):
                if exists(n):
                    multiply_k(n, b, 0)
                if exists(n + 3, NB):
                    moments(n + 3, tiles_of(n + 3))
                if exists(n - 1):
                    multiply_q(n - 1, 1 - b, 1)
                if exists(n):
                    multiply_k(n, b, 1)
                if exists(n + 1):
                    sums(n + 1, 1 - b)
                if exists(n + 3, NB):
                    normalise(n + 3, tiles_of(n + 3))
                if exists(n):
                    change(n, b, 0)
                    change(n, b, 1)
                    multiply_q(n, b, 0)
                if exists(n + 1):
                    unit(n + 1, 1 - b)

            nc.vector.memset(S[:, :, :, :], 0.0).then_inc(state_zero, 1)
            dve.wait_ge(consts, 3)
            for k in range(3):
                moments(k, tiles_of(k))
                normalise(k, tiles_of(k))
            dve.wait_ge(row_in, 32)
            k = kvq[0][:, 0, U - 1]
            nc.vector.tensor_tensor(ksq[:, U - 1], k, k, ALU.mult).then_inc(cls_squared, 1)
            dve.wait_ge(cls_squared, 1)
            sums(0, 0)
            unit(0, 0)
            all_turns(dve, turn)


def route(nc, H, xn, place, share, whose, shared_w, args):
    with ExitStack() as stack:
        m = Memory(nc, stack, "rt_")
        ident = m.sb("ident", [P, P])
        mhalf = m.sb("mhalf", [P, 2])
        eps = m.sb("eps", [P, 2])
        ones = m.sb("ones", [P, P])
        earlier = m.sb("earlier", [P, P])
        gw = m.sb("gw", [P, 2, E])
        gb = m.sb("gb", [P, E])
        first_wins = m.sb("first_wins", [P, E])
        is_token = m.sb("is_token", [P, NT])
        tile_no = m.sb("tile_no", [P, ROUTED])
        xp = [m.sb(f"xp{b}", [P, 2, D]) for b in range(2)]
        xT = [m.sb(f"xT{b}", [P, 2, 2 * P]) for b in range(2)]
        stats = m.sb("stats", [P, 2, 6])
        mv = m.sb("mv", [P, 2, 2])
        rstd = m.sb("rstd", [P, 2])
        logits = m.sb("logits", [P, NT, E])
        top = m.sb("top", [P, NT])
        scores = m.sb("scores", [P, NT, E])
        biased = m.sb("biased", [P, NT, E])
        tied = m.sb("tied", [P, NT, E])
        chosen = [m.sb(f"chosen{k}", [P, NT, E]) for k in range(2)]
        taken = m.sb("taken", [P, NT, E])
        upto = m.sb("upto", [P, E, NT])
        one_row = m.sb("one_row", [P, NT])
        tiles_of = m.sb("tiles_of", [P, E])
        ends = m.sb("ends", [P, E])
        start = m.sb("start", [P, E])
        row = m.sb("row", [P, NT, E])
        tmp = m.sb("tmp", [P, NT, E])
        ended = m.sb("ended", [P, ROUTED, E])
        owner = m.sb("owner", [P, ROUTED])
        placef = m.sb("placef", [P, NT])

        ps_xT = m.ps("ps_xT", [P, 2, 2 * P])
        ps_lg = m.ps("ps_lg", [P, 2, E])
        ps_rank = m.ps("ps_rank", [P, NT, E])
        ps_total = m.ps("ps_total", [P, NT, E])

        consts_in = m.sem("consts_in")
        consts = m.sem("consts")
        ident_done = m.sem("ident_done")
        var_done = m.sem("var_done")
        rstd_done = m.sem("rstd_done")
        xn_done = m.sem("xn_done")
        xT_done = m.sem("xT_done")
        xT_copied = m.sem("xT_copied")
        lg_done = m.sem("lg_done")
        lg_copied = m.sem("lg_copied")
        less_max = m.sem("less_max")
        exp_done = m.sem("exp_done")
        taken_done = m.sem("taken_done")
        ranks_done = m.sem("ranks_done")
        shared_w_in = m.sem("shared_w_in")
        PAIRS = NT // 2

        def exists(k):
            return not isinstance(k, int) or k < PAIRS

        def all_turns(engine, turn):
            pairs = (PAIRS - 3) // 2
            with engine.Fori(0, pairs) as i:
                turn(2 * i, 0)
                turn(2 * i + 1, 1)
            for k in range(2 * pairs, PAIRS):
                turn(k, k % 2)

        block = stack.enter_context(nc.Block())

        @block.sync
        def _(sp):
            sp.dma_start(gw[:, :, :], args["gate_wT"].rearrange("(c p) e -> p c e", p=P)).then_inc(consts_in, 16)
            sp.dma_start(gb[:, :], args["gate_b"].partition_broadcast(P)).then_inc(consts_in, 16)
            sp.dma_start(earlier[:, :], args["earlier"]).then_inc(consts_in, 16)
            sp.dma_start(first_wins[:, :], args["first_wins"].partition_broadcast(P)).then_inc(consts_in, 16)
            sp.dma_start(is_token[:, :], args["is_token"]).then_inc(consts_in, 16)
            sp.dma_start(tile_no[:, :], args["tile_no"].partition_broadcast(P)).then_inc(consts_in, 16)
            sp.dma_start(shared_w[:, :], args["experts"][E]).then_inc(shared_w_in, 16)
            sp.wait_ge(shared_w_in, 16)

        @block.gpsimd
        def _(pool):
            nc.gpsimd.memset(mhalf[:, :], -0.5).then_inc(consts, 1)
            nc.gpsimd.memset(eps[:, :], EPS).then_inc(consts, 1)
            nc.gpsimd.memset(ones[:, :], 1.0).then_inc(consts, 1)
            nc.gpsimd.memset(one_row[:, :], 1.0).then_inc(consts, 1)
            nc.gpsimd.memset(ident[:, :], 0.0).then_inc(consts, 1)
            pool.wait_ge(consts, 5)
            nc.gpsimd.affine_select(out=ident[:, :], in_=ident[:, :], compare_op=ALU.not_equal, fill=1.0,
                                    base=0, pattern=[[-1, P]], channel_multiplier=1).then_inc(ident_done, 1)
            steps = Steps(pool, m.sem("pool_rstd"), 1)
            with pool.Fori(0, PAIRS) as k:
                steps.round(k)
                pool.wait_ge(var_done, k + 1)
                steps.then_wait(nc.gpsimd.tensor_tensor(rstd[:, :], mv[:, :, 1], eps[:, :], ALU.add))
                nc.gpsimd.tensor_tensor(rstd[:, :], rstd[:, :], mhalf[:, :], ALU.pow).then_inc(rstd_done, 1)

        @block.tensor
        def _(pe):
            pe.wait_ge(ident_done, 1)
            pe.wait_ge(consts_in, 6 * 16)

            def turn_x(k, b):
                pe.wait_ge(xn_done, k + 1)
                if not isinstance(k, int) or k > 0:
                    pe.wait_ge(xT_copied, k)
                for c in range(2):
                    for s in range(2):
                        last = nc.tensor.transpose(ps_xT[:, c, s * P:(s + 1) * P],
                                                   xp[b][:, s, c * P:(c + 1) * P], ident[:, :])
                last.then_inc(xT_done, 1)

            def turn(k, b):
                if exists(k + 1):
                    turn_x(k + 1, 1 - b)
                pe.wait_ge(xT_copied, k + 1)
                pe.wait_ge(lg_copied, k + 1)
                for s in range(2):
                    for c in range(2):
                        last = nc.tensor.matmul(ps_lg[:, s, :], xT[b][:, c, s * P:(s + 1) * P], gw[:, c, :],
                                                start=c == 0, stop=c == 1)
                last.then_inc(lg_done, 1)

            turn_x(0, 0)
            all_turns(pe, turn)
            pe.wait_ge(taken_done, 1)
            nc.tensor.matmul(ps_rank[:, :, :], earlier[:, :], taken[:, :, :], start=True, stop=True)
            nc.tensor.matmul(ps_total[:, :, :], ones[:, :], taken[:, :, :], start=True, stop=True)\
                .then_inc(ranks_done, 1)

        @block.scalar
        def _(act):
            def copy_x(k, b):
                act.wait_ge(xn_done, k + 1)
                nc.scalar.activation(xn[:, bass.ds(2 * k, 2), :], xp[b][:, :, :], ACT.Copy)
                act.wait_ge(xT_done, k + 1)
                if not isinstance(k, int) or k >= 2:
                    act.wait_ge(lg_done, k - 1)
                nc.scalar.activation(xT[b][:, :, :], ps_xT[:, :, :], ACT.Copy).then_inc(xT_copied, 1)

            def turn(k, b):
                if exists(k + 1):
                    copy_x(k + 1, 1 - b)

            copy_x(0, 0)
            all_turns(act, turn)
            act.wait_ge(less_max, 1)
            nc.scalar.activation(scores[:, :, :], scores[:, :, :], ACT.Exp).then_inc(exp_done, 1)

        @block.vector
        def _(dve):
            stat_steps = Steps(dve, m.sem("dve_stat"), 1)
            dve.sem_inc(lg_copied, 1)
            dve.wait_ge(consts_in, 6 * 16)

            def moments(k):
                stat_steps.round(k)
                for s in range(2):
                    last = nc.vector.bn_stats(stats[:, s, :], H[:, bass.ds(2 * k + s, 1), :])
                stat_steps.then_wait(last, (consts_in, 6 * 16))
                for s in range(2):
                    last = nc.vector.bn_aggr(mv[:, s, :], stats[:, s, :])
                last.then_inc(var_done, 1)

            def normalise(k, b):
                dve.wait_ge(rstd_done, k + 1)
                if not isinstance(k, int) or k >= 2:
                    dve.wait_ge(xT_copied, k - 1)
                for s in range(2):
                    last = nc.vector.tensor_scalar(xp[b][:, s, :], H[:, bass.ds(2 * k + s, 1), :],
                                                   mv[:, s, 0:1], rstd[:, s:s + 1], ALU.subtract, ALU.mult)
                last.then_inc(xn_done, 1)

            def turn(k, b):
                if exists(k + 2):
                    normalise(k + 2, b)
                if exists(k + 3):
                    moments(k + 3)
                dve.wait_ge(lg_done, k + 1)
                nc.vector.tensor_copy(logits[:, bass.ds(2 * k, 2), :], ps_lg[:, :, :]).then_inc(lg_copied, 1)

            for k in range(2):
                moments(k)
                normalise(k, k)
            moments(2)
            all_turns(dve, turn)

            one = Steps(dve, m.sem("dve_route"), 100)
            dve.wait_ge(lg_copied, PAIRS + 1)
            go = one.then_wait
            v = nc.vector
            go(v.tensor_reduce(top[:, :], logits[:, :, :], axis=AX.X, op=ALU.max))
            v.tensor_tensor(scores[:, :, :], logits[:, :, :], over(top[:, :], 2, E), ALU.subtract)\
                .then_inc(less_max, 1)
            dve.wait_ge(exp_done, 1)
            go(v.tensor_reduce(top[:, :], scores[:, :, :], axis=AX.X, op=ALU.add))
            go(v.reciprocal(top[:, :], top[:, :]))
            go(v.tensor_tensor(scores[:, :, :], scores[:, :, :], over(top[:, :], 2, E), ALU.mult))
            go(v.tensor_tensor(biased[:, :, :], scores[:, :, :], over(gb[:, :], 1, NT), ALU.add))
            for k in range(2):
                go(v.tensor_reduce(top[:, :], biased[:, :, :], axis=AX.X, op=ALU.max))
                go(v.tensor_tensor(tied[:, :, :], biased[:, :, :], over(top[:, :], 2, E), ALU.is_equal))
                go(v.tensor_tensor(tied[:, :, :], tied[:, :, :], over(first_wins[:, :], 1, NT), ALU.mult))
                go(v.tensor_reduce(top[:, :], tied[:, :, :], axis=AX.X, op=ALU.max))
                go(v.tensor_tensor(chosen[k][:, :, :], tied[:, :, :], over(top[:, :], 2, E), ALU.is_equal))
                go(v.tensor_tensor(tmp[:, :, :], chosen[k][:, :, :], scores[:, :, :], ALU.mult))
                go(v.tensor_reduce(share[k][:, :], tmp[:, :, :], axis=AX.X, op=ALU.add))
                if k == 0:
                    go(v.tensor_scalar(tmp[:, :, :], chosen[k][:, :, :], -1e30, None, ALU.mult))
                    go(v.tensor_tensor(biased[:, :, :], biased[:, :, :], tmp[:, :, :], ALU.add))
            go(v.tensor_tensor(taken[:, :, :], chosen[0][:, :, :], chosen[1][:, :, :], ALU.add))
            v.tensor_tensor(taken[:, :, :], taken[:, :, :], over(is_token[:, :], 2, E), ALU.mult)\
                .then_inc(taken_done, 1)
            dve.wait_ge(ranks_done, 1)
            for e in range(E):
                last = v.tensor_tensor_scan(upto[:, e, :], one_row[:, :], ps_total[:, :, e], 0.0, ALU.mult, ALU.add)
            go(last)
            go(v.tensor_scalar(tiles_of[:, :], upto[:, :, NT - 1], 1.0 / MT, (MT - 1) / MT - 0.5 + 0.25 / MT,
                               ALU.mult, ALU.add))
            go(v.tensor_scalar(tiles_of[:, :], tiles_of[:, :], MAGIC, None, ALU.add))
            go(v.tensor_scalar(tiles_of[:, :], tiles_of[:, :], MAGIC, None, ALU.subtract))
            go(v.tensor_tensor_scan(ends[:, :], one_row[:, 0:E], tiles_of[:, :], 0.0, ALU.mult, ALU.add))
            go(v.tensor_tensor(start[:, :], ends[:, :], tiles_of[:, :], ALU.subtract))
            go(v.tensor_scalar(start[:, :], start[:, :], float(MT), None, ALU.mult))
            go(v.tensor_tensor(row[:, :, :], upto[:, :, :].rearrange("p e t -> p t e"), ps_total[:, :, :],
                               ALU.subtract))
            go(v.tensor_tensor(row[:, :, :], row[:, :, :], ps_rank[:, :, :], ALU.add))
            go(v.tensor_tensor(row[:, :, :], row[:, :, :], over(start[:, :], 1, NT), ALU.add))
            for k in range(2):
                go(v.tensor_tensor(tmp[:, :, :], row[:, :, :], chosen[k][:, :, :], ALU.mult))
                go(v.tensor_reduce(placef[:, :], tmp[:, :, :], axis=AX.X, op=ALU.add))
                go(v.tensor_copy(place[k][:, :, 0], placef[:, :]))
            go(v.tensor_tensor(ended[:, :, :], over(tile_no[:, :], 2, E), over(ends[:, :], 1, ROUTED), ALU.is_ge))
            go(v.tensor_reduce(owner[:, :], ended[:, :, :], axis=AX.X, op=ALU.add))
            go(v.tensor_scalar(owner[:, :], owner[:, :], float(E - 1), None, ALU.min))
            v.tensor_copy(whose[:, :], owner[0:1, :])


class Tile:

    def __init__(self, n, b, g=None, u=None, i=None, gap=None):
        self.n, self.b, self.g, self.i, self.gap = n, b, g, i, gap
        self.shared = i is not None
        self.w = 2 if self.shared else u
        self.row = None if self.shared else 2 * g + u


def experts(nc, H, xn, xs, ys, place, share, whose, shared_w, args):
    SHARED = NT // 2
    MIXED = 8
    GROUPS = ROUTED // 2
    LEAD = 4
    TRAIL = SHARED - LEAD - MIXED
    assert ROUTED % 2 == 0 and MIXED % 2 == 0 and LEAD % 2 == 0 and TRAIL > 1
    TOKEN_TILES = CLS + 1
    RING = 8

    def lead(i):
        return Tile(i, i % 2, i=i)

    def mixed(q):
        tiles = []
        for half in range(2):
            n, g = LEAD + 6 * q + 3 * half, 2 * q + half
            tiles += [Tile(n, half, g=g, u=0, gap=3), Tile(n + 1, 1 - half, g=g, u=1, gap=3),
                      Tile(n + 2, half, i=LEAD + g)]
        return tiles

    def plain(g, gap=2):
        n = LEAD + MIXED + 2 * g
        return [Tile(n, 0, g=g, u=0, gap=gap), Tile(n + 1, 1, g=g, u=1, gap=gap)]

    def trail(k):
        n = LEAD + MIXED + 2 * GROUPS + k
        return Tile(n, k % 2, i=LEAD + MIXED + k)

    def all_tiles(engine, tile):
        def run(tiles, before, after):
            tiles = [before] + tiles + [after]
            for k in range(1, len(tiles) - 1):
                tile(tiles[k - 1], tiles[k], tiles[k + 1])

        run([lead(i) for i in range(LEAD)], None, mixed(0)[0])
        run(mixed(0), lead(LEAD - 1), mixed(1)[0])
        with engine.Fori(1, MIXED // 2) as q:
            run(mixed(q), mixed(q - 1)[-1], mixed(q + 1)[0])
        run(plain(MIXED, 3), mixed(MIXED // 2 - 1)[-1], plain(MIXED + 1)[0])
        with engine.Fori(MIXED + 1, GROUPS - 1) as g:
            run(plain(g), plain(g - 1)[-1], plain(g + 1)[0])
        run(plain(GROUPS - 1), plain(GROUPS - 2)[-1], trail(0))
        run([trail(k) for k in range(TRAIL)], plain(GROUPS - 1)[-1], None)

    CH = I // P
    W13 = 2 * 2 * 2 * I
    with ExitStack() as stack:
        m = Memory(nc, stack, "ex_")
        ident = m.sb("ident", [P, P])
        wt = [m.sb(f"wt{u}", [P, EXPERT_COLS]) for u in range(2)] + [shared_w]
        w13 = [w[:, 0:W13].rearrange("p (c w g i) -> p c w g i", c=2, w=2, g=2) for w in wt]
        w2 = [w[:, W13:W13 + CH * D].rearrange("p (h d) -> p h d", h=CH) for w in wt]
        b13 = [w[:, W13 + CH * D:EXPERT_COLS].rearrange("p (h w g) -> p h w g", h=CH, w=2) for w in wt]
        b2 = [m.sb(f"b2{u}", [P, D]) for u in range(3)]
        xrow = [m.sb(f"xrow{b}", [P, 2, D]) for b in range(2)]
        xT = [m.sb(f"xT{b}", [P, 2, MT]) for b in range(2)]
        x3 = m.sb("x3", [P, 2, MT])
        gl = m.sb("gl", [P, 2, MT])
        glc = m.sb("glc", [P, 2, MT])
        th = m.sb("th", [P, MT])
        gate = m.sb("gate", [P, MT])
        hT = [m.sb(f"hT{b}", [P, CH, MT]) for b in range(2)]
        yrow = [m.sb(f"yrow{b}", [P, 2, D]) for b in range(2)]
        routed = m.sb("routed", [P, RING, 2, D])

        ps_xT = m.ps("ps_xT", [P, 2, MT])
        ps_up = [m.ps(f"ps_up{b}", [P, 2, 2, MT]) for b in range(2)]
        ps_y = m.ps("ps_y", [P, 2, D])

        ident_done = m.sem("ident_done")
        rows_out = m.sem("rows_out")
        shared_b2_in = m.sem("shared_b2_in")
        w_in = [m.sem(f"w_in{u}") for u in range(2)]
        x_in = [m.sem(f"x_in{b}") for b in range(2)]
        x_taken = m.sem("x_taken")
        xT_done = m.sem("xT_done")
        xT_copied = m.sem("xT_copied")
        up_done = m.sem("up_done")
        x3_done = m.sem("x3_done")
        half_gate = m.sem("half_gate")
        th_done = m.sem("th_done")
        h_done = m.sem("h_done")
        down_done = m.sem("down_done")
        y_copied = m.sem("y_copied")
        y_out = [m.sem(f"y_out{b}") for b in range(2)]
        gathered = [m.sem(f"gathered{s}") for s in range(RING)]
        added = m.sem("added")

        xs_v = xs.rearrange("(j s p) d -> j p s d", s=2, p=P)
        ys_v = ys.rearrange("(j s p) d -> j p s d", s=2, p=P)

        block = stack.enter_context(nc.Block())

        @block.sync
        def _(sp):
            sp.dma_start(b2[2][:, :], args["experts_b2"][E:E + 1, :].broadcast_to([P, D])).then_inc(shared_b2_in, 16)

            def load(before, t, after):
                if t.shared:
                    return
                first = isinstance(t.g, int) and t.g == 0
                e = sp.value_load(whose[0:1, bass.ds(t.row, 1)], min_val=0, max_val=E - 1)
                sp.wait_ge(xT_done, t.n - 1)
                sp.dma_start(xrow[t.b][:, :, :], xs_v[bass.ds(t.row, 1)].rearrange("o p s d -> (o p) s d"))\
                    .then_inc(x_in[t.b], 16)
                if not first:
                    sp.wait_ge(down_done, t.n - t.gap + 1)
                sp.dma_start(wt[t.w][:, :], args["experts"][bass.ds(e, 1)].rearrange("o p n -> (o p) n"))\
                    .then_inc(w_in[t.w], 16)
                if not first:
                    sp.wait_ge(y_copied, t.n - t.gap + 2)
                sp.dma_start(b2[t.w][:, :], args["experts_b2"][bass.ds(e, 1), :].broadcast_to([P, D]))\
                    .then_inc(w_in[t.w], 16)

            sp.wait_ge(rows_out, 16 * 2 * TOKEN_TILES)
            all_tiles(sp, load)

        @block.gpsimd
        def _(pool):
            zeroed = m.sem("zeroed")
            nc.gpsimd.memset(ident[:, :], 0.0).then_inc(zeroed, 1)
            pool.wait_ge(zeroed, 1)
            nc.gpsimd.affine_select(out=ident[:, :], in_=ident[:, :], compare_op=ALU.not_equal, fill=1.0,
                                    base=0, pattern=[[-1, P]], channel_multiplier=1).then_inc(ident_done, 1)
            for t in range(TOKEN_TILES):
                n = P if t < CLS else NB
                for k in range(2):
                    pool.indirect_dma_start(
                        out=xs, out_offset=bass.IndirectOffsetOnAxis(ap=place[k][0:n, t, :], axis=0),
                        in_=xn[0:n, t, :], in_offset=None).then_inc(rows_out, 16)
            for b in range(2):
                pool.wait_ge(y_out[b], 16 * (GROUPS + 1))
            for t in range(TOKEN_TILES):
                n = P if t < CLS else NB
                if t >= RING:
                    pool.wait_ge(added, t - RING + 1)
                for k in range(2):
                    pool.indirect_dma_start(
                        out=routed[0:n, t % RING, k, :], out_offset=None, in_=ys,
                        in_offset=bass.IndirectOffsetOnAxis(ap=place[k][0:n, t, :], axis=0))\
                        .then_inc(gathered[t % RING], 16)

        @block.tensor
        def _(pe):
            def turn(t):
                if t.shared:
                    pe.wait_ge(x_taken, t.i + 1)
                else:
                    pe.wait_ge(x_in[t.b], 16 * t.g + 16)
                for c in range(2):
                    for s in range(2):
                        last = nc.tensor.transpose(ps_xT[:, c, s * P:(s + 1) * P],
                                                   xrow[t.b][:, s, c * P:(c + 1) * P], ident[:, :])
                last.then_inc(xT_done, 1)

            def up(t, h, first):
                if h == 0:
                    if not t.shared:
                        pe.wait_ge(w_in[t.w], 32 * t.g + 32)
                    pe.wait_ge(xT_copied, t.n + 1)
                if not first:
                    pe.wait_ge(half_gate, 4 * t.n + h - 1)
                for w in range(2):
                    for k in range(2):
                        for c in range(2):
                            last = nc.tensor.matmul(ps_up[h % 2][:, w, k, :],
                                                    w13[t.w][:, c, w, k, h * P:(h + 1) * P], xT[t.b][:, c, :],
                                                    start=c == 0, stop=c == 1)
                last.then_inc(up_done, 1)

            def down(t):
                pe.wait_ge(h_done, 4 * t.n + 4)
                pe.wait_ge(y_copied, t.n + 1)
                for s in range(2):
                    for h in range(CH):
                        last = nc.tensor.matmul(ps_y[:, s, :], hT[t.b][:, h, s * P:(s + 1) * P], w2[t.w][:, h, :],
                                                start=h == 0, stop=h == CH - 1)
                last.then_inc(down_done, 1)

            def tile(before, t, after):
                up(t, 0, before is None)
                if before:
                    down(before)
                up(t, 1, before is None)
                if after:
                    turn(after)
                up(t, 2, False)
                up(t, 3, False)

            pe.wait_ge(ident_done, 1)
            turn(lead(0))
            all_tiles(pe, tile)
            down(trail(TRAIL - 1))

        @block.scalar
        def _(act):
            def copy(t):
                act.wait_ge(xT_done, t.n + 1)
                nc.scalar.activation(xT[t.b][:, :, :], ps_xT[:, :, :], ACT.Copy).then_inc(xT_copied, 1)

            def chunk(t, h, first):
                q = 4 * t.n + h
                act.wait_ge(up_done, q + 1)
                if not first:
                    act.wait_ge(half_gate, q)
                for k in range(2):
                    last = nc.scalar.activation(x3[:, k, :], ps_up[h % 2][:, 1, k, :], ACT.Identity,
                                                bias=b13[t.w][:, h, 1, k:k + 1])
                last.then_inc(x3_done, 1)
                act.wait_ge(half_gate, q + 1)
                nc.scalar.activation(th[:, :], glc[:, 0, :], ACT.Tanh, scale=1.702).then_inc(th_done, 1)

            def store(t):
                act.wait_ge(y_copied, t.n + 2)
                act.dma_start(ys_v[bass.ds(t.row, 1)].rearrange("o p s d -> (o p) s d"), yrow[t.b][:, :, :])\
                    .then_inc(y_out[t.b], 16)

            def take(t):
                nc.scalar.activation(xrow[t.b][:, :, :], xn[:, bass.ds(2 * t.i, 2), :], ACT.Copy).then_inc(x_taken, 1)

            def tile(before, t, after):
                for h in range(CH):
                    chunk(t, h, before is None and h == 0)
                    if h == 0 and after and after.shared:
                        take(after)
                    if h == 1 and after:
                        copy(after)
                    if h == 2 and before and not before.shared:
                        store(before)

            for b in range(2):
                act.sem_inc(y_out[b], 16)
            take(lead(0))
            copy(lead(0))
            all_tiles(act, tile)

        @block.vector
        def _(dve):
            head_steps = Steps(dve, m.sem("dve_head"), 1)
            tail_steps = Steps(dve, m.sem("dve_tail"), 1)
            shared_added = m.sem("shared_added")
            routed_added = m.sem("routed_added")
            dve.sem_inc(y_copied, 1)
            dve.wait_ge(shared_b2_in, 16)

            def chunk(t, h):
                q = 4 * t.n + h
                head_steps.round(q)
                tail_steps.round(q)
                dve.wait_ge(x3_done, q + 1)
                for k in range(2):
                    last = nc.vector.scalar_tensor_tensor(gl[:, k, :], ps_up[h % 2][:, 0, k, :],
                                                          b13[t.w][:, h, 0, k:k + 1], x3[:, k, :], ALU.add, ALU.mult)
                head_steps.then_wait(last)
                nc.vector.tensor_scalar(glc[:, 0, :], gl[:, 0, :], 7.0, 0.5, ALU.min, ALU.mult)
                nc.vector.tensor_scalar(glc[:, 1, :], gl[:, 1, :], -7.0, 7.0, ALU.max, ALU.min)\
                    .then_inc(half_gate, 1)
                dve.wait_ge(th_done, q + 1)
                tail_steps.then_wait(nc.vector.scalar_tensor_tensor(gate[:, :], th[:, :], 1.0, glc[:, 0, :],
                                                                    ALU.add, ALU.mult))
                nc.vector.scalar_tensor_tensor(hT[t.b][:, h, :], glc[:, 1, :], 1.0, gate[:, :],
                                               ALU.add, ALU.mult).then_inc(h_done, 1)

            def copy_y(t):
                dve.wait_ge(down_done, t.n + 1)
                if not t.shared:
                    dve.wait_ge(y_out[t.b], 16 * t.g + 16)
                    nc.vector.tensor_tensor(yrow[t.b][:, :, :], ps_y[:, :, :], over(b2[t.w][:, :], 1, 2), ALU.add)\
                        .then_inc(y_copied, 1)
                    return
                n, s = (NB, 1) if isinstance(t.i, int) and 2 * t.i == CLS else (P, 2)
                h = H[0:n, bass.ds(2 * t.i, s), :]
                nc.vector.tensor_tensor(h, h, ps_y[0:n, 0:s, :], ALU.add).then_inc(y_copied, 1)
                dve.wait_ge(y_copied, t.n + 2)
                nc.vector.tensor_tensor(h, h, over(b2[2][0:n, :], 1, s), ALU.add).then_inc(shared_added, 1)

            def add_routed(t):
                n = P if t < CLS else NB
                h = H[0:n, t, :]
                dve.wait_ge(gathered[t % RING], 32 * (t // RING + 1))
                dve.wait_ge(shared_added, t // 2 + 1)
                nc.vector.scalar_tensor_tensor(h, routed[0:n, t % RING, 0, :], share[0][0:n, t:t + 1], h,
                                               ALU.mult, ALU.add).then_inc(routed_added, 1)
                dve.wait_ge(routed_added, t + 1)
                nc.vector.scalar_tensor_tensor(h, routed[0:n, t % RING, 1, :], share[1][0:n, t:t + 1], h,
                                               ALU.mult, ALU.add).then_inc(added, 1)

            tokens = iter(range(TOKEN_TILES))
            each = -(-TOKEN_TILES // (4 * (TRAIL - 1) + 1))

            def tile(before, t, after):
                ending = t.shared and isinstance(t.i, int) and t.i > SHARED - TRAIL
                for h in range(CH):
                    chunk(t, h)
                    if h == 1 and before:
                        copy_y(before)
                    if ending:
                        for _, token_tile in zip(range(each), tokens):
                            add_routed(token_tile)

            all_tiles(dve, tile)
            copy_y(trail(TRAIL - 1))
            for token_tile in tokens:
                add_routed(token_tile)


def queries_keys_values(nc, H, qkv, class_keys, vcls, args):
    G = AH // 2
    with ExitStack() as stack:
        m = Memory(nc, stack, "pj_")
        w = m.sb("w", [P, 2, 3 * D])
        cos = m.sb("cos", [P, 2, DH])
        sin = m.sb("sin", [P, 2, DH])
        ident = m.sb("ident", [P, P])
        mhalf = m.sb("mhalf", [P, 2])
        eps = m.sb("eps", [P, 2])
        stats = m.sb("stats", [P, 2, 6])
        mv = m.sb("mv", [P, 2, 2])
        rstd = m.sb("rstd", [P, 2])
        xp = m.sb("xp", [P, 2, D])
        xT = [m.sb(f"xT{b}", [P, 2, 2 * P]) for b in range(2)]
        straight = m.sb("straight", [P, 2, 2 * D])
        crossed = m.sb("crossed", [P, 2, 2 * D])
        kpad = m.sb("kpad", [P, AH, 64])

        ps_xT = m.ps("ps_xT", [P, 2, 2 * P])
        ps_qk = [m.ps(f"ps_qk{b}", [P, 2, 2, D]) for b in range(2)]
        ps_v = [m.ps(f"ps_v{b}", [P, 2, D]) for b in range(2)]
        ps_kT = ps_qk[1].rearrange("p s j d -> p (s j d)").rearrange("p (g t) -> p g t", g=G)

        consts_in = m.sem("consts_in")
        consts = m.sem("consts")
        zeroed = m.sem("zeroed")
        ident_done = m.sem("ident_done")
        var_done = m.sem("var_done")
        rstd_done = m.sem("rstd_done")
        xp_done = m.sem("xp_done")
        xT_done = m.sem("xT_done")
        xT_copied = m.sem("xT_copied")
        p_done = m.sem("p_done")
        v_copied = m.sem("v_copied")
        turned = m.sem("turned")
        added = m.sem("added")
        high_done = m.sem("high_done")
        kpad_done = m.sem("kpad_done")
        kT_done = m.sem("kT_done")
        keys_done = m.sem("keys_done")
        vcls_out = m.sem("vcls_out")
        PAIRS = NT // 2

        def exists(k, last=PAIRS - 1):
            return not isinstance(k, int) or k <= last

        def all_turns(engine, turn):
            pairs = (PAIRS - 3) // 2
            with engine.Fori(0, pairs) as i:
                turn(2 * i, 0)
                turn(2 * i + 1, 1)
            for k in range(2 * pairs, PAIRS):
                turn(k, k % 2)

        block = stack.enter_context(nc.Block())

        @block.sync
        def _(sp):
            sp.dma_start(w[:, :, :], args["att_w"].rearrange("(c p) n -> p c n", p=P)).then_inc(consts_in, 16)
            sp.dma_start(cos[:, :, :], args["rope_cos"].rearrange("(s p) j -> p s j", p=P)).then_inc(consts_in, 16)
            sp.dma_start(sin[:, :, :], args["rope_sin"].rearrange("(s p) j -> p s j", p=P)).then_inc(consts_in, 16)
            sp.wait_ge(v_copied, PAIRS + 2)
            sp.dma_start(vcls, qkv[0:NB, CLS, 2 * D:3 * D]).then_inc(vcls_out, 16)
            sp.wait_ge(vcls_out, 16)

        @block.gpsimd
        def _(pool):
            pool.sem_inc(added, 1)
            nc.gpsimd.memset(mhalf[:, :], -0.5).then_inc(consts, 1)
            nc.gpsimd.memset(eps[:, :], EPS).then_inc(consts, 1)
            nc.gpsimd.memset(ident[:, :], 0.0).then_inc(consts, 1)
            pool.wait_ge(consts, 3)
            nc.gpsimd.affine_select(out=ident[:, :], in_=ident[:, :], compare_op=ALU.not_equal, fill=1.0,
                                    base=0, pattern=[[-1, P]], channel_multiplier=1).then_inc(ident_done, 1)
            nc.gpsimd.memset(kpad[:, :, :], 0.0).then_inc(zeroed, 1)
            nc.gpsimd.memset(class_keys[:, :, :, :], 0.0).then_inc(zeroed, 1)
            steps = Steps(pool, m.sem("pool_rstd"), 1)

            def root(k):
                steps.round(k)
                pool.wait_ge(var_done, k + 1)
                steps.then_wait(nc.gpsimd.tensor_tensor(rstd[:, :], mv[:, :, 1], eps[:, :], ALU.add))
                nc.gpsimd.tensor_tensor(rstd[:, :], rstd[:, :], mhalf[:, :], ALU.pow).then_inc(rstd_done, 1)

            def add(k):
                pool.wait_ge(turned, k + 3)
                nc.gpsimd.tensor_tensor(qkv[:, bass.ds(2 * k, 2), 0:2 * D], straight[:, :, :], crossed[:, :, :],
                                        ALU.add).then_inc(added, 1)

            root(0)
            root(1)
            root(2)
            with pool.Fori(0, PAIRS - 3) as k:
                root(k + 3)
                add(k)
            add(PAIRS - 3)
            add(PAIRS - 2)

        @block.tensor
        def _(pe):
            pe.wait_ge(ident_done, 1)
            pe.wait_ge(consts_in, 3 * 16)

            def turn_x(k):
                pe.wait_ge(xp_done, k + 1)
                if not isinstance(k, int) or k > 0:
                    pe.wait_ge(xT_copied, k)
                for c in range(2):
                    for s in range(2):
                        last = nc.tensor.transpose(ps_xT[:, c, s * P:(s + 1) * P],
                                                   xp[:, s, c * P:(c + 1) * P], ident[:, :])
                last.then_inc(xT_done, 1)

            def turn(k, b):
                if exists(k + 1):
                    turn_x(k + 1)
                pe.wait_ge(xT_copied, k + 1)
                pe.wait_ge(v_copied, k + 1)
                pe.wait_ge(turned, k + 1)
                for s in range(2):
                    for j in range(3):
                        for c in range(2):
                            to = ps_qk[b][:, s, j, :] if j < 2 else ps_v[b][:, s, :]
                            last = nc.tensor.matmul(to, xT[b][:, c, s * P:(s + 1) * P],
                                                    w[:, c, j * D:(j + 1) * D], start=c == 0, stop=c == 1)
                last.then_inc(p_done, 1)

            turn_x(0)
            all_turns(pe, turn)
            pe.wait_ge(turned, PAIRS + 1)
            pe.wait_ge(v_copied, PAIRS + 1)
            pe.wait_ge(kpad_done, 1)
            for g in range(G):
                last = nc.tensor.transpose(ps_kT[:, g, :], kpad[:, 2 * g:2 * g + 2, :], ident[:, :])
            last.then_inc(kT_done, 1)

        @block.scalar
        def _(act):
            act.sem_inc(v_copied, 2)

            def copy_x(k, b):
                act.wait_ge(xT_done, k + 1)
                if not isinstance(k, int) or k >= 2:
                    act.wait_ge(p_done, k - 1)
                nc.scalar.activation(xT[b][:, :, :], ps_xT[:, :, :], ACT.Copy).then_inc(xT_copied, 1)

            def turn(k, b):
                if exists(k + 1):
                    copy_x(k + 1, 1 - b)
                act.wait_ge(p_done, k + 1)
                nc.scalar.activation(qkv[:, bass.ds(2 * k, 2), 2 * D:3 * D], ps_v[b][:, :, :], ACT.Copy)\
                    .then_inc(v_copied, 1)

            copy_x(0, 0)
            all_turns(act, turn)
            nc.scalar.activation(qkv[:, CLS:NT, 0:D], ps_v[0][:, :, :], ACT.Copy)
            keys = ps_qk[0][:, 0, 1, :].rearrange("p (h j) -> p h j", h=AH)
            act.wait_ge(zeroed, 1)
            for slot in (0, 2):
                last = nc.scalar.activation(kpad[:, :, slot * DH:(slot + 1) * DH].bitcast(F32R), keys, ACT.Copy)
            last.then_inc(high_done, 1)
            act.wait_ge(kT_done, 1)
            act.wait_ge(zeroed, 2)
            for hh in range(2):
                rows = slice(64 * hh, 64 * hh + 64)
                last = nc.scalar.activation(class_keys[rows, :, hh, :].bitcast(F32R), ps_kT[rows, :, 0:NB], ACT.Copy)
            last.then_inc(keys_done, 1)

        @block.vector
        def _(dve):
            stat_steps = Steps(dve, m.sem("dve_stat"), 1)
            dve.sem_inc(turned, 2)
            dve.wait_ge(consts_in, 3 * 16)

            def moments(k):
                stat_steps.round(k)
                for s in range(2):
                    last = nc.vector.bn_stats(stats[:, s, :], H[:, bass.ds(2 * k + s, 1), :])
                stat_steps.then_wait(last, (consts_in, 3 * 16))
                for s in range(2):
                    last = nc.vector.bn_aggr(mv[:, s, :], stats[:, s, :])
                last.then_inc(var_done, 1)

            def normalise(k):
                dve.wait_ge(rstd_done, k + 1)
                if not isinstance(k, int) or k > 0:
                    dve.wait_ge(xT_done, k)
                for s in range(2):
                    last = nc.vector.tensor_scalar(xp[:, s, :], H[:, bass.ds(2 * k + s, 1), :],
                                                   mv[:, s, 0:1], rstd[:, s:s + 1], ALU.subtract, ALU.mult)
                last.then_inc(xp_done, 1)

            def rotate(k, b):
                dve.wait_ge(p_done, k + 1)
                dve.wait_ge(added, k + 1)
                hd = DH // 2
                for s in range(2):
                    p = ps_qk[b][:, s, :, :].rearrange("p a (h j) -> p (a h) j", j=DH)
                    o = straight[:, s, :].rearrange("p (h j) -> p h j", j=DH)
                    x = crossed[:, s, :].rearrange("p (h j) -> p h j", j=DH)
                    nc.vector.tensor_tensor(o, p, over(cos[:, s, :], 1, 2 * AH), ALU.mult)
                    nc.vector.tensor_tensor(x[:, :, 0:hd], p[:, :, hd:DH], over(sin[:, s, 0:hd], 1, 2 * AH),
                                            ALU.mult)
                    last = nc.vector.tensor_tensor(x[:, :, hd:DH], p[:, :, 0:hd],
                                                   over(sin[:, s, hd:DH], 1, 2 * AH), ALU.mult)
                last.then_inc(turned, 1)

            def turn(k, b):
                if exists(k + 2):
                    normalise(k + 2)
                if exists(k + 3):
                    moments(k + 3)
                if exists(k + 1):
                    rotate(k, b)

            for k in range(2):
                moments(k)
                normalise(k)
            moments(2)
            all_turns(dve, turn)
            dve.wait_ge(high_done, 1)
            nc.vector.tensor_tensor(kpad[:, :, DH:2 * DH], ps_qk[0][:, 0, 1, :].rearrange("p (h j) -> p h j", h=AH),
                                    kpad[:, :, 0:DH], ALU.subtract).then_inc(kpad_done, 1)


def attention(nc, qkv, class_keys, vcls, args):
    R = AH // 2
    QK = 0.25
    K = 3 * DH
    with ExitStack() as stack:
        m = Memory(nc, stack, "at_")
        ident = m.sb("ident", [P, P])
        ident16 = m.sb("ident16", [P, P], BF16)
        hidden = m.sb("hidden", [P, 2, P], BF16)
        pad = [m.sb(f"pad{b}", [P, 2, 2, 2, 64]) for b in range(2)]
        vc = m.sb("vc", [P, D])
        qkT = [m.sb(f"qkT{b}", [P, R, 2, 2, P], F32R) for b in range(2)]
        sc = m.sb("sc", [P, 2, AH])
        mx = m.sb("mx", [P, AH, 2])
        nmx = m.sb("nmx", [P, AH, 2])
        pr = [m.sb(f"pr{b}", [P, 2, 3 * P]) for b in range(2)]
        pT = [m.sb(f"pT{b}", [P, 2, 3 * P]) for b in range(2)]
        pc = m.sb("pc", [P, 2, AH])
        weights = [m.sb(f"weights{b}", [P, 2, AH]) for b in range(2)]
        den = m.sb("den", [P, 2, AH])
        o = m.sb("o", [P, 2, AH, DH])

        ps_s = [m.ps(f"ps_s{b}", [P, 2, 512]) for b in range(2)]
        ps_t = m.ps("ps_t", [P, 2, 512])
        ps_c = ps_t[:, :, 384:384 + AH]
        ps_n = m.ps("ps_n", [P, 2, 2, P])
        ps_v = m.ps("ps_v", [P, 2, AH, DH])

        zeroed = m.sem("zeroed")
        ident_done = m.sem("ident_done")
        ident16_done = m.sem("ident16_done")
        padded = m.sem("padded")
        turned = m.sem("turned")
        qk_copied = m.sem("qk_copied")
        vc_in = m.sem("vc_in")
        sc_done = m.sem("sc_done")
        sc_copied = m.sem("sc_copied")
        s_done = m.sem("s_done")
        nmx_done = m.sem("nmx_done")
        exp_done = m.sem("exp_done")
        pT_done = m.sem("pT_done")
        pT_copied = m.sem("pT_copied")
        pv_done = m.sem("pv_done")
        sc_less = m.sem("sc_less")
        pc_done = m.sem("pc_done")
        o_read = m.sem("o_read")
        o_done = m.sem("o_done")

        def all_sequences(engine, sequence):
            with engine.Fori(0, (NB - 2) // 2) as i:
                sequence(2 * i, 0)
                sequence(2 * i + 1, 1)
            sequence(NB - 2, 0)
            sequence(NB - 1, 1)

        def exists(n):
            return not isinstance(n, int) or n < NB

        block = stack.enter_context(nc.Block())

        @block.sync
        def _(sp):
            sp.dma_start(vc[:, :], vcls[0:1, :].broadcast_to([P, D])).then_inc(vc_in, 16)
            with sp.Fori(1, NB) as n:
                sp.wait_ge(o_read, n + 1)
                sp.dma_start(vc[:, :], vcls[bass.ds(n, 1), :].broadcast_to([P, D])).then_inc(vc_in, 16)

        @block.gpsimd
        def _(pool):
            nc.gpsimd.memset(ident[:, :], 0.0).then_inc(zeroed, 1)
            nc.gpsimd.memset(hidden[:, :, :], 0.0).then_inc(zeroed, 1)
            for b in range(2):
                nc.gpsimd.memset(pad[b][:, :, :, :, :], 0.0).then_inc(zeroed, 1)
            pool.wait_ge(zeroed, 4)
            nc.gpsimd.affine_select(out=ident[:, :], in_=ident[:, :], compare_op=ALU.not_equal, fill=1.0,
                                    base=0, pattern=[[-1, P]], channel_multiplier=1).then_inc(ident_done, 1)
            nc.gpsimd.affine_select(out=hidden[:, :, :], in_=hidden[:, :, :], compare_op=ALU.is_ge, fill=-1e30,
                                    base=0, pattern=[[0, 2], [-1, P]], channel_multiplier=1).then_inc(ident_done, 1)
            pool.wait_ge(ident_done, 2)
            nc.gpsimd.tensor_copy(ident16[:, :], ident[:, :]).then_inc(ident16_done, 1)

            steps = Steps(pool, m.sem("pool_high"), 1)

            def split(n, r, first):
                if not first:
                    pool.wait_ge(turned, R * n + r - 1)
                tiles = bass.ds(2 * n, 2)
                to = pad[r % 2]
                for a in range(2):
                    x = qkv[:, tiles, a * D + 2 * r * DH:a * D + (2 * r + 2) * DH].rearrange(
                        "p s (h j) -> p s h j", h=2)
                    for slot in ((0, 1), (0, 2))[a]:
                        last = nc.gpsimd.tensor_copy(to[:, a, :, :, slot * DH:(slot + 1) * DH].bitcast(F32R), x)
                steps.round(R * n + r)
                steps.then_wait(last, (ident_done, 2))
                for a in range(2):
                    x = qkv[:, tiles, a * D + 2 * r * DH:a * D + (2 * r + 2) * DH].rearrange(
                        "p s (h j) -> p s h j", h=2)
                    slot = (2, 1)[a]
                    last = nc.gpsimd.tensor_tensor(to[:, a, :, :, slot * DH:(slot + 1) * DH], x,
                                                   to[:, a, :, :, 0:DH], ALU.subtract)
                last.then_inc(padded, 1)

            for r in range(R):
                split(0, r, r < 2)
            with pool.Fori(1, NB) as n:
                for r in range(R):
                    split(n, r, False)

        @block.tensor
        def _(pe):
            pe.wait_ge(ident16_done, 1)

            def turn_qk(n, r):
                pe.wait_ge(padded, R * n + r + 1)
                pe.wait_ge(qk_copied, R * n + r + 1)
                for a in range(2):
                    for s in range(2):
                        last = nc.tensor.transpose(ps_n[:, a, s, :], pad[r % 2][:, a, s, :, :], ident[:, :])
                last.then_inc(turned, 1)

            def class_scores(n, nb):
                pe.wait_ge(qk_copied, R * n + R + 1)
                pe.wait_ge(pT_copied, R * n + 1)
                for s in range(2):
                    for g in range(R):
                        last = nc.tensor.matmul(ps_c[:, s, 2 * g:2 * g + 2], qkT[nb][:, g, 0, s, :],
                                                class_keys[:, g, :, bass.ds(n, 1)].bitcast(F32R),
                                                start=True, stop=True)
                last.then_inc(sc_done, 1)

            def scores(n, nb, r):
                b = r % 2
                pe.wait_ge(exp_done, R * n + r)
                for hh in range(2):
                    rows = slice(64 * hh, 64 * hh + K)
                    q, k = qkT[nb][rows, r, 0], qkT[nb][rows, r, 1]
                    nc.tensor.matmul(ps_s[b][:, hh, 0:P], q[:, 0, :], k[:, 0, :], start=True, stop=False)
                    nc.tensor.matmul(ps_s[b][:, hh, P:3 * P], q[:, 1, :], k.rearrange("p s t -> p (s t)"),
                                     start=False, stop=False)
                    last = nc.tensor.matmul(
                        ps_s[b][:, hh, 0:3 * P].rearrange("p (c t) -> p c t", c=3)[:, 0:3:2, :],
                        ident16[:, :], hidden[:, :, :], start=False, stop=True)
                last.then_inc(s_done, 1)

            def turn(n, r):
                pe.wait_ge(exp_done, R * n + r + 3)
                if r == 0:
                    pe.wait_ge(sc_copied, n + 1)
                else:
                    pe.wait_ge(pT_copied, R * n + r + 1)
                for hh in range(2):
                    for c in range(3):
                        last = nc.tensor.transpose(ps_t[:, hh, c * P:(c + 1) * P],
                                                   pr[r % 2][:, hh, c * P:(c + 1) * P], ident[:, :])
                last.then_inc(pT_done, 1)

            def values(n, r):
                if r == 0:
                    pe.wait_ge(o_read, n + 1)
                pe.wait_ge(pT_copied, R * n + r + 2)
                for hh in range(2):
                    h = 2 * r + hh
                    p = pT[r % 2]
                    v = [qkv[:, bass.ds(2 * n + s, 1), 2 * D + h * DH:2 * D + (h + 1) * DH] for s in range(2)]
                    nc.tensor.matmul(ps_v[:, 0, h, :], p[:, hh, 0:P], v[0], start=True, stop=True)
                    nc.tensor.matmul(ps_v[:, 1, h, :], p[:, hh, P:2 * P], v[0], start=True, stop=False)
                    last = nc.tensor.matmul(ps_v[:, 1, h, :], p[:, hh, 2 * P:3 * P], v[1], start=False, stop=True)
                last.then_inc(pv_done, 1)

            def sequence(n, nb):
                class_scores(n, nb)
                scores(n, nb, 0)
                for r in range(R):
                    if r + 1 < R:
                        scores(n, nb, r + 1)
                    if exists(n + 1):
                        turn_qk(n + 1, r)
                    turn(n, r)
                    if r:
                        values(n, r - 1)
                values(n, R - 1)

            for r in range(R):
                turn_qk(0, r)
            all_sequences(pe, sequence)

        @block.scalar
        def _(act):
            act.sem_inc(exp_done, 2)
            act.sem_inc(qk_copied, 1)

            def copy_qk(n, nb, r):
                act.wait_ge(turned, R * n + r + 1)
                nc.scalar.activation(qkT[nb][:, r], ps_n[:, :, :, :], ACT.Copy).then_inc(qk_copied, 1)

            def sequence(n, nb):
                for r in range(R):
                    act.wait_ge(nmx_done, R * n + r + 1)
                    if not isinstance(n, int) or n > 0 or r >= 2:
                        act.wait_ge(pT_done, R * n + r + 1)
                    for hh in range(2):
                        h = 2 * r + hh
                        nc.scalar.activation(pr[r % 2][:, hh, 0:P], ps_s[r % 2][:, hh, 0:P], ACT.Exp,
                                             bias=nmx[:, h, 0:1], scale=QK, accum_out=weights[nb][:, 0, h:h + 1])
                        last = nc.scalar.activation(pr[r % 2][:, hh, P:3 * P], ps_s[r % 2][:, hh, P:3 * P], ACT.Exp,
                                                    bias=nmx[:, h, 1:2], scale=QK,
                                                    accum_out=weights[nb][:, 1, h:h + 1])
                    last.then_inc(exp_done, 1)
                    if exists(n + 1):
                        copy_qk(n + 1, 1 - nb, r)
                act.wait_ge(sc_less, n + 1)
                nc.scalar.activation(pc[:, :, :], pc[:, :, :], ACT.Exp, scale=QK).then_inc(pc_done, 1)

            for r in range(R):
                copy_qk(0, 0, r)
            act.sem_inc(pT_done, 2)
            all_sequences(act, sequence)

        @block.vector
        def _(dve):
            mx_steps = Steps(dve, m.sem("dve_mx"), 2)
            out_steps = Steps(dve, m.sem("dve_out"), 1)
            dve.sem_inc(pT_copied, 1)
            dve.sem_inc(o_read, 1)

            def maxima(n, r):
                mx_steps.round(R * n + r)
                dve.wait_ge(s_done, R * n + r + 1)
                two = slice(2 * r, 2 * r + 2)
                nc.vector.tensor_reduce(mx[:, two, 0], ps_s[r % 2][:, :, 0:P], axis=AX.X, op=ALU.max)
                mx_steps.then_wait(nc.vector.tensor_reduce(mx[:, two, 1], ps_s[r % 2][:, :, P:3 * P],
                                                           axis=AX.X, op=ALU.max))
                mx_steps.then_wait(nc.vector.tensor_tensor(mx[:, two, :], mx[:, two, :],
                                                           sc[:, :, two].rearrange("p q h -> p h q"), ALU.max))
                nc.vector.tensor_scalar(nmx[:, two, :], mx[:, two, :], -QK, None, ALU.mult).then_inc(nmx_done, 1)

            def copy_pT(n, r):
                dve.wait_ge(pT_done, R * n + r + 3)
                if r >= 2:
                    dve.wait_ge(pv_done, R * n + r - 1)
                elif not isinstance(n, int) or n > 0:
                    dve.wait_ge(pv_done, R * n)
                nc.vector.tensor_copy(pT[r % 2][:, :, :], ps_t[:, :, 0:3 * P]).then_inc(pT_copied, 1)

            def finish(n, nb):
                out_steps.round(n)
                dve.wait_ge(pc_done, n + 1)
                dve.wait_ge(vc_in, 16 * n + 16)
                nc.vector.tensor_tensor(o[:, :, :, :], over(pc[:, :, :], 3, DH),
                                        over(vc[:, :].rearrange("p (h j) -> p h j", h=AH), 1, 2), ALU.mult)
                out_steps.then_wait(nc.vector.tensor_tensor(den[:, :, :], weights[nb][:, :, :], pc[:, :, :], ALU.add))
                nc.vector.reciprocal(den[:, :, :], den[:, :, :])
                dve.wait_ge(pv_done, R * n + R)
                nc.vector.tensor_tensor(o[:, :, :, :], o[:, :, :, :], ps_v[:, :, :, :], ALU.add).then_inc(o_read, 1)
                dve.wait_ge(o_read, n + 2)
                nc.vector.tensor_tensor(
                    qkv[:, bass.ds(2 * n, 2), 0:D].rearrange("p s (h j) -> p s h j", h=AH), o[:, :, :, :],
                    over(den[:, :, :], 3, DH), ALU.mult).then_inc(o_done, 1)

            def sequence(n, nb, first=False):
                dve.wait_ge(sc_done, n + 1)
                nc.vector.tensor_copy(sc[:, :, :], ps_c).then_inc(sc_copied, 1)
                dve.wait_ge(sc_copied, n + 1)
                maxima(n, 0)
                for r in range(R):
                    if r + 1 < R:
                        maxima(n, r + 1)
                    else:
                        dve.wait_ge(nmx_done, R * n + R)
                        nc.vector.tensor_tensor(pc[:, :, :], sc[:, :, :], mx[:, :, :].rearrange("p h q -> p q h"),
                                                ALU.subtract).then_inc(sc_less, 1)
                    if r == 0 and not first:
                        finish(n - 1, 1 - nb)
                    copy_pT(n, r)

            sequence(0, 0, first=True)
            sequence(1, 1)
            with dve.Fori(1, NB // 2) as i:
                sequence(2 * i, 0)
                sequence(2 * i + 1, 1)
            finish(NB - 1, 1)


def bitlinear_ffn(nc, H, att, args, out):
    F = 1024
    FC = F // P
    HALF = F // 2
    T = CLS + 1
    with ExitStack() as stack:
        m = Memory(nc, stack, "ff_")
        ident = m.sb("ident", [P, P])
        ident16 = m.sb("ident16", [P, P], BF16)
        ones = m.sb("ones", [P, P])
        mhalf = m.sb("mhalf", [P, 1])
        eps = m.sb("eps", [P, 1])
        wo = m.sb("wo", [P, 2, D])
        wf = m.sb("wf", [P, 2, 2 * F])
        wdf = m.sb("wdf", [P, FC, D])
        wq = m.sb("wq", [P, 2, 2 * F], BF16)
        wdq = m.sb("wdq", [P, FC, D], BF16)
        sums = m.sb("sums", [P, 3])
        wscale = m.sb("wscale", [P, 3])
        winv = m.sb("winv", [P, 3])
        ao = [m.sb(f"ao{b}", [P, D]) for b in range(2)]
        aoT = m.sb("aoT", [P, 2, P])
        stats = m.sb("stats", [P, 6])
        mv = m.sb("mv", [P, 2])
        rstd = m.sb("rstd", [P, 1])
        xn = m.sb("xn", [P, D])
        xr = m.sb("xr", [P, D])
        xq = m.sb("xq", [P, D], BF16)
        xqT = m.sb("xqT", [P, 2, P], BF16)
        amax = m.sb("amax", [P, 1])
        ascale = m.sb("ascale", [P, 1])
        scales = [m.sb(f"scales{b}", [P, 2]) for b in range(2)]
        gate_scale, up_scale = ([x[:, k:k + 1] for x in scales] for k in range(2))
        silu = m.sb("silu", [P, F])
        z = [m.sb(f"z{b}", [P, F]) for b in range(2)]
        zq = m.sb("zq", [P, F], BF16)
        zqT = m.sb("zqT", [P, FC, P], BF16)
        zmax = m.sb("zmax", [P, 1])
        zscale = m.sb("zscale", [P, 1])
        zmul = m.sb("zmul", [P, 1])
        down_scale = [m.sb(f"down_scale{b}", [P, 1]) for b in range(2)]
        res = [m.sb(f"res{b}", [P, D]) for b in range(2)]

        ps_gu = m.ps("ps_gu", [P, 2, 2, HALF])
        ps_tr = m.ps("ps_tr", [P, 4, P])
        ps_aoT = ps_tr[:, 0:2, :]
        ps_xqT = ps_tr[:, 2, :].bitcast(BF16).rearrange("p (c t) -> p c t", c=2)
        ps_h = m.ps("ps_h", [P, D])
        ps_d = m.ps("ps_d", [P, D])
        ps_zqT = m.ps("ps_zqT", [P, FC, P], BF16)

        w_in = m.sem("w_in")
        part_in = [m.sem(f"part_in{k}") for k in range(3)]
        part_rounded = m.sem("part_rounded")
        consts = m.sem("consts")
        ident_done = m.sem("ident_done")
        sums_done = m.sem("sums_done")
        total_done = m.sem("total_done")
        wq_done = m.sem("wq_done")
        ao_copied = m.sem("ao_copied")
        aoT_done = m.sem("aoT_done")
        aoT_copied = m.sem("aoT_copied")
        h_done = m.sem("h_done")
        var_done = m.sem("var_done")
        rstd_done = m.sem("rstd_done")
        xq_done = m.sem("xq_done")
        xqT_done = m.sem("xqT_done")
        xqT_copied = m.sem("xqT_copied")
        gu_done = m.sem("gu_done")
        silu_done = m.sem("silu_done")
        gu_read = m.sem("gu_read")
        zr_done = m.sem("zr_done")
        zq_done = m.sem("zq_done")
        zqT_done = m.sem("zqT_done")
        zqT_copied = m.sem("zqT_copied")
        down_done = m.sem("down_done")
        scaled = m.sem("scaled")
        res_done = m.sem("res_done")
        stored = [m.sem(f"stored{b}") for b in range(2)]

        def exists(t):
            return not isinstance(t, int) or 0 <= t < T

        def all_turns(engine, turn):
            turn(0, 0)
            pairs = (T - 4) // 2
            with engine.Fori(0, pairs) as i:
                turn(2 * i + 1, 1)
                turn(2 * i + 2, 0)
            for t in range(2 * pairs + 1, T + 1):
                turn(t, t % 2)

        block = stack.enter_context(nc.Block())

        @block.sync
        def _(sp):
            gate_up = args["ffn_gu"].rearrange("(c p) n -> p c n", p=P)
            for k in range(2):
                sp.dma_start(wf[:, :, k * F:(k + 1) * F], gate_up[:, :, k * F:(k + 1) * F]).then_inc(part_in[k], 16)
            sp.dma_start(wdf[:, :, :], args["ffn_down"].rearrange("(c p) n -> p c n", p=P)).then_inc(part_in[2], 16)
            sp.dma_start(wo[:, :, :], args["att_wo"].rearrange("(c p) n -> p c n", p=P)).then_inc(w_in, 16)
            for b in range(2):
                sp.sem_inc(stored[b], 16)
            with sp.Fori(0, NB) as i:
                for b in range(2):
                    sp.wait_ge(res_done, 2 * i + b + 1)
                    sp.dma_start(out[bass.ds(i, 1), 1 + b * P:1 + (b + 1) * P, :].rearrange("o p d -> (o p) d"),
                                 res[b][:, :]).then_inc(stored[b], 16)
            sp.wait_ge(res_done, 2 * NB + 1)
            sp.dma_start(out[:, 0, :], res[0][0:NB, :]).then_inc(stored[0], 16)
            sp.wait_ge(stored[0], 16 * (NB + 2))
            sp.wait_ge(stored[1], 16 * (NB + 1))

        @block.gpsimd
        def _(pool):
            nc.gpsimd.memset(mhalf[:, :], -0.5).then_inc(consts, 1)
            nc.gpsimd.memset(eps[:, :], EPS).then_inc(consts, 1)
            nc.gpsimd.memset(ones[:, :], 1.0).then_inc(consts, 1)
            nc.gpsimd.memset(ident[:, :], 0.0).then_inc(consts, 1)
            pool.wait_ge(consts, 4)
            nc.gpsimd.affine_select(out=ident[:, :], in_=ident[:, :], compare_op=ALU.not_equal, fill=1.0,
                                    base=0, pattern=[[-1, P]], channel_multiplier=1).then_inc(ident_done, 1)
            pool.wait_ge(ident_done, 1)
            nc.gpsimd.tensor_copy(ident16[:, :], ident[:, :]).then_inc(ident_done, 1)
            steps = Steps(pool, m.sem("pool_rstd"), 1)

            def take(t, b):
                if not isinstance(t, int) or t >= 2:
                    pool.wait_ge(aoT_done, t - 1)
                nc.gpsimd.tensor_copy(ao[b][:, :], att[:, bass.ds(t, 1), 0:D]).then_inc(ao_copied, 1)

            def root(t):
                steps.round(t)
                pool.wait_ge(var_done, t + 1)
                steps.then_wait(nc.gpsimd.tensor_tensor(rstd[:, :], mv[:, 1:2], eps[:, :], ALU.add))
                nc.gpsimd.tensor_tensor(rstd[:, :], rstd[:, :], mhalf[:, :], ALU.pow).then_inc(rstd_done, 1)

            def finish(t, b):
                count = t + 1 if isinstance(t, int) else pool.to_reg(t + 1)
                pool.wait_ge(consts, 4)
                pool.wait_ge(scaled, count)
                nc.gpsimd.tensor_tensor(res[b][:, :], res[b][:, :], H[:, bass.ds(t, 1), :], ALU.add)\
                    .then_inc(res_done, 1)

            def turn(t, b):
                if exists(t + 3):
                    take(t + 3, 1 - b)
                if exists(t - 1):
                    finish(t - 1, 1 - b)
                if exists(t + 2):
                    root(t + 2)

            for t in range(3):
                take(t, t % 2)
            for t in range(2):
                root(t)
            all_turns(pool, turn)

        @block.tensor
        def _(pe):
            pe.wait_ge(consts, 4)
            pe.wait_ge(sums_done, 1)
            nc.tensor.matmul(ps_aoT[:, 0, 0:3], ones[:, :], sums[:, :], start=True, stop=True).then_inc(total_done, 1)
            pe.wait_ge(wq_done, 3)
            pe.wait_ge(ident_done, 2)
            pe.wait_ge(w_in, 16)

            def turn_ao(t, b):
                pe.wait_ge(ao_copied, t + 1)
                for c in range(2):
                    last = nc.tensor.transpose(ps_aoT[:, c, :], ao[b][:, c * P:(c + 1) * P], ident[:, :])
                last.then_inc(aoT_done, 1)

            def project(t):
                pe.wait_ge(aoT_copied, t + 1)
                for c in range(2):
                    last = nc.tensor.matmul(ps_h[:, :], aoT[:, c, :], wo[:, c, :], start=c == 0, stop=c == 1)
                last.then_inc(h_done, 1)

            def turn_x(t):
                pe.wait_ge(xq_done, t + 1)
                pe.wait_ge(aoT_copied, t + 2 if not isinstance(t, int) else max(3, min(t + 2, T)))
                for c in range(2):
                    last = nc.tensor.transpose(ps_xqT[:, c, :], xq[:, c * P:(c + 1) * P], ident16[:, :])
                last.then_inc(xqT_done, 1)

            def up(t, half):
                if half == 0:
                    pe.wait_ge(xqT_copied, t + 1)
                if not isinstance(t, int) or t > 0:
                    pe.wait_ge(gu_read, 2 * t - 1 + half)
                for k in range(2):
                    for c in range(2):
                        cols = slice(k * F + half * HALF, k * F + (half + 1) * HALF)
                        last = nc.tensor.matmul(ps_gu[:, half, k, :], xqT[:, c, :], wq[:, c, cols],
                                                start=c == 0, stop=c == 1)
                last.then_inc(gu_done, 1)

            def turn_z(t):
                pe.wait_ge(zq_done, t + 1)
                for c in range(FC):
                    last = nc.tensor.transpose(ps_zqT[:, c, :], zq[:, c * P:(c + 1) * P], ident16[:, :])
                last.then_inc(zqT_done, 1)

            def down(t):
                pe.wait_ge(zqT_copied, t + 1)
                for c in range(FC):
                    last = nc.tensor.matmul(ps_d[:, :], zqT[:, c, :], wdq[:, c, :], start=c == 0, stop=c == FC - 1)
                last.then_inc(down_done, 1)

            def turn(t, b):
                if exists(t + 2):
                    pe.wait_ge(var_done, t + 2)
                    project(t + 2)
                if exists(t - 1):
                    turn_z(t - 1)
                if exists(t + 1):
                    turn_x(t + 1)
                if exists(t - 1):
                    if not isinstance(t, int) or t > 1:
                        pe.wait_ge(scaled, t - 1)
                    down(t - 1)
                if exists(t + 1):
                    up(t + 1, 0)
                    up(t + 1, 1)
                if exists(t + 3):
                    turn_ao(t + 3, 1 - b)

            turn_ao(0, 0)
            project(0)
            turn_ao(1, 1)
            pe.wait_ge(var_done, 1)
            project(1)
            turn_ao(2, 0)
            turn_x(0)
            up(0, 0)
            up(0, 1)
            all_turns(pe, turn)

        @block.scalar
        def _(act):
            def copy_ao(t):
                act.wait_ge(aoT_done, t + 1)
                nc.scalar.activation(aoT[:, :, :], ps_aoT, ACT.Copy).then_inc(aoT_copied, 1)

            def copy_x(t):
                act.wait_ge(xqT_done, t + 1)
                nc.scalar.activation(xqT[:, :, :], ps_xqT, ACT.Copy).then_inc(xqT_copied, 1)

            def gate(t, b, half):
                act.wait_ge(gu_done, 2 * t + half + 1)
                nc.scalar.activation(silu[:, half * HALF:(half + 1) * HALF], ps_gu[:, half, 0, :], ACT.Silu,
                                     scale=gate_scale[b]).then_inc(silu_done, 1)

            def round_z(t, b):
                act.wait_ge(zr_done, t + 1)
                nc.scalar.activation(zq[:, :], z[b][:, :], ACT.Copy, bias=-MAGIC).then_inc(zq_done, 1)

            def copy_z(t):
                act.wait_ge(zqT_done, t + 1)
                nc.scalar.activation(zqT[:, :, :], ps_zqT[:, :, :], ACT.Copy).then_inc(zqT_copied, 1)

            def scale_down(t, b):
                act.wait_ge(down_done, t + 1)
                act.wait_ge(stored[b], 16 * (t // 2 + 1) if isinstance(t, int) else 8 * (t - b) + 16)
                nc.scalar.activation(res[b][:, :], ps_d[:, :], ACT.Copy, scale=down_scale[b][:, :])\
                    .then_inc(scaled, 1)

            def turn(t, b):
                if exists(t + 1):
                    copy_x(t + 1)
                if exists(t - 1):
                    copy_z(t - 1)
                    scale_down(t - 1, 1 - b)
                if exists(t + 1):
                    gate(t + 1, 1 - b, 0)
                    gate(t + 1, 1 - b, 1)
                if exists(t):
                    round_z(t, b)
                if exists(t + 3):
                    copy_ao(t + 3)

            parts = [wf[:, :, 0:F], wf[:, :, F:2 * F], wdf[:, :, :]]
            rounded = [wq[:, :, 0:F], wq[:, :, F:2 * F], wdq[:, :, :]]
            for k in range(3):
                act.wait_ge(part_rounded, k + 1)
                nc.scalar.activation(rounded[k], parts[k], ACT.Copy, bias=-MAGIC).then_inc(wq_done, 1)
            for t in range(3):
                copy_ao(t)
            copy_x(0)
            gate(0, 0, 0)
            gate(0, 0, 1)
            all_turns(act, turn)

        @block.vector
        def _(dve):
            v = nc.vector
            setup = Steps(dve, m.sem("dve_setup"), 100)
            go = setup.then_wait
            parts = [wf[:, :, 0:F], wf[:, :, F:2 * F], wdf[:, :, :]]
            for k, part in enumerate(parts):
                dve.wait_ge(part_in[k], 16)
                last = v.tensor_reduce(sums[:, k:k + 1], part, axis=AX.XY, op=ALU.add, apply_absolute_value=True)
            last.then_inc(sums_done, 1)
            dve.wait_ge(w_in, 16)
            dve.wait_ge(total_done, 1)
            go(v.tensor_scalar(winv[:, :], ps_aoT[:, 0, 0:3], 1.0 / (F * D), 1e-5, ALU.mult, ALU.max))
            go(v.reciprocal(wscale[:, :], winv[:, :]))
            go(v.reciprocal(winv[:, :], wscale[:, :]))
            for k, part in enumerate(parts):
                go(v.tensor_scalar(part, part, wscale[:, k:k + 1], MAGIC, ALU.mult, ALU.add))
                v.tensor_scalar(part, part, MAGIC - 1, MAGIC + 1, ALU.max, ALU.min).then_inc(part_rounded, 1)

            add_steps = Steps(dve, m.sem("dve_add"), 2)
            round_steps = Steps(dve, m.sem("dve_round"), 6)
            z_steps = Steps(dve, m.sem("dve_z"), 5)

            def add_projection(t):
                add_steps.round(t)
                go = add_steps.then_wait
                h = H[:, bass.ds(t, 1), :]
                dve.wait_ge(h_done, t + 1)
                go(v.tensor_tensor(h, ps_h[:, :], h, ALU.add), (w_in, 16))
                go(v.bn_stats(stats[:, :], h), (w_in, 16))
                v.bn_aggr(mv[:, :], stats[:, :]).then_inc(var_done, 1)

            def round_x(t, b):
                round_steps.round(t)
                go = round_steps.then_wait
                dve.wait_ge(rstd_done, t + 1)
                go(v.tensor_scalar(xn[:, :], H[:, bass.ds(t, 1), :], mv[:, 0:1], rstd[:, :],
                                   ALU.subtract, ALU.mult))
                go(v.tensor_reduce(amax[:, :], xn[:, :], axis=AX.X, op=ALU.max, apply_absolute_value=True))
                go(v.tensor_scalar(amax[:, :], amax[:, :], 1e-5, 1.0 / 127.0, ALU.max, ALU.mult))
                go(v.reciprocal(ascale[:, :], amax[:, :]))
                go(v.tensor_scalar(xr[:, :], xn[:, :], ascale[:, :], MAGIC, ALU.mult, ALU.add))
                v.tensor_scalar(scales[b][:, :], winv[:, 0:2], amax[:, :], None, ALU.mult)
                go(v.tensor_scalar(xr[:, :], xr[:, :], MAGIC - 128, MAGIC + 127, ALU.max, ALU.min))
                if not isinstance(t, int) or t > 0:
                    dve.wait_ge(xqT_done, t)
                v.tensor_scalar(xq[:, :], xr[:, :], MAGIC, None, ALU.subtract).then_inc(xq_done, 1)

            def multiply(t, b):
                z_steps.round(t)
                go = z_steps.then_wait
                for half in range(2):
                    cols = slice(half * HALF, (half + 1) * HALF)
                    dve.wait_ge(silu_done, 2 * t + half + 1)
                    v.tensor_tensor(z[b][:, cols], silu[:, cols], ps_gu[:, half, 1, :], ALU.mult)\
                        .then_inc(gu_read, 1)
                dve.wait_ge(gu_read, 2 * t + 2)
                go(v.tensor_reduce(zmax[:, :], z[b][:, :], axis=AX.X, op=ALU.max, apply_absolute_value=True))
                go(v.tensor_scalar(zmax[:, :], zmax[:, :], up_scale[b], 1e-5, ALU.mult, ALU.max))
                go(v.reciprocal(zscale[:, :], zmax[:, :]))
                go(v.tensor_scalar(zmul[:, :], zscale[:, :], up_scale[b], 127.0, ALU.mult, ALU.mult))
                v.tensor_scalar(down_scale[b][:, :], zmax[:, :], winv[:, 2:3], 1.0 / 127.0, ALU.mult, ALU.mult)
                go(v.tensor_scalar(z[b][:, :], z[b][:, :], zmul[:, :], MAGIC, ALU.mult, ALU.add))
                v.tensor_scalar(z[b][:, :], z[b][:, :], MAGIC - 128, MAGIC + 127, ALU.max, ALU.min)\
                    .then_inc(zr_done, 1)

            def turn(t, b):
                if exists(t + 1):
                    round_x(t + 1, 1 - b)
                if exists(t):
                    multiply(t, b)
                if exists(t + 2):
                    add_projection(t + 2)

            add_projection(0)
            round_x(0, 0)
            add_projection(1)
            all_turns(dve, turn)


def build(nc, args, out):
    with ExitStack() as stack:
        H = stack.enter_context(nc.sbuf_tensor("H", [P, NT, D], F32))
        xs = nc.dram_tensor("xs_dram", (ROUTED * MT, D), F32).ap()
        ys = nc.dram_tensor("ys_dram", (ROUTED * MT, D), F32).ap()
        vcls = nc.dram_tensor("vcls_dram", (NB, D), F32).ap()
        with nc.cleanup_on_exit():
            tokenizer(nc, H, args)
            recurrence(nc, H, xs, args)
        with nc.cleanup_on_exit(), ExitStack() as moe:
            place = [moe.enter_context(nc.sbuf_tensor(f"place{k}", [P, NT, 1], U32)) for k in range(2)]
            share = [moe.enter_context(nc.sbuf_tensor(f"share{k}", [P, NT], F32)) for k in range(2)]
            whose = moe.enter_context(nc.sbuf_tensor("whose", [1, ROUTED], I32))
            xn = moe.enter_context(nc.sbuf_tensor("xn", [P, NT, D], F32))
            shared_w = moe.enter_context(nc.sbuf_tensor("shared_w", [P, EXPERT_COLS], F32))
            route(nc, H, xn, place, share, whose, shared_w, args)
            experts(nc, H, xn, xs, ys, place, share, whose, shared_w, args)
        with ExitStack() as att:
            qkv = att.enter_context(nc.sbuf_tensor("qkv", [P, NT, 3 * D], F32))
            class_keys = att.enter_context(nc.sbuf_tensor("class_keys", [P, AH // 2, 2, NB], F32))
            queries_keys_values(nc, H, qkv, class_keys, vcls, args)
            attention(nc, qkv, class_keys, vcls, args)
            bitlinear_ffn(nc, H, qkv, args, out)


def expert_rows(np, a):
    def up(w, sw):
        w = np.concatenate([w, sw[None]])
        return w.reshape(E + 1, 2, P, I, 2).transpose(0, 2, 1, 4, 3)

    def bias(b, sb):
        b = np.concatenate([b, sb[None]])
        return b.reshape(E + 1, I // P, P, 2).transpose(0, 2, 1, 3)

    w13 = np.stack([up(a["L0_ffn_w1"], a["L0_ffn_sw1"]), up(a["L0_ffn_w3"], a["L0_ffn_sw3"])], axis=3)
    w2 = np.concatenate([a["L0_ffn_w2"], a["L0_ffn_sw2"][None]]).reshape(E + 1, I // P, P, D).transpose(0, 2, 1, 3)
    b13 = np.stack([bias(a["L0_ffn_b1"], a["L0_ffn_sb1"]), bias(a["L0_ffn_b3"], a["L0_ffn_sb3"])], axis=3)
    return np.concatenate([w13.reshape(E + 1, P, -1), w2.reshape(E + 1, P, -1), b13.reshape(E + 1, P, -1)], axis=2)


def kernel(**inputs):
    import numpy as np
    import concourse.bacc as bacc
    from concourse.bass_utils import run_bass_kernel_spmd

    a = {k: np.asarray(v) for k, v in inputs.items()}
    x = a["x"]
    angle = np.outer(np.arange(1, L + 1, dtype=np.float32),
                     1.0 / 10000.0 ** (np.arange(0, DH, 2, dtype=np.float32) / DH)).astype(np.float32)
    laid = {
        "tok_x": np.concatenate([x.transpose(0, 1, 3, 2).reshape(NB, C, HT * L),
                                 np.ones((NB, 1, HT * L), np.float32)], axis=1),
        "tok_xr": x.transpose(0, 2, 3, 1).reshape(NB, L, D),
        "tok_wqkv": np.concatenate([
            np.concatenate([a[f"L0_tok_W{c}_w"].T for c in "qkv"], axis=1),
            np.concatenate([a[f"L0_tok_W{c}_b"] for c in "qkv"])[None]], axis=0),
        "tok_wbT": a["L0_tok_w_bias"].T,
        "tok_maskT": a["L0_tok_local_mask"].T,
        "L0_tok_out_w": a["L0_tok_out_w"], "L0_tok_out_b": a["L0_tok_out_b"],
        "L0_tok_ln_g": a["L0_tok_ln_g"], "L0_tok_ln_b": a["L0_tok_ln_b"],
        "cls_row": a["cls_tok"].reshape(D),
        "att_w": np.concatenate([a[f"L1_attn_W_{c}"].T for c in "QKV"], axis=1),
        "att_wo": a["L1_attn_W_O"].T,
        "ffn_gu": np.concatenate([a["L1_ffn_w_gate"].T, a["L1_ffn_w_up"].T], axis=1),
        "ffn_down": a["L1_ffn_w_down"].T,
        "rope_cos": np.concatenate([np.cos(angle), np.cos(angle)], axis=1),
        "rope_sin": np.concatenate([-np.sin(angle), np.sin(angle)], axis=1),
        "gate_wT": a["L0_ffn_gate_w"].T, "gate_b": a["L0_ffn_gate_b"],
        "experts": expert_rows(np, a), "experts_b2": np.concatenate([a["L0_ffn_b2"], a["L0_ffn_sb2"][None]]),
        "earlier": np.triu(np.ones((P, P), np.float32), 1),
        "first_wins": np.arange(E, 0, -1, dtype=np.float32),
        "is_token": np.concatenate([np.ones((P, CLS), np.float32), (np.arange(P)[:, None] < NB).astype(np.float32),
                                    np.zeros((P, 1), np.float32)], axis=1),
        "tile_no": np.arange(ROUTED, dtype=np.float32),
        "rec_w": np.concatenate([a[f"L0_attn_W_{c}"].T for c in "kvq"], axis=1),
    }
    nc = bacc.Bacc("TRN2", target_bir_lowering=False, num_devices=1)
    arrays, args = {}, {}
    for name, v in laid.items():
        arrays[name + "_dram"] = np.ascontiguousarray(v)
        args[name] = nc.dram_tensor(name + "_dram", v.shape, mybir.dt.from_np(v.dtype), kind="ExternalInput").ap()
    out = nc.dram_tensor("out_dram", (NB, L + 1, D), F32, kind="ExternalOutput").ap()
    build(nc, args, out)
    r = run_bass_kernel_spmd(nc, [arrays], core_ids=[0])
    return r.results[0]["out_dram"]
```
